# Optimizing a Trainium2 kernel written in Bass

```python
import numpy as np
import jax
import jax.numpy as jnp

def _softmax(x, axis=-1):
    return jax.nn.softmax(x, axis=axis)

def _gelu(x):
    return jax.nn.gelu(x, approximate=True)

def _silu(x):
    return jax.nn.silu(x)

def _sigmoid(x):
    return jax.nn.sigmoid(x)

def _layernorm(x, axis=-1, eps=1e-05):
    m = jnp.mean(x, axis=axis, keepdims=True)
    v = jnp.var(x, axis=axis, keepdims=True)
    return (x - m) / jnp.sqrt(v + eps)

def _scatter_add(tgt, idx, src, axis=0):
    return tgt.at[idx].add(src)

def _segment_sum(src, seg, n):
    return jax.ops.segment_sum(src, seg, n)
kernel_name = 'mk_gnn_preln_d4_gnn_r8_ad1e23'

def setup_inputs(seed: int=0):
    np.random.seed(seed)
    _w = jnp.asarray

    def _rec_inputs():
        import jax
        import jax.numpy as jnp
        _gk = jax.random.key(seed)
        x = -0.0003713 + 1 * jax.random.normal(jax.random.fold_in(_gk, 1), (6250, 128), jnp.float32)
        _s = jax.random.randint(jax.random.fold_in(_gk, 2), (50000,), 0, 6250, jnp.int32)
        _d = jax.random.randint(jax.random.fold_in(_gk, 3), (50000,), 0, 6250, jnp.int32)
        _loop = jnp.arange(6250, dtype=jnp.int32)
        src = jnp.concatenate([_s, _d, _loop])
        dst = jnp.concatenate([_d, _s, _loop])
        _o = jnp.argsort(dst, stable=True)
        src = src[_o]
        dst = dst[_o]
        edge_attr_128 = -8.16379e-05 + 0.999858 * jax.random.normal(jax.random.fold_in(_gk, 12), (106250, 128), jnp.float32)
        edge_attr_16 = -0.00010739 + 0.99994 * jax.random.normal(jax.random.fold_in(_gk, 13), (106250, 16), jnp.float32)
        edge_attr_32 = jax.random.uniform(jax.random.fold_in(_gk, 14), (106250, 32), jnp.float32, 0.0, 1)
        edge_weight = jax.random.uniform(jax.random.fold_in(_gk, 16), (106250,), jnp.float32, 0.0, 0.999999)
        return (x, src, dst, edge_attr_128, edge_attr_16, edge_attr_32, edge_weight)
    x, src, dst, edge_attr_128, edge_attr_16, edge_attr_32, edge_weight = _rec_inputs()

    def _L0_gnn_setup():
        import jax, jax.numpy as jnp
        import numpy as np
        LOG2 = float(np.log(2.0))

        def ssp(v):
            return jax.nn.softplus(v) - jnp.asarray(LOG2, v.dtype)
        key = jax.random.key(seed)
        ks = jax.random.split(key, 16)
        N, B, F, R, P = (12500, 128, 64, 32, 200000)
        inp = {'x': jax.random.normal(ks[0], (N, B), jnp.float32), 'f_ij': jax.random.uniform(ks[1], (P, R), jnp.float32), 'rcut_ij': jax.random.uniform(ks[2], (P,), jnp.float32), 'pairlist': jax.random.randint(ks[3], (2, P), 0, N, jnp.int64), 'w_in': jax.random.normal(ks[4], (B, F), jnp.float32) * (1.0 / np.sqrt(B)), 'b_in': jnp.zeros((F,), jnp.float32), 'w_f1': jax.random.normal(ks[5], (R, F), jnp.float32) * (1.0 / np.sqrt(R)), 'b_f1': jnp.zeros((F,), jnp.float32), 'w_f2': jax.random.normal(ks[6], (F, F), jnp.float32) * (1.0 / np.sqrt(F)), 'b_f2': jnp.zeros((F,), jnp.float32), 'w_o1': jax.random.normal(ks[7], (F, B), jnp.float32) * (1.0 / np.sqrt(F)), 'b_o1': jnp.zeros((B,), jnp.float32), 'w_o2': jax.random.normal(ks[8], (B, B), jnp.float32) * (1.0 / np.sqrt(B)), 'b_o2': jnp.zeros((B,), jnp.float32)}
        return inp
    _L0_gnn_all = _L0_gnn_setup()
    _L0_gnn_in = {k: v for k, v in _L0_gnn_all.items() if k in ('w_in', 'b_in', 'w_f1', 'b_f1', 'w_f2', 'b_f2', 'w_o1', 'b_o1', 'w_o2', 'b_o2')}
    del _L0_gnn_all

    def _L1_gnn_setup():
        import jax, jax.numpy as jnp
        import numpy as np
        N_NODES = 6250
        N_EDGES = 80000
        D = 128
        key = jax.random.key(seed)
        k_x, k_ei, k_ew, k_w = jax.random.split(key, 4)
        x = jax.random.normal(k_x, (N_NODES, D), dtype=jnp.float32)
        edge_index = jax.random.randint(k_ei, (2, N_EDGES), 0, N_NODES, dtype=jnp.int64)
        edge_weight = jax.random.uniform(k_ew, (N_EDGES,), dtype=jnp.float32)
        W = jax.random.normal(k_w, (D, D), dtype=jnp.float32) / np.sqrt(D)
        b = jnp.zeros((D,), dtype=jnp.float32)
        return {'x': x, 'edge_index': edge_index, 'edge_weight': edge_weight, 'W': W, 'b': b}
    _L1_gnn_all = _L1_gnn_setup()
    _L1_gnn_in = {k: v for k, v in _L1_gnn_all.items() if k in ('W', 'b')}
    del _L1_gnn_all

    def _L2_gnn_setup():
        import jax, jax.numpy as jnp
        import numpy as np
        N, E, DIM = (6250, 100000, 128)
        H, EH, HD = (8, 8, 16)
        key = jax.random.key(seed)
        ks = jax.random.split(key, 10)
        s = 0.05
        return {'x': jax.random.normal(ks[0], (N, DIM), jnp.float32), 'edges': jax.random.normal(ks[1], (E, DIM), jnp.float32), 'Wq': jax.random.normal(ks[2], (DIM, DIM), jnp.float32) * s, 'Wk': jax.random.normal(ks[3], (DIM, DIM), jnp.float32) * s, 'Wv': jax.random.normal(ks[4], (DIM, EH * HD), jnp.float32) * s, 'Wek': jax.random.normal(ks[5], (DIM, DIM), jnp.float32) * s, 'Wev': jax.random.normal(ks[6], (DIM, EH * HD), jnp.float32) * s, 'W_exp': jax.random.normal(ks[7], (H, EH), jnp.float32) * s, 'W_out': jax.random.normal(ks[8], (EH * HD, DIM), jnp.float32) * s, 'edge_index': jax.random.randint(ks[9], (2, E), 0, N, jnp.int64)}
    _L2_gnn_all = _L2_gnn_setup()
    _L2_gnn_in = {k: v for k, v in _L2_gnn_all.items() if k in ('Wq', 'Wk', 'Wv', 'Wek', 'Wev', 'W_exp', 'W_out')}
    del _L2_gnn_all

    def _L3_gnn_setup():
        import jax, jax.numpy as jnp
        import numpy as np
        BN_EPS = 0.001
        D = 128
        EDGE_DIM = 16
        N_NODES = 6250
        N_EDGES = 100000

        def _bn(x, gamma, beta, mean, var):
            return (x - mean) * jax.lax.rsqrt(var + BN_EPS) * gamma + beta
        key = jax.random.key(seed)
        ks = jax.random.split(key, 12)
        inp = {'node_feat': jax.random.normal(ks[0], (N_NODES, D), jnp.float32), 'edge_feat': jax.random.normal(ks[1], (N_EDGES, EDGE_DIM), jnp.float32), 'src': jax.random.randint(ks[2], (N_EDGES,), 0, N_NODES, jnp.int32), 'dst': jax.random.randint(ks[3], (N_EDGES,), 0, N_NODES, jnp.int32), 'We1': jax.random.normal(ks[4], (EDGE_DIM, 2 * D), jnp.float32) * 0.05, 'be1': jnp.zeros((2 * D,), jnp.float32), 'We2': jax.random.normal(ks[5], (2 * D, D), jnp.float32) * 0.05, 'be2': jnp.zeros((D,), jnp.float32), 'eps': jax.random.normal(ks[6], (1,), jnp.float32) * 0.05, 'Wm1': jax.random.normal(ks[7], (D, 2 * D), jnp.float32) * 0.05, 'bm1': jnp.zeros((2 * D,), jnp.float32), 'g1': jnp.ones((2 * D,), jnp.float32), 'b1': jnp.zeros((2 * D,), jnp.float32), 'm1': jnp.zeros((2 * D,), jnp.float32), 'v1': jnp.ones((2 * D,), jnp.float32), 'Wm2': jax.random.normal(ks[8], (2 * D, D), jnp.float32) * 0.05, 'bm2': jnp.zeros((D,), jnp.float32), 'g2': jnp.ones((D,), jnp.float32), 'b2': jnp.zeros((D,), jnp.float32), 'm2': jnp.zeros((D,), jnp.float32), 'v2': jnp.ones((D,), jnp.float32)}
        return inp
    _L3_gnn_all = _L3_gnn_setup()
    _L3_gnn_in = {k: v for k, v in _L3_gnn_all.items() if k in ('We1', 'be1', 'We2', 'be2', 'eps', 'Wm1', 'bm1', 'g1', 'b1', 'm1', 'v1', 'Wm2', 'bm2', 'g2', 'b2', 'm2', 'v2')}
    del _L3_gnn_all
    return {'x': x, 'src': src, 'dst': dst, 'edge_attr_128': edge_attr_128, 'edge_attr_16': edge_attr_16, 'edge_attr_32': edge_attr_32, 'edge_weight': edge_weight, 'L0_gnn_w_in': _L0_gnn_in['w_in'], 'L0_gnn_b_in': _L0_gnn_in['b_in'], 'L0_gnn_w_f1': _L0_gnn_in['w_f1'], 'L0_gnn_b_f1': _L0_gnn_in['b_f1'], 'L0_gnn_w_f2': _L0_gnn_in['w_f2'], 'L0_gnn_b_f2': _L0_gnn_in['b_f2'], 'L0_gnn_w_o1': _L0_gnn_in['w_o1'], 'L0_gnn_b_o1': _L0_gnn_in['b_o1'], 'L0_gnn_w_o2': _L0_gnn_in['w_o2'], 'L0_gnn_b_o2': _L0_gnn_in['b_o2'], 'L1_gnn_W': _L1_gnn_in['W'], 'L1_gnn_b': _L1_gnn_in['b'], 'L2_gnn_Wq': _L2_gnn_in['Wq'], 'L2_gnn_Wk': _L2_gnn_in['Wk'], 'L2_gnn_Wv': _L2_gnn_in['Wv'], 'L2_gnn_Wek': _L2_gnn_in['Wek'], 'L2_gnn_Wev': _L2_gnn_in['Wev'], 'L2_gnn_W_exp': _L2_gnn_in['W_exp'], 'L2_gnn_W_out': _L2_gnn_in['W_out'], 'L3_gnn_We1': _L3_gnn_in['We1'], 'L3_gnn_be1': _L3_gnn_in['be1'], 'L3_gnn_We2': _L3_gnn_in['We2'], 'L3_gnn_be2': _L3_gnn_in['be2'], 'L3_gnn_eps': _L3_gnn_in['eps'], 'L3_gnn_Wm1': _L3_gnn_in['Wm1'], 'L3_gnn_bm1': _L3_gnn_in['bm1'], 'L3_gnn_g1': _L3_gnn_in['g1'], 'L3_gnn_b1': _L3_gnn_in['b1'], 'L3_gnn_m1': _L3_gnn_in['m1'], 'L3_gnn_v1': _L3_gnn_in['v1'], 'L3_gnn_Wm2': _L3_gnn_in['Wm2'], 'L3_gnn_bm2': _L3_gnn_in['bm2'], 'L3_gnn_g2': _L3_gnn_in['g2'], 'L3_gnn_b2': _L3_gnn_in['b2'], 'L3_gnn_m2': _L3_gnn_in['m2'], 'L3_gnn_v2': _L3_gnn_in['v2']}

def reference(x, src, dst, edge_attr_128, edge_attr_16, edge_attr_32, edge_weight, L0_gnn_w_in, L0_gnn_b_in, L0_gnn_w_f1, L0_gnn_b_f1, L0_gnn_w_f2, L0_gnn_b_f2, L0_gnn_w_o1, L0_gnn_b_o1, L0_gnn_w_o2, L0_gnn_b_o2, L1_gnn_W, L1_gnn_b, L2_gnn_Wq, L2_gnn_Wk, L2_gnn_Wv, L2_gnn_Wek, L2_gnn_Wev, L2_gnn_W_exp, L2_gnn_W_out, L3_gnn_We1, L3_gnn_be1, L3_gnn_We2, L3_gnn_be2, L3_gnn_eps, L3_gnn_Wm1, L3_gnn_bm1, L3_gnn_g1, L3_gnn_b1, L3_gnn_m1, L3_gnn_v1, L3_gnn_Wm2, L3_gnn_bm2, L3_gnn_g2, L3_gnn_b2, L3_gnn_m2, L3_gnn_v2):
    import jax
    import jax.numpy as jnp

    def _L0_gnn_ref(x, f_ij, rcut_ij, pairlist, w_in, b_in, w_f1, b_f1, w_f2, b_f2, w_o1, b_o1, w_o2, b_o2):
        import jax, jax.numpy as jnp
        import numpy as np
        LOG2 = float(np.log(2.0))

        def ssp(v):
            return jax.nn.softplus(v) - jnp.asarray(LOG2, v.dtype)
        n_atoms = x.shape[0]
        h = x @ w_in + b_in
        Wij = ssp(f_ij @ w_f1 + b_f1) @ w_f2 + b_f2
        Wij = Wij * rcut_ij[:, None]
        idx_i, idx_j = (pairlist[0], pairlist[1])
        x_ij = h[idx_j] * Wij
        agg = jax.ops.segment_sum(x_ij, idx_i, num_segments=n_atoms)
        out = ssp(agg @ w_o1 + b_o1) @ w_o2 + b_o2
        return out

    def _L1_gnn_ref(x, edge_index, edge_weight, W, b):
        import jax, jax.numpy as jnp
        import numpy as np
        N_NODES = 6250
        N_EDGES = 80000
        D = 128
        N = x.shape[0]
        src, dst = (edge_index[0], edge_index[1])
        loop = jnp.arange(N, dtype=src.dtype)
        src = jnp.concatenate([src, loop])
        dst = jnp.concatenate([dst, loop])
        ew = jnp.concatenate([edge_weight, jnp.ones((N,), dtype=x.dtype)])
        deg = jax.ops.segment_sum(ew, dst, num_segments=N)
        dinv = jnp.where(deg > 0, jax.lax.rsqrt(deg), 0.0)
        norm = dinv[src] * ew * dinv[dst]
        h = x @ W
        msg = h[src] * norm[:, None]
        agg = jax.ops.segment_sum(msg, dst, num_segments=N) + b
        z = jax.nn.relu(agg)
        return x + z

    def _L2_gnn_ref(x, edges, Wq, Wk, Wv, Wek, Wev, W_exp, W_out, edge_index):
        import jax, jax.numpy as jnp
        import numpy as np
        N, E, DIM = (6250, 100000, 128)
        H, EH, HD = (8, 8, 16)
        n = x.shape[0]
        scale = HD ** (-0.5)
        src, dst = (edge_index[0], edge_index[1])
        q = (x @ Wq).reshape(n, H, HD)[src]
        k = (x @ Wk).reshape(n, H, HD)[dst]
        v_nodes = (x @ Wv).reshape(n, EH, HD)
        v = v_nodes[dst]
        ek = (edges @ Wek).reshape(-1, H, HD)
        ev = (edges @ Wev).reshape(-1, EH, HD)
        attn = jnp.einsum('ehd,ehd->eh', q, (k + ek) * scale)
        attn = attn @ W_exp
        mx = jax.ops.segment_max(attn, src, num_segments=n)
        ex = jnp.exp(attn - mx[src])
        denom = jax.ops.segment_sum(ex, src, num_segments=n)
        attn = ex / denom[src]
        out_e = attn[:, :, None] * (v + ev)
        agg = jax.ops.segment_sum(out_e, src, num_segments=n)
        out = (v_nodes - agg).reshape(n, EH * HD) @ W_out
        return out

    def _L3_gnn_ref(node_feat, edge_feat, src, dst, We1, be1, We2, be2, eps, Wm1, bm1, g1, b1, m1, v1, Wm2, bm2, g2, b2, m2, v2):
        import jax, jax.numpy as jnp
        import numpy as np
        BN_EPS = 0.001
        D = 128
        EDGE_DIM = 16
        N_NODES = 6250
        N_EDGES = 100000

        def _bn(x, gamma, beta, mean, var):
            return (x - mean) * jax.lax.rsqrt(var + BN_EPS) * gamma + beta
        e = (edge_feat @ We1 + be1) @ We2 + be2
        msg = jax.nn.relu(e + node_feat[src])
        pooled = jax.ops.segment_sum(msg, dst, num_segments=node_feat.shape[0])
        h = (1.0 + eps) * node_feat + pooled
        h = jax.nn.relu(_bn(h @ Wm1 + bm1, g1, b1, m1, v1)) @ Wm2 + bm2
        return _bn(h, g2, b2, m2, v2)
    edge_index = jnp.stack([src, dst])
    h = jnp.maximum(_layernorm(x, axis=-1), 0.0)
    x = x + _L0_gnn_ref(h, edge_attr_32, edge_weight, edge_index, L0_gnn_w_in, L0_gnn_b_in, L0_gnn_w_f1, L0_gnn_b_f1, L0_gnn_w_f2, L0_gnn_b_f2, L0_gnn_w_o1, L0_gnn_b_o1, L0_gnn_w_o2, L0_gnn_b_o2)
    h = jnp.maximum(_layernorm(x, axis=-1), 0.0)
    x = x + _L1_gnn_ref(h, edge_index, edge_weight, L1_gnn_W, L1_gnn_b)
    h = jnp.maximum(_layernorm(x, axis=-1), 0.0)
    x = x + _L2_gnn_ref(h, edge_attr_128, L2_gnn_Wq, L2_gnn_Wk, L2_gnn_Wv, L2_gnn_Wek, L2_gnn_Wev, L2_gnn_W_exp, L2_gnn_W_out, edge_index)
    h = jnp.maximum(_layernorm(x, axis=-1), 0.0)
    x = x + _L3_gnn_ref(h, edge_attr_16, src, dst, L3_gnn_We1, L3_gnn_be1, L3_gnn_We2, L3_gnn_be2, L3_gnn_eps, L3_gnn_Wm1, L3_gnn_bm1, L3_gnn_g1, L3_gnn_b1, L3_gnn_m1, L3_gnn_v1, L3_gnn_Wm2, L3_gnn_bm2, L3_gnn_g2, L3_gnn_b2, L3_gnn_m2, L3_gnn_v2)
    return x

_drawn_inputs = setup_inputs


def setup_inputs(seed=0):
    import zlib

    import numpy as np

    out = dict(_drawn_inputs(seed))
    spreads = {'L0_gnn_b_in': (0.0, 0.1),
     'L0_gnn_b_f1': (0.0, 0.1),
     'L0_gnn_b_f2': (0.0, 0.1),
     'L0_gnn_b_o1': (0.0, 0.1),
     'L0_gnn_b_o2': (0.0, 0.1),
     'L1_gnn_b': (0.0, 0.1),
     'L3_gnn_be1': (0.0, 0.1),
     'L3_gnn_be2': (0.0, 0.1),
     'L3_gnn_bm1': (0.0, 0.448),
     'L3_gnn_g1': (1.0, 0.2),
     'L3_gnn_b1': (0.0, 0.509),
     'L3_gnn_m1': (0.0, 0.392),
     'L3_gnn_v1': (1.0, 0.2),
     'L3_gnn_bm2': (0.0, 0.296),
     'L3_gnn_g2': (1.0, 0.2),
     'L3_gnn_b2': (0.0, 0.325),
     'L3_gnn_m2': (0.0, 0.281),
     'L3_gnn_v2': (1.0, 0.2)}
    factors = {'L2_gnn_Wq': 8.0, 'L2_gnn_Wk': 8.0, 'L2_gnn_Wek': 8.0, 'L2_gnn_W_exp': 8.0}
    for name, (base, spread) in spreads.items():
        noise = np.random.default_rng([zlib.crc32(name.encode()), seed]).standard_normal(out[name].shape)
        drawn = base * np.exp(spread * noise) if base else spread * noise
        out[name] = jnp.asarray(drawn.astype(out[name].dtype))
    for name, factor in factors.items():
        out[name] = (out[name] * factor).astype(out[name].dtype)
    return out
```

```python
from contextlib import ExitStack

import concourse.bass as bass
from concourse import mybir

F32 = mybir.dt.float32
I32 = mybir.dt.int32
BF16 = mybir.dt.bfloat16
ALU = mybir.AluOpType
ACT = mybir.ActivationFunctionType
AX_X = mybir.AxisListType.X
DVE = mybir.EngineType.DVE
PE = mybir.EngineType.PE

P = 128
N = 6250
E = 106250
D = 128
NB = -(-N // P)
NR = NB * P
NW = NR + P
G = 8
GE = G * P
T = -(-E // (2 * GE)) * 2 * G
NG = T // G
EP = T * P
R = 7
NI = NB // R
assert NI * R == NB and N < NR
F0 = 64
XC = F0 + 1
H = 8
HD = D // H
LOG2 = 0.6931471805599453
LN_EPS = 1e-5
BN_EPS = 1e-3
FAR = 1.0e37
IN_RANGE = "node numbers are 0..N by the kind of the inputs, and tables are padded past N"


def load_values(nc, engine, ap, top):
    return nc.values_load_multi_w_load_instructions(
        ap, engines=(engine,), min_val=0, max_val=top, skip_runtime_bounds_check_because=IN_RANGE)[1]


class Space:

    def __init__(self, nc, tag):
        self.nc, self.tag, self.ctx, self.sems = nc, tag, ExitStack(), []

    def __enter__(self):
        return self

    def __exit__(self, *a):
        for sem in self.sems:
            self.nc.sync.sem_clear(sem)
        return self.ctx.__exit__(*a)

    def sb(self, name, shape, dt=F32):
        return self.ctx.enter_context(self.nc.sbuf_tensor(f"{self.tag}_{name}", shape, dt))

    def ps(self, name, shape, dt=F32):
        return self.ctx.enter_context(self.nc.psum_tensor(f"{self.tag}_{name}", shape, dt))

    def sem(self, name):
        self.sems.append(self.ctx.enter_context(self.nc.semaphore(f"{self.tag}_{name}")))
        return self.sems[-1]


def setup(nc, A, K, s):
    loaded, made, tidy = s.sem("loaded"), s.sem("made"), s.sem("tidy")
    pairs = [
        (K.x[:], A["x"].rearrange("(b p) d -> p b d", p=P)),
        (K.src_i[:], A["src"]), (K.dst_i[:], A["dst"]), (K.ew[:], A["ew"]),
        (K.w_in[:], A["L0_gnn_w_in"]), (K.b_in[:], A["L0_gnn_b_in"].unsqueeze(0)),
        (K.w_f1[:, 0:F0], A["L0_gnn_w_f1"]), (K.w_f1[:, F0:2 * F0], A["L0_gnn_w_f1"]),
        (K.b_f1[0:F0, :], A["L0_gnn_b_f1"].unsqueeze(1)), (K.b_f1[F0:2 * F0, :], A["L0_gnn_b_f1"].unsqueeze(1)),
        (K.w_f2[0:F0, :], A["L0_gnn_w_f2"]), (K.w_f2[F0:2 * F0, :], A["L0_gnn_w_f2"]),
        (K.b_f2[:], A["L0_gnn_b_f2"].unsqueeze(0)),
        (K.w_o1[:], A["L0_gnn_w_o1"]), (K.b_o1[:], A["L0_gnn_b_o1"].unsqueeze(1)),
        (K.w_o2[:], A["L0_gnn_w_o2"]), (K.b_o2[:], A["L0_gnn_b_o2"].unsqueeze(0)),
        (K.w1[:], A["L1_gnn_W"]), (K.b1[:], A["L1_gnn_b"].unsqueeze(0).broadcast_to([P, D])),
        (K.wqkv[:, 0:D], A["L2_gnn_Wq"]), (K.wqkv[:, D:2 * D], A["L2_gnn_Wk"]), (K.wqkv[:, 2 * D:], A["L2_gnn_Wv"]),
        (K.wekv[:, 0:D], A["L2_gnn_Wek"]), (K.wekv[:, D:], A["L2_gnn_Wev"]),
        (K.w_exp[:], A["L2_gnn_W_exp"]), (K.w_out[:], A["L2_gnn_W_out"]),
        (K.we1[:], A["L3_gnn_We1"]), (K.be1[:], A["L3_gnn_be1"].rearrange("(m p) -> p m", p=P)),
        (K.we2[:], A["L3_gnn_We2"].rearrange("(m p) d -> p m d", p=P)),
        (K.be2[:], A["L3_gnn_be2"].unsqueeze(0)),
        (K.eps[:], A["L3_gnn_eps"].unsqueeze(0).broadcast_to([P, 1])),
        (K.wm1[:], A["L3_gnn_Wm1"]), (K.wm2[:], A["L3_gnn_Wm2"].rearrange("(m p) d -> p m d", p=P)),
    ]
    pairs += [(K.bn1[:, :, k], A[f"L3_gnn_{n}"].rearrange("(m p) -> p m", p=P)) for k, n in enumerate(("bm1", "g1", "b1", "m1", "v1"))]
    pairs += [(K.bn2[:, k, :], A[f"L3_gnn_{n}"].unsqueeze(0).broadcast_to([P, D])) for k, n in enumerate(("bm2", "g2", "b2", "m2", "v2"))]
    with nc.Block() as block:
        @block.sync
        def _(sp):
            for to, of in pairs:
                with nc.allow_non_contiguous_dma("vectors of weights, once"):
                    sp.dma_start(to, of).then_inc(loaded, 16)

        @block.gpsimd
        def _(pool):
            nc.gpsimd.iota(K.lane[:], [[1, P]], base=0, channel_multiplier=0, allow_small_or_imprecise_dtypes=True)
            nc.gpsimd.iota(K.node_col[:], [[P, NB + 1]], base=0, channel_multiplier=1, allow_small_or_imprecise_dtypes=True)
            nc.gpsimd.memset(K.ident[:], 0.0).then_inc(made, 1)
            nc.gpsimd.memset(K.below[:], 1.0).then_inc(made, 1)
            nc.gpsimd.memset(K.above[:], 1.0).then_inc(made, 1)
            nc.gpsimd.memset(K.rep[:], 0.0).then_inc(made, 1)
            nc.gpsimd.memset(K.ones[:], 1.0)
            pool.wait_ge(made, 4)
            nc.gpsimd.affine_select(out=K.ident[:], in_=K.ident[:], compare_op=ALU.not_equal, fill=1.0, base=0,
                                    pattern=[[-1, P]], channel_multiplier=1).then_inc(made, 1)
            nc.gpsimd.affine_select(out=K.below[:], in_=K.below[:], compare_op=ALU.is_gt, fill=0.0, base=0,
                                    pattern=[[-1, P]], channel_multiplier=1).then_inc(made, 1)
            nc.gpsimd.affine_select(out=K.above[:], in_=K.above[:], compare_op=ALU.is_gt, fill=0.0, base=0,
                                    pattern=[[1, P]], channel_multiplier=-1).then_inc(made, 1)
            nc.gpsimd.affine_select(out=K.rep[:].rearrange("h (g d) -> h g d", g=H), in_=K.rep[:].rearrange("h (g d) -> h g d", g=H),
                                    compare_op=ALU.not_equal, fill=1.0, base=0,
                                    pattern=[[-1, H], [0, HD]], channel_multiplier=1).then_inc(made, 1)
            pool.wait_ge(made, 8)

        @block.vector
        def _(dve):
            dve.wait_ge(loaded, 16 * len(pairs))
            nc.vector.tensor_copy(K.src_f[:], K.src_i[:])
            nc.vector.tensor_copy(K.dst_f[:], K.dst_i[:])
            nc.vector.tensor_single_scalar(K.key_i[:], K.src_i[:], 7, ALU.logical_shift_right).then_inc(tidy, 1)
            nc.vector.tensor_single_scalar(K.low_i[:], K.src_i[:], P - 1, ALU.bitwise_and).then_inc(tidy, 1)
            dve.wait_ge(tidy, 2)
            nc.vector.tensor_copy(K.src_hi[:], K.key_i[:]).then_inc(tidy, 1)
            nc.vector.tensor_copy(K.src_lo[:], K.low_i[:]).then_inc(tidy, 1)
            dve.wait_ge(tidy, 4)
            nc.vector.tensor_single_scalar(K.key_i[:], K.dst_i[:], 7, ALU.logical_shift_right).then_inc(tidy, 1)
            nc.vector.tensor_single_scalar(K.low_i[:], K.dst_i[:], P - 1, ALU.bitwise_and).then_inc(tidy, 1)
            dve.wait_ge(tidy, 6)
            nc.vector.tensor_copy(K.dst_hi[:], K.key_i[:])
            nc.vector.tensor_copy(K.dst_lo[:], K.low_i[:])
            nc.vector.tensor_copy(K.dst_blk[0:1, :], K.key_i[0:1, :])


def histograms(nc, K, s):
    oh_hi = s.sb("oh_hi", [P, 2, G, NB], BF16)
    oh_lo = s.sb("oh_lo", [P, 2, G, P], BF16)
    d_hi = s.sb("d_hi", [P, 2, G, NB])
    d_hiw = s.sb("d_hiw", [P, 2, G, NB])
    d_lo = s.sb("d_lo", [P, 2, G, P])
    zero = s.sb("zero", [P, P])
    count = s.sb("count", [NB, P])
    upto = s.sb("upto", [NB, P])
    deg = s.sb("deg", [P, NB])
    pos = s.sb("positive", [P, NB])
    p_count, p_deg, p_off = s.ps("p_count", [P, 512]), s.ps("p_deg", [P, 512]), s.ps("p_off", [P, 512])
    src_hot, dst_hot, part, free = s.sem("src_hot"), s.sem("dst_hot"), s.sem("part"), s.sem("free")
    summed, chain, off_done, root, zeroed = (s.sem(n) for n in ("summed", "chain", "off", "root", "zeroed"))

    def step(dve, ins, n):
        ins.then_inc(chain, 1)
        dve.wait_ge(chain, n)

    with nc.Block() as block:
        @block.vector
        def _(dve):
            nc.vector.memset(zero[:], 0.0).then_inc(zeroed, 1)
            with nc.vector.Fori(0, NG // 2) as i:
                for h in range(2):
                    cols = bass.ds(i * 2 * G + h * G, G)
                    dve.wait_ge(free, i * 2 + h + 1)
                    nc.vector.tensor_tensor(out=oh_hi[:, h], in0=K.lane[:, 0:NB].unsqueeze(1).broadcast_to([P, G, NB]),
                                            in1=K.src_hi[:, cols].unsqueeze(2).broadcast_to([P, G, NB]), op=ALU.is_equal)
                    nc.vector.tensor_tensor(out=oh_lo[:, h], in0=K.lane[:, 0:P].unsqueeze(1).broadcast_to([P, G, P]),
                                            in1=K.src_lo[:, cols].unsqueeze(2).broadcast_to([P, G, P]), op=ALU.is_equal).then_inc(src_hot, 1)
                    nc.vector.tensor_tensor(out=d_hi[:, h], in0=K.lane[:, 0:NB].unsqueeze(1).broadcast_to([P, G, NB]),
                                            in1=K.dst_hi[:, cols].unsqueeze(2).broadcast_to([P, G, NB]), op=ALU.is_equal).then_inc(part, 1)
                    dve.wait_ge(part, i * 2 + h + 1)
                    nc.vector.tensor_tensor(out=d_hiw[:, h], in0=d_hi[:, h],
                                            in1=K.ew[:, cols].unsqueeze(2).broadcast_to([P, G, NB]), op=ALU.mult)
                    nc.vector.tensor_tensor(out=d_lo[:, h], in0=K.lane[:, 0:P].unsqueeze(1).broadcast_to([P, G, P]),
                                            in1=K.dst_lo[:, cols].unsqueeze(2).broadcast_to([P, G, P]), op=ALU.is_equal).then_inc(dst_hot, 1)
            dve.wait_ge(summed, 1)
            step(dve, nc.vector.tensor_copy(count[:], p_count[0:NB, 0:P]), 1)
            step(dve, nc.vector.tensor_scalar(deg[:], p_deg[:, 0:NB], 1.0, None, ALU.add), 2)
            step(dve, nc.vector.tensor_tensor_scan(out=upto[:], data0=count[:], data1=zero[0:NB, :], initial=0.0, op0=ALU.add, op1=ALU.add), 3)
            step(dve, nc.vector.tensor_scalar(pos[:], deg[:], 0.0, None, ALU.is_gt), 4)
            step(dve, nc.vector.tensor_scalar(K.root[:], deg[:], 1e-30, None, ALU.max), 5)
            dve.wait_ge(off_done, 1)
            step(dve, nc.vector.tensor_sub(upto[:], upto[:], count[:]), 6)
            nc.vector.tensor_scalar(K.place0[:], upto[:], p_off[0:NB, 0:1], None, ALU.add)
            dve.wait_ge(root, 1)
            step(dve, nc.vector.reciprocal(K.dinv[:], K.root[:]), 7)
            nc.vector.tensor_mul(K.dinv[:], K.dinv[:], pos[:])

        @block.tensor
        def _(pe):
            pe.sem_inc(free, 2)
            pe.wait_ge(zeroed, 1)
            nc.tensor.matmul(p_count[0:NB, 0:P], zero[:, 0:NB], zero[:], start=True, stop=False, skip_group_check=True)
            nc.tensor.matmul(p_deg[:, 0:NB], zero[:], zero[:, 0:NB], start=True, stop=False, skip_group_check=True)
            with nc.tensor.Fori(0, NG // 2) as i:
                for h in range(2):
                    pe.wait_ge(src_hot, i * 2 + h + 1)
                    for j in range(G):
                        nc.tensor.matmul(p_count[0:NB, 0:P], oh_hi[:, h, j, :], oh_lo[:, h, j, :], start=False, stop=False, skip_group_check=True)
                    pe.wait_ge(dst_hot, i * 2 + h + 1)
                    for j in range(G):
                        mm = nc.tensor.matmul(p_deg[:, 0:NB], d_lo[:, h, j, :], d_hiw[:, h, j, :], start=False, stop=False, skip_group_check=True)
                    mm.then_inc(free, 1)
            pe.wait_ge(free, NG + 2)
            pe.sem_inc(summed, 1)
            pe.wait_ge(chain, 3)
            nc.tensor.matmul(p_off[0:NB, 0:1], K.above[0:NB, 0:NB], upto[:, P - 1:P], start=True, stop=True).then_inc(off_done, 1)

        @block.scalar
        def _(act):
            act.wait_ge(chain, 5)
            nc.scalar.activation(K.root[:], K.root[:], ACT.Sqrt).then_inc(root, 1)


def layer_norm_stats(nc, K, s):
    st = s.sb("stats", [P, R, 6])
    mv = s.sb("mean_var", [P, NB, 2])
    mv_r = s.sb("mean_var_r", [P, R, 2])
    tick, have, aggregated, copied, chain, root = (s.sem(n) for n in ("tick", "have", "aggregated", "copied", "chain", "root"))
    with nc.Block() as block:
        @block.vector
        def _(dve):
            dve.sem_inc(copied, 1)
            with nc.vector.Fori(0, NI) as i:
                for r in range(R):
                    nc.vector.bn_stats(st[:, r, :], K.x[:, bass.ds(i * R + r, 1), :].rearrange("p a d -> p (a d)")).then_inc(have, 1)
                dve.wait_ge(copied, i + 1)
                dve.wait_ge(have, i * R + R)
                dve.sem_inc(tick, 1)
                for r in range(R):
                    nc.vector.bn_aggr(mv_r[:, r, :], st[:, r, :]).then_inc(aggregated, 1)
                dve.wait_ge(aggregated, i * R + R)
                nc.vector.tensor_copy(mv[:, bass.ds(i * R, R), :], mv_r[:]).then_inc(copied, 1)
            dve.wait_ge(copied, NI + 1)
            nc.vector.tensor_scalar(K.rstd[:], mv[:, :, 1], LN_EPS, None, ALU.add).then_inc(chain, 1)
            dve.wait_ge(root, 1)
            nc.vector.reciprocal(K.rstd[:], K.sd[:]).then_inc(chain, 1)
            dve.wait_ge(chain, 2)
            nc.vector.scalar_tensor_tensor(out=K.shift[:], in0=mv[:, :, 0], scalar=-1.0, in1=K.rstd[:], op0=ALU.mult, op1=ALU.mult)

        @block.scalar
        def _(act):
            act.wait_ge(chain, 1)
            nc.scalar.activation(K.sd[:], K.rstd[:], ACT.Sqrt).then_inc(root, 1)


def normed(nc, K, act, i, to, tick):
    act.sem_inc(tick, 1)
    for r in range(R):
        ins = nc.scalar.activation(to[:, r, :], K.x[:, bass.ds(i * R + r, 1), :].rearrange("p a d -> p (a d)"), ACT.Relu,
                                   bias=K.shift[:, bass.ds(i * R + r, 1)], scale=K.rstd[:, bass.ds(i * R + r, 1)])
    return ins


def in_step(i):
    return bass.ds(i * R * P, R * P)


def nodes_before_filter(nc, K, s):
    hs, hT = s.sb("h", [P, R, D]), s.sb("hT", [P, R, D])
    minus = s.sb("minus", [P, 1])
    p_t = s.ps("p_t", [P, 1024])
    p_y = s.ps("p_y", [P, 512])
    p_b = s.ps("p_b", [1, 512])
    h_ready, turned, copied, projected, kept, tick, biases, filled = (
        s.sem(n) for n in ("h_ready", "turned", "copied", "projected", "kept", "tick", "biases", "filled"))

    with nc.Block() as block:
        @block.scalar
        def _(act):
            with nc.scalar.Fori(0, NI) as i:
                act.wait_ge(copied, i + 1)
                normed(nc, K, act, i, hs, tick).then_inc(h_ready, 1)

        @block.tensor
        def _(pe):
            pe.sem_inc(projected, 1)
            pe.wait_ge(filled, 1)
            nc.tensor.matmul(p_b[0:1, 0:F0], minus[0:F0, 0:1], K.w_f2[0:F0, :], start=True, stop=True)
            nc.tensor.matmul(p_b[0:1, D:2 * D], minus[:, 0:1], K.w_o2[:], start=True, stop=True).then_inc(biases, 1)
            with nc.tensor.Fori(0, NI) as i:
                pe.wait_ge(h_ready, i + 1)
                for r in range(R):
                    tr = nc.tensor.transpose(p_t[:, r * D:(r + 1) * D], hs[:, r, :], K.ident[:])
                tr.then_inc(turned, 1)
                pe.wait_ge(copied, i + 2)
                pe.wait_ge(kept, i + 1)
                for r in range(R):
                    y = p_y[:, r * F0:(r + 1) * F0]
                    nc.tensor.matmul(y, hT[:, r, :], K.w_in[:], start=True, stop=False)
                    mm = nc.tensor.matmul(y, K.ones[0:1, :], K.b_in[:], start=False, stop=True)
                mm.then_inc(projected, 1)

        @block.vector
        def _(dve):
            dve.sem_inc(copied, 1)
            dve.sem_inc(kept, 1)
            nc.vector.memset(minus[:], -LOG2).then_inc(filled, 1)
            nc.vector.memset(K.h_in[:, NB:NB + 1, :], 0.0)
            with nc.vector.Fori(0, NI) as i:
                dve.wait_ge(turned, i + 1)
                dve.wait_ge(projected, i + 1)
                nc.vector.tensor_copy(hT[:].rearrange("p r d -> p (r d)"), p_t[:, 0:R * D]).then_inc(copied, 1)
                dve.wait_ge(projected, i + 2)
                dve.sem_inc(tick, 1)
                nc.vector.tensor_copy(K.h_in[:, bass.ds(i * R, R), :], p_y[:, 0:R * F0].rearrange("p (r f) -> p r f", f=F0)).then_inc(kept, 1)
            dve.wait_ge(biases, 1)
            nc.vector.tensor_add(K.b_f2g[:].rearrange("a (j f) -> a j f", f=F0), K.b_f2[:].unsqueeze(1).broadcast_to([1, G, F0]),
                                 p_b[0:1, 0:F0].unsqueeze(1).broadcast_to([1, G, F0]))
            nc.vector.tensor_add(K.b_o2[:], K.b_o2[:], p_b[0:1, D:2 * D])


def filter_edges(nc, K, Dr, A, s):
    aT = s.sb("attrT", [32, 2, GE])
    dst_b = s.sb("dst_b", [P, 2, GE], I32)
    src_b = s.sb("src_b", [P, 2, GE], I32)
    mag, low = s.sb("mag", [P, GE]), s.sb("low", [P, GE])
    sp = s.sb("softplus", [P, 2, GE])
    ws = s.sb("w_cut", [P, 2, G, F0])
    dhot = s.sb("dst_hotT", [P, 2, G, 2, P])
    oh_hi = s.sb("src_hi_hot", [P, 2, G, NB], BF16)
    oh_lo = s.sb("src_lo_hot", [P, 2, G, P], BF16)
    hiT = s.sb("src_hi_hotT", [NB, 2, GE])
    place = s.sb("place", [NB, 2 * G, P])
    scrap = s.sb("scrap", [P, 2, 2, G, P], BF16)
    before, among = s.sb("before", [P, 2, G]), s.sb("among", [P, 2, G])
    ident16 = s.sb("ident16", [P, P], BF16)
    pos = s.sb("pos", [P, 2, G], I32)
    rows = s.sb("rows", [P, 2, G, XC])
    p_z = s.ps("p_z", [P, 2, 512])
    p_w = s.ps("p_w", [P, G, F0])
    p_hd = s.ps("p_hd", [P, G, F0])
    p_first = s.ps("p_first", [P, 2, 4, P])
    p_new = s.ps("p_new", [NB, 4, P])
    p_hiT = s.ps("p_hiT", [NB, GE], BF16)
    landed = [s.sem("landed0"), s.sem("landed1")]
    scattered = [s.sem("scattered0"), s.sem("scattered1")]
    (z_ready, sp_ready, w_ready, ws_ready, dhot_ready, hd_ready, hot_ready, hiT_ps, hiT_ready, new_ready, place_ready, first_ready,
     pos_ready, rows_ready, summed, tick, chain, a_mag, a_exp, among_ready, before_ready, start16) = (
        s.sem(n) for n in ("z", "sp", "w", "ws", "dhot", "hd", "hot", "hiT_ps", "hiT", "new", "place", "first", "pos", "rows",
                           "summed", "tick", "chain", "mag", "exp", "among", "before", "start"))

    with nc.Block() as block:
        @block.sync
        def _(sp_):
            with nc.sync.Fori(0, NG // 2) as i:
                for h in range(2):
                    edges = bass.ds((i * 2 + h) * GE, GE)
                    sp_.wait_ge(z_ready, 2 * (i * 2 + h) + 2)
                    nc.sync.sem_inc(tick, 1)
                    sp_.wait_ge(pos_ready, i * 2 + h + 1)
                    nc.sync.sem_inc(tick, 1)
                    nc.sync.dma_start(aT[:, h, :], A["attr32T"][:, edges]).then_inc(landed[h], 16)
                    nc.sync.dma_start(dst_b[:, h, :], A["dst_row"][:, edges].broadcast_to([P, GE])).then_inc(landed[h], 16)
                    nc.sync.dma_start(src_b[:, h, :], A["src_row"][:, edges].broadcast_to([P, GE])).then_inc(landed[h], 16)

        @block.tensor
        def _(pe):
            pe.sem_inc(z_ready, 4)
            pe.sem_inc(hd_ready, 2)
            pe.sem_inc(w_ready, 2)
            pe.sem_inc(first_ready, 4)
            pe.sem_inc(new_ready, 4)
            pe.wait_ge(start16, 1)

            def filter_first(g, h, loads):
                pe.wait_ge(landed[h], loads * 48)
                for c in range(2):
                    pe.wait_ge(a_mag, 2 * g + c + 1)
                    nc.tensor.matmul(p_z[:, c, :], K.w_f1[:], aT[:, h, c * 512:(c + 1) * 512], start=True, stop=True).then_inc(z_ready, 1)

            def sources(g, h, c):
                pe.wait_ge(place_ready, 2 * g + c + 1)
                for j in range(4 * c, 4 * c + 4):
                    mm = nc.tensor.matmul(p_new[:, j % 4, :], oh_hi[:, h, j, :], oh_lo[:, h, j, :], start=True, stop=True)
                mm.then_inc(new_ready, 1)

            def turn(g, h):
                pe.wait_ge(hot_ready, g + 1)
                pe.wait_ge(hiT_ready, g + 2)
                pe.sem_inc(tick, 1)
                for j in range(G):
                    tr = nc.tensor.transpose(p_hiT[:, j * P:(j + 1) * P], oh_hi[:, h, j, :], ident16[:])
                tr.then_inc(hiT_ps, 1)

            def group(g, h, loads, last):
                if not last:
                    filter_first(g + 1, 1 - h, loads)
                sources(g, h, 1)
                blk = load_values(nc, PE, K.dst_blk[0:1, bass.ds(g * G, G)], NB - 1)
                pe.wait_ge(dhot_ready, g + 1)
                pe.wait_ge(rows_ready, g + 1)
                pe.sem_inc(tick, 1)
                for j in range(G):
                    nc.tensor.matmul(p_hd[:, j, :], dhot[:, h, j, 0, :], K.h_in[:, bass.ds(blk[j], 1), :].rearrange("p a f -> p (a f)"), start=True, stop=False)
                    mm = nc.tensor.matmul(p_hd[:, j, :], dhot[:, h, j, 1, :], K.h_in[:, bass.ds(blk[j] + 1, 1), :].rearrange("p a f -> p (a f)"), start=False, stop=True)
                mm.then_inc(hd_ready, 1)
                pe.wait_ge(hiT_ready, g + 3)
                for c in range(2):
                    pe.wait_ge(place_ready, 2 * g + c + 2)
                    pe.wait_ge(before_ready, 2 * g + c + 1)
                    for j in range(4 * c, 4 * c + 4):
                        mm = nc.tensor.matmul(p_first[:, c, j % 4, :], hiT[:, h, j * P:(j + 1) * P], place[:, h * G + j, :], start=True, stop=True)
                    mm.then_inc(first_ready, 1)
                pe.wait_ge(sp_ready, g + 1)
                pe.wait_ge(ws_ready, g + 2)
                pe.sem_inc(tick, 1)
                nc.tensor.matmul(p_w[:].rearrange("p j f -> p (j f)"), K.ones[0:1, :], K.b_f2g[:], start=True, stop=False, skip_group_check=True)
                for j in range(G):
                    mm = nc.tensor.matmul(p_w[:, j, :], sp[:, h, j * P:(j + 1) * P], K.w_f2[:], start=False, stop=(j == G - 1), skip_group_check=True)
                mm.then_inc(w_ready, 1)
                if not last:
                    turn(g + 1, 1 - h)
                    sources(g + 1, 1 - h, 0)

            filter_first(0, 0, 1)
            turn(0, 0)
            sources(0, 0, 0)
            with nc.tensor.Fori(0, NG // 2 - 1) as i:
                for h in range(2):
                    group(i * 2 + h, h, i + 1 + h, False)
            group(NG - 2, 0, NG // 2, False)
            group(NG - 1, 1, 0, True)

        @block.scalar
        def _(act):
            act.sem_inc(a_mag, 2)
            act.sem_inc(hiT_ready, 2)
            act.sem_inc(ws_ready, 2)

            def softplus(g, h):
                act.wait_ge(w_ready, g + 1)
                for c in range(2):
                    cols = slice(c * 512, (c + 1) * 512)
                    act.wait_ge(z_ready, 2 * g + c + 5)
                    nc.scalar.activation(mag[F0:P, cols], p_z[F0:P, c, :], ACT.Abs, bias=K.b_f1[F0:P, :]).then_inc(chain, 1)
                    nc.scalar.activation(sp[0:F0, h, cols], p_z[0:F0, c, :], ACT.Relu, bias=K.b_f1[0:F0, :]).then_inc(a_mag, 1)
                act.wait_ge(chain, 2 * g + 2)
                nc.scalar.activation(low[F0:P, :], mag[F0:P, :], ACT.Exp, scale=-1.0).then_inc(a_exp, 1)
                act.wait_ge(a_exp, g + 1)
                nc.scalar.activation(sp[F0:P, h, :], low[F0:P, :], ACT.Ln, bias=K.ones[F0:P, 0:1]).then_inc(sp_ready, 1)

            def keep_turned(g, h):
                act.wait_ge(hiT_ps, g + 1)
                act.wait_ge(first_ready, 2 * g + 2)
                nc.scalar.copy(hiT[:, h, :], p_hiT[:]).then_inc(hiT_ready, 1)

            def group(g, h, last):
                if not last:
                    softplus(g + 1, 1 - h)
                act.wait_ge(w_ready, g + 3)
                act.wait_ge(rows_ready, g + 1)
                act.sem_inc(tick, 1)
                for j in range(G):
                    ins = nc.scalar.activation(ws[:, h, j, :], p_w[:, j, :], ACT.Copy, scale=K.ew[:, bass.ds(g * G + j, 1)])
                ins.then_inc(ws_ready, 1)
                if not last:
                    keep_turned(g + 1, 1 - h)

            softplus(0, 0)
            keep_turned(0, 0)
            with nc.scalar.Fori(0, NG // 2 - 1) as i:
                for h in range(2):
                    group(i * 2 + h, h, False)
            group(NG - 2, 0, False)
            group(NG - 1, 1, True)

        @block.vector
        def _(dve):
            dve.sem_inc(place_ready, 1)
            dve.sem_inc(rows_ready, 1)
            dve.sem_inc(before_ready, 2)
            dve.sem_inc(pos_ready, 2)
            nc.vector.tensor_copy(ident16[:], K.ident[:]).then_inc(start16, 1)
            nc.vector.tensor_copy(place[:, 0, :], K.place0[:]).then_inc(start16, 1)
            dve.wait_ge(start16, 2)

            def source_hots(g, h):
                cols = bass.ds(g * G, G)
                nc.vector.tensor_tensor(out=oh_hi[:, h], in0=K.lane[:, 0:NB].unsqueeze(1).broadcast_to([P, G, NB]),
                                        in1=K.src_hi[:, cols].unsqueeze(2).broadcast_to([P, G, NB]), op=ALU.is_equal)
                nc.vector.tensor_tensor(out=oh_lo[:, h], in0=K.lane[:, 0:P].unsqueeze(1).broadcast_to([P, G, P]),
                                        in1=K.src_lo[:, cols].unsqueeze(2).broadcast_to([P, G, P]), op=ALU.is_equal).then_inc(hot_ready, 1)

            def destination_hots(g, h, loads):
                blk = load_values(nc, DVE, K.dst_blk[0:1, bass.ds(g * G, G)], NB - 1)
                dve.wait_ge(landed[h], loads * 48)
                dve.wait_ge(hd_ready, g + 1)
                dve.sem_inc(tick, 1)
                for j in range(G):
                    for k in range(2):
                        ins = nc.vector.tensor_scalar(dhot[:, h, j, k, :], dst_b[:, h, j * P:(j + 1) * P],
                                                      K.node_col[:, bass.ds(blk[j] + k, 1)], None, ALU.is_equal)
                ins.then_inc(dhot_ready, 1)

            def places(g, h, c):
                dve.wait_ge(new_ready, 2 * g + c + 5)
                for j in range(4 * c, 4 * c + 4):
                    k = h * G + j
                    if j:
                        dve.wait_ge(summed, g * G + j)
                    nc.vector.tensor_add(place[:, (k + 1) % (2 * G), :], place[:, k, :], p_new[:, j % 4, :]).then_inc(summed, 1)
                    if j % 4 == 3:
                        dve.wait_ge(summed, g * G + j + 1)
                        dve.sem_inc(place_ready, 1)
                    ins = nc.vector.scalar_tensor_tensor(out=scrap[:, 0, h, j, :], in0=src_b[:, h, j * P:(j + 1) * P], scalar=K.src_f[:, bass.ds(g * G + j, 1)],
                                                         in1=K.below[:], op0=ALU.is_equal, op1=ALU.mult, accum_out=among[:, h, j:j + 1])
                if c == 1:
                    ins.then_inc(among_ready, 1)

            def positions(g, h, i, first):
                for c in range(2):
                    dve.wait_ge(first_ready, 2 * g + c + 5)
                    dve.sem_inc(tick, 1)
                    for j in range(4 * c, 4 * c + 4):
                        ins = nc.vector.scalar_tensor_tensor(out=scrap[:, 1, h, j, :], in0=K.lane[:, 0:P], scalar=K.src_lo[:, bass.ds(g * G + j, 1)],
                                                             in1=p_first[:, c, j % 4, :], op0=ALU.is_equal, op1=ALU.mult, accum_out=before[:, h, j:j + 1])
                    ins.then_inc(before_ready, 1)
                if not first:
                    dve.wait_ge(scattered[h], i * 16 * G)
                    dve.sem_inc(tick, 1)
                dve.wait_ge(among_ready, g + 1)
                dve.wait_ge(before_ready, 2 * g + 4)
                nc.vector.tensor_add(pos[:, h, :], before[:, h, :], among[:, h, :]).then_inc(pos_ready, 1)
                dve.wait_ge(pos_ready, g + 3)
                dve.sem_inc(tick, 1)
                nc.vector.tensor_copy(K.pos[:, bass.ds(g * G, G)], pos[:, h, :])

            def products(g, h):
                nc.vector.tensor_copy(rows[:, h, :, F0], K.src_f[:, bass.ds(g * G, G)])
                dve.wait_ge(ws_ready, g + 3)
                dve.wait_ge(hd_ready, g + 3)
                nc.vector.tensor_mul(rows[:, h, :, 0:F0], p_hd[:], ws[:, h]).then_inc(rows_ready, 1)

            def group(i, h, first, last):
                g = i * 2 + h
                if not last:
                    source_hots(g + 1, 1 - h)
                if not (first and h == 0):
                    products(g - 1, 1 - h)
                places(g, h, 0)
                places(g, h, 1)
                if not last:
                    destination_hots(g + 1, 1 - h, i + 1 + h)
                positions(g, h, i, first)

            source_hots(0, 0)
            destination_hots(0, 0, 1)
            for h in range(2):
                group(0, h, True, False)
            with nc.vector.Fori(1, NG // 2 - 1) as i:
                for h in range(2):
                    group(i, h, False, False)
            group(NG // 2 - 1, 0, False, False)
            group(NG // 2 - 1, 1, False, True)
            products(NG - 1, 1)

        @block.gpsimd
        def _(pool):
            with nc.gpsimd.Fori(0, NG // 2) as i:
                for h in range(2):
                    g = i * 2 + h
                    pool.wait_ge(pos_ready, g + 3)
                    pool.wait_ge(rows_ready, g + 2)
                    pool.sem_inc(tick, 1)
                    for j in range(G):
                        nc.gpsimd.indirect_dma_start(Dr.by_src0, bass.IndirectOffsetOnAxis(pos[:, h, j:j + 1], 0), rows[:, h, j, :], None).then_inc(scattered[h], 16)
            for h in range(2):
                pool.wait_ge(scattered[h], NG // 2 * G * 16)


def sum_by_source(nc, K, Dr, s):
    rows = s.sb("rows", [P, 2, G, XC])
    hot = s.sb("hot", [P, 2, G, P])
    p_sum = s.ps("p_sum", [F0, 2, 4, P])
    landed = [s.sem("landed0"), s.sem("landed1")]
    numbered, hot_ready, summed, added, tick, noted, cleared = (s.sem(n) for n in ("numbered", "hot", "summed", "added", "tick", "noted", "cleared"))
    with nc.Block() as block:
        @block.sync
        def _(sp):
            with nc.sync.Fori(0, NG // 2) as i:
                for h in range(2):
                    g = i * 2 + h
                    sp.wait_ge(summed, 2 * g + 2)
                    nc.sync.sem_inc(tick, 1)
                    nc.sync.dma_start(rows[:, h], Dr.by_src0[bass.ds(g * GE, GE), :].rearrange("(j p) f -> p j f", p=P)).then_inc(landed[h], 16)

        @block.gpsimd
        def _(pool):
            nc.gpsimd.iota(K.node_row[:], [[1, NW]], base=0, channel_multiplier=0, allow_small_or_imprecise_dtypes=True).then_inc(numbered, 1)
            with nc.gpsimd.Fori(0, NG // 2) as i:
                for h in range(2):
                    g = i * 2 + h
                    pool.wait_ge(landed[h], i * 16 + 16)
                    pool.sem_inc(tick, 1)
                    nc.gpsimd.tensor_copy(K.srt_f[:, bass.ds(g * G, G)], rows[:, h, :, F0])
                    nc.gpsimd.tensor_copy(K.srt_i[0:1, bass.ds(g * G, G)], rows[0:1, h, :, F0]).then_inc(noted, 1)

        @block.vector
        def _(dve):
            dve.sem_inc(added, G)
            nc.vector.memset(K.acc[:], 0.0).then_inc(cleared, 1)
            dve.wait_ge(cleared, 1)
            dve.wait_ge(numbered, 1)

            def first_nodes(g):
                return load_values(nc, DVE, K.srt_i[0:1, bass.ds(g * G, G)], N)

            def one_hot(h, j, at):
                ins = nc.vector.tensor_scalar(hot[:, h, j, :], K.node_row[:, bass.ds(at[j], P)], rows[:, h, j, F0:XC], None, ALU.is_equal)
                if j % 4 == 3:
                    ins.then_inc(hot_ready, 1)

            def group(g, h, last):
                if not last:
                    dve.wait_ge(noted, g + 2)
                    dve.wait_ge(summed, 2 * g + 4)
                    dve.sem_inc(tick, 1)
                    ahead = first_nodes(g + 1)
                at = first_nodes(g)
                for j in range(G):
                    if not last:
                        one_hot(1 - h, j, ahead)
                    if j % 4 == 0:
                        dve.wait_ge(summed, 2 * g + j // 4 + 5)
                    dve.wait_ge(added, (g + 1) * G + j)
                    window = K.acc[0:F0, bass.ds(at[j], P)]
                    nc.vector.tensor_tensor(out=window, in0=window, in1=p_sum[:, j // 4, j % 4, :], op=ALU.add).then_inc(added, 1)

            dve.wait_ge(noted, 1)
            dve.wait_ge(summed, 4)
            dve.sem_inc(tick, 1)
            at = first_nodes(0)
            for j in range(G):
                one_hot(0, j, at)
            with nc.vector.Fori(0, NG // 2 - 1) as i:
                for h in range(2):
                    group(i * 2 + h, h, False)
            group(NG - 2, 0, False)
            group(NG - 1, 1, True)

        @block.tensor
        def _(pe):
            pe.sem_inc(summed, 4)
            with nc.tensor.Fori(0, NG // 2) as i:
                for h in range(2):
                    g = i * 2 + h
                    pe.wait_ge(landed[h], i * 16 + 16)
                    pe.wait_ge(noted, g + 1)
                    for c in range(2):
                        pe.wait_ge(hot_ready, 2 * g + c + 1)
                        pe.wait_ge(added, g * G + 4 * c + 4)
                        for j in range(4 * c, 4 * c + 4):
                            mm = nc.tensor.matmul(p_sum[:, c, j % 4, :], rows[:, h, j, 0:F0], hot[:, h, j, :], start=True, stop=True)
                        mm.then_inc(summed, 1)


def sorted_row(nc, K, Dr, s):
    turned = s.sb("turned", [P, -(-T // P), P])
    p_t = s.ps("p_t", [P, -(-T // 512), 512])
    p_first = s.ps("p_first", [P, 2, 1024])
    t_ready, c_ready, f_ready, stored = s.sem("t"), s.sem("c"), s.sem("f"), s.sem("stored")
    chunks = [(c, min(P, T - c * P)) for c in range(-(-T // P))]
    with nc.Block() as block:
        @block.tensor
        def _(pe):
            for k, numbers in enumerate((K.srt_f, K.dst_f)):
                for c in range(0, T, 512):
                    n = min(512, T - c)
                    mm = nc.tensor.matmul(p_first[:, k, c:c + n], K.ones[0:1, :], numbers[0:1, c:c + n], start=True, stop=True)
                mm.then_inc(f_ready, 1)
            for c, n in chunks:
                nc.tensor.transpose(p_t[0:n, c // 4, c % 4 * P:(c % 4 + 1) * P], K.srt_f[:, c * P:c * P + n], K.ident[:]).then_inc(t_ready, 1)

        @block.vector
        def _(dve):
            nc.vector.tensor_single_scalar(K.srt_blk[:], K.srt_i[:], 7, ALU.logical_shift_right)
            for k, (numbers, within) in enumerate(((K.srt_f, K.srt_in), (K.dst_f, K.dst_in))):
                dve.wait_ge(f_ready, k + 1)
                nc.vector.tensor_sub(within[:], numbers[:], p_first[:, k, 0:T])
            dve.wait_ge(t_ready, len(chunks))
            for c, n in chunks:
                nc.vector.tensor_copy(turned[0:n, c, :], p_t[0:n, c // 4, c % 4 * P:(c % 4 + 1) * P]).then_inc(c_ready, 1)

        @block.sync
        def _(sp):
            for c, n in chunks:
                sp.wait_ge(c_ready, c + 1)
                nc.sync.dma_start(Dr.srt.rearrange("a (t p) -> (a t) p", p=P)[c * P:c * P + n, :], turned[0:n, c, :]).then_inc(stored, 16)
            sp.wait_ge(stored, 16 * len(chunks))


def nodes_after_filter(nc, K, s):
    C = R * P
    mag, low, re, ln = s.sb("mag", [D, C]), s.sb("low", [D, C]), s.sb("relu", [D, C]), s.sb("ln", [D, C])
    p_u, p_o = s.ps("p_u", [D, 2, 512]), s.ps("p_o", [P, 1024])
    u_ready, m_ready, e_ready, sp_ready, o_ready, added, tick = (s.sem(n) for n in ("u", "m", "e", "sp", "o", "added", "tick"))
    with nc.Block() as block:
        @block.tensor
        def _(pe):
            pe.sem_inc(o_ready, 1)
            with nc.tensor.Fori(0, NI) as i:
                pe.wait_ge(sp_ready, i + 1)
                pe.sem_inc(tick, 1)
                for c in range(2):
                    mm = nc.tensor.matmul(p_u[:, c, 0:C // 2], K.w_o1[:], K.acc[0:F0, bass.ds(i * C + c * (C // 2), C // 2)], start=True, stop=True)
                mm.then_inc(u_ready, 1)
                pe.wait_ge(sp_ready, i + 2)
                pe.wait_ge(added, i + 1)
                for r in range(R):
                    o, cols = p_o[:, r * D:(r + 1) * D], slice(r * P, (r + 1) * P)
                    nc.tensor.matmul(o, re[:, cols], K.w_o2[:], start=True, stop=False)
                    nc.tensor.matmul(o, ln[:, cols], K.w_o2[:], start=False, stop=False)
                    mm = nc.tensor.matmul(o, K.ones[0:1, :], K.b_o2[:], start=False, stop=True)
                mm.then_inc(o_ready, 1)

        @block.scalar
        def _(act):
            act.sem_inc(sp_ready, 1)
            with nc.scalar.Fori(0, NI) as i:
                act.wait_ge(u_ready, i + 1)
                act.wait_ge(o_ready, i + 1)
                nc.scalar.activation(mag[:].rearrange("p (c n) -> p c n", c=2), p_u[:, :, 0:C // 2], ACT.Abs, bias=K.b_o1[:]).then_inc(m_ready, 1)
                nc.scalar.activation(re[:].rearrange("p (c n) -> p c n", c=2), p_u[:, :, 0:C // 2], ACT.Relu, bias=K.b_o1[:])
                act.wait_ge(m_ready, i + 1)
                nc.scalar.activation(low[:], mag[:], ACT.Exp, scale=-1.0).then_inc(e_ready, 1)
                act.wait_ge(e_ready, i + 1)
                nc.scalar.activation(ln[:], low[:], ACT.Ln, bias=K.ones[:, 0:1]).then_inc(sp_ready, 1)

        @block.vector
        def _(dve):
            dve.sem_inc(added, 1)
            with nc.vector.Fori(0, NI) as i:
                x = K.x[:, bass.ds(i * R, R), :]
                dve.wait_ge(o_ready, i + 2)
                nc.vector.tensor_tensor(out=x, in0=x, in1=p_o[:, 0:R * D].rearrange("p (r d) -> p r d", d=D), op=ALU.add).then_inc(added, 1)


def nodes_before_gcn(nc, K, Dr, s):
    hs, dh = s.sb("h", [P, R, D]), s.sb("dh", [P, R, D])
    p_t = s.ps("p_t", [P, 1024])
    h_ready, x_ready, dh_ready, turned, kept, stored, tick = (s.sem(n) for n in ("h", "x", "dh", "t", "kept", "stored", "tick"))
    with nc.Block() as block:
        @block.scalar
        def _(act):
            with nc.scalar.Fori(0, NI) as i:
                act.wait_ge(dh_ready, i + 1)
                normed(nc, K, act, i, hs, tick).then_inc(h_ready, 1)

        @block.vector
        def _(dve):
            dve.sem_inc(dh_ready, 1)
            dve.sem_inc(kept, 1)
            nc.vector.memset(K.acc[:, NR:NW], 0.0)
            with nc.vector.Fori(0, NI) as i:
                x = K.x[:, bass.ds(i * R, R), :]
                dve.wait_ge(h_ready, i + 1)
                nc.vector.tensor_tensor(out=x, in0=x, in1=hs[:], op=ALU.add)
                dve.wait_ge(stored, i * 16 + 16)
                dve.wait_ge(kept, i + 1)
                nc.vector.tensor_tensor(out=dh[:], in0=hs[:], in1=K.dinv[:, bass.ds(i * R, R)].unsqueeze(2).broadcast_to([P, R, D]), op=ALU.mult).then_inc(dh_ready, 1)
                dve.wait_ge(turned, i + 1)
                dve.sem_inc(tick, 1)
                nc.vector.tensor_copy(K.acc[:, in_step(i)], p_t[:, 0:R * P]).then_inc(kept, 1)

        @block.tensor
        def _(pe):
            with nc.tensor.Fori(0, NI) as i:
                pe.wait_ge(dh_ready, i + 2)
                pe.wait_ge(kept, i + 1)
                for r in range(R):
                    tr = nc.tensor.transpose(p_t[:, r * P:(r + 1) * P], dh[:, r, :], K.ident[:])
                tr.then_inc(turned, 1)

        @block.sync
        def _(sp):
            sp.sem_inc(stored, 16)
            with nc.sync.Fori(0, NI) as i:
                sp.wait_ge(dh_ready, i + 2)
                sp.sem_inc(tick, 1)
                nc.sync.dma_start(Dr.table.rearrange("(b p) d -> p b d", p=P)[:, bass.ds(i * R, R), :], dh[:]).then_inc(stored, 16)
            sp.wait_ge(stored, 16 * NI + 16)


def sum_by_target(nc, K, Dr, A, s, gine):
    idx = s.sb("idx", [P, 2, G], I32)
    rows = s.sb("rows", [P, 2, G, D])
    hot = s.sb("hot", [P, 2, G, P])
    p_sum = s.ps("p_sum", [D, 2, 4, P])
    if gine:
        aT = s.sb("attrT", [16, 2, GE])
        msg = s.sb("msg", [P, 2, G, D])
        p_msg = s.ps("p_msg", [P, 2, 4, D])
    loads = 2 if gine else 1
    landed = [s.sem("landed0"), s.sem("landed1")]
    fetched = [s.sem("fetched0"), s.sem("fetched1")]
    hot_ready, summed, added, tick, m_ready, msg_ready = (s.sem(n) for n in ("hot", "summed", "added", "tick", "m", "msg"))
    used = m_ready if gine else summed
    with nc.Block() as block:
        @block.sync
        def _(sp):
            with nc.sync.Fori(0, NG // 2) as i:
                for h in range(2):
                    g = i * 2 + h
                    sp.wait_ge(used, 2 * g + 2)
                    sp.sem_inc(tick, 1)
                    nc.sync.dma_start(idx[:, h, :], A["src"][:, bass.ds(g * G, G)]).then_inc(landed[h], 16)
                    if gine:
                        nc.sync.dma_start(aT[:, h, :], A["attr16T"][:, bass.ds(g * GE, GE)]).then_inc(landed[h], 16)

        @block.gpsimd
        def _(pool):
            with nc.gpsimd.Fori(0, NG // 2) as i:
                for h in range(2):
                    pool.wait_ge(landed[h], (i + 1) * 16 * loads)
                    pool.sem_inc(tick, 1)
                    for j in range(G):
                        nc.gpsimd.indirect_dma_start(rows[:, h, j, :], None, Dr.table, bass.IndirectOffsetOnAxis(idx[:, h, j:j + 1], 0)).then_inc(fetched[h], 16)

        @block.vector
        def _(dve):
            dve.sem_inc(added, G)

            def one_hot(g, h, j):
                to, weight = K.dst_in[:, bass.ds(g * G + j, 1)], K.ew[:, bass.ds(g * G + j, 1)]
                if gine:
                    ins = nc.vector.tensor_scalar(hot[:, h, j, :], K.lane[:, 0:P], to, None, ALU.is_equal)
                else:
                    ins = nc.vector.tensor_scalar(hot[:, h, j, :], K.lane[:, 0:P], to, weight, ALU.is_equal, ALU.mult)
                if j % 4 == 3:
                    ins.then_inc(hot_ready, 1)

            def group(g, h, last):
                at = load_values(nc, DVE, K.dst_i[0:1, bass.ds(g * G, G)], N)
                if not last:
                    dve.wait_ge(summed, 2 * g + 4)
                    dve.sem_inc(tick, 1)
                for j in range(G):
                    if not last:
                        one_hot(g + 1, 1 - h, j)
                    if j % 4 == 0:
                        dve.wait_ge(summed, 2 * g + j // 4 + 5)
                    dve.wait_ge(added, (g + 1) * G + j)
                    window = K.acc[:, bass.ds(at[j], P)]
                    nc.vector.tensor_tensor(out=window, in0=window, in1=p_sum[:, j // 4, j % 4, :], op=ALU.add).then_inc(added, 1)

            for j in range(G):
                one_hot(0, 0, j)
            with nc.vector.Fori(0, NG // 2 - 1) as i:
                for h in range(2):
                    group(i * 2 + h, h, False)
            group(NG - 2, 0, False)
            group(NG - 1, 1, True)

        @block.tensor
        def _(pe):
            pe.sem_inc(summed, 4)
            if gine:
                pe.sem_inc(m_ready, 4)
            with nc.tensor.Fori(0, NG // 2) as i:
                for h in range(2):
                    g = i * 2 + h
                    pe.wait_ge(fetched[h], (i + 1) * 16 * G)
                    if gine:
                        pe.wait_ge(landed[h], (i + 1) * 32)
                        for c in range(2):
                            pe.wait_ge(msg_ready, 2 * g + c + 1)
                            for j in range(4 * c, 4 * c + 4):
                                nc.tensor.matmul(p_msg[:, c, j % 4, :], aT[:, h, j * P:(j + 1) * P], K.wc[:], start=True, stop=False)
                                mm = nc.tensor.matmul(p_msg[:, c, j % 4, :], K.ident[:], rows[:, h, j, :], start=False, stop=True)
                            mm.then_inc(m_ready, 1)
                    for c in range(2):
                        pe.wait_ge(hot_ready, 2 * g + c + 1)
                        pe.wait_ge(added, g * G + 4 * c + 4)
                        if gine:
                            pe.wait_ge(msg_ready, 2 * g + c + 3)
                        for j in range(4 * c, 4 * c + 4):
                            mm = nc.tensor.matmul(p_sum[:, c, j % 4, :], (msg if gine else rows)[:, h, j, :], hot[:, h, j, :], start=True, stop=True)
                        mm.then_inc(summed, 1)

        if gine:
            @block.scalar
            def _(act):
                act.sem_inc(msg_ready, 2)
                with nc.scalar.Fori(0, NG // 2) as i:
                    for h in range(2):
                        g = i * 2 + h
                        act.wait_ge(summed, 2 * g + 2)
                        for c in range(2):
                            act.wait_ge(m_ready, 2 * g + c + 5)
                            nc.scalar.activation(msg[:, h, 4 * c:4 * c + 4, :], p_msg[:, c], ACT.Relu).then_inc(msg_ready, 1)


def nodes_after_gcn(nc, K, s):
    sums, t, z = s.sb("sums", [D, R * P]), s.sb("t", [P, R, D]), s.sb("z", [P, R, D])
    p_o = s.ps("p_o", [P, 1024])
    s_ready, o_ready, t_ready, z_ready, added, tick = (s.sem(n) for n in ("s", "o", "t", "z", "added", "tick"))
    with nc.Block() as block:
        @block.scalar
        def _(act):
            with nc.scalar.Fori(0, NI) as i:
                act.wait_ge(o_ready, i + 1)
                act.sem_inc(tick, 1)
                nc.scalar.copy(sums[:], K.acc[:, in_step(i)]).then_inc(s_ready, 1)

        @block.tensor
        def _(pe):
            pe.sem_inc(o_ready, 1)
            with nc.tensor.Fori(0, NI) as i:
                pe.wait_ge(s_ready, i + 1)
                pe.wait_ge(t_ready, i + 1)
                for r in range(R):
                    mm = nc.tensor.matmul(p_o[:, r * D:(r + 1) * D], sums[:, r * P:(r + 1) * P], K.w1[:], start=True, stop=True)
                mm.then_inc(o_ready, 1)

        @block.vector
        def _(dve):
            dve.sem_inc(t_ready, 1)
            dve.sem_inc(added, 1)
            with nc.vector.Fori(0, NI) as i:
                x = K.x[:, bass.ds(i * R, R), :]
                dve.wait_ge(o_ready, i + 2)
                nc.vector.tensor_tensor(out=t[:], in0=p_o[:, 0:R * D].rearrange("p (r d) -> p r d", d=D),
                                        in1=K.dinv[:, bass.ds(i * R, R)].unsqueeze(2).broadcast_to([P, R, D]), op=ALU.mult).then_inc(t_ready, 1)
                dve.wait_ge(t_ready, i + 2)
                dve.wait_ge(added, i + 1)
                nc.vector.tensor_tensor(out=z[:], in0=t[:], in1=K.b1[:].unsqueeze(1).broadcast_to([P, R, D]), op=ALU.add).then_inc(z_ready, 1)
                dve.wait_ge(z_ready, i + 1)
                nc.vector.scalar_tensor_tensor(out=x, in0=z[:], scalar=0.0, in1=x, op0=ALU.max, op1=ALU.add).then_inc(added, 1)


def nodes_before_attention(nc, K, s):
    hs, hT = s.sb("h", [P, R, D]), s.sb("hT", [P, R, D])
    p_t, p_q, p_kv = s.ps("p_t", [P, 1024]), s.ps("p_q", [P, 4, D]), s.ps("p_kv", [P, 4, 2 * D])
    p_x = s.ps("p_x", [P, 512])
    h_ready, turned, copied, made, q_kept, kv_kept, tick, mixed = (s.sem(n) for n in ("h", "t", "copied", "made", "q", "kv", "tick", "mixed"))
    parts = [(0, 4), (4, 3)]
    with nc.Block() as block:
        @block.scalar
        def _(act):
            act.sem_inc(q_kept, 1)
            with nc.scalar.Fori(0, NI) as i:
                act.wait_ge(copied, i + 1)
                normed(nc, K, act, i, hs, tick).then_inc(h_ready, 1)
                for c, (r, n) in enumerate(parts):
                    act.wait_ge(made, 2 * i + c + 2)
                    act.sem_inc(tick, 1)
                    nc.scalar.copy(K.q[:, bass.ds(i * R + r, n), :], p_q[:, 0:n, :]).then_inc(q_kept, 1)

        @block.tensor
        def _(pe):
            pe.sem_inc(made, 1)
            nc.tensor.matmul(p_x[:, 0:H], K.rep[:], K.w_exp[:], start=True, stop=True).then_inc(mixed, 1)
            with nc.tensor.Fori(0, NI) as i:
                pe.wait_ge(h_ready, i + 1)
                for r in range(R):
                    tr = nc.tensor.transpose(p_t[:, r * P:(r + 1) * P], hs[:, r, :], K.ident[:])
                tr.then_inc(turned, 1)
                pe.wait_ge(copied, i + 2)
                for c, (r, n) in enumerate(parts):
                    pe.wait_ge(q_kept, 2 * i + c + 1)
                    pe.wait_ge(kv_kept, 2 * i + c + 1)
                    for m in range(n):
                        nc.tensor.matmul(p_q[:, m, :], hT[:, r + m, :], K.wqkv[:, 0:D], start=True, stop=True)
                        mm = nc.tensor.matmul(p_kv[:, m, :], hT[:, r + m, :], K.wqkv[:, D:], start=True, stop=True)
                    mm.then_inc(made, 1)

        @block.vector
        def _(dve):
            dve.sem_inc(copied, 1)
            dve.sem_inc(kv_kept, 1)
            nc.vector.memset(K.q[:, NB:NB + 1, :], 0.0)
            nc.vector.memset(K.kv[:, NB:NB + 1, :], 0.0)
            dve.wait_ge(mixed, 1)
            nc.vector.tensor_scalar(K.mix[:], p_x[:, 0:H], float(HD) ** -0.5, None, ALU.mult)
            with nc.vector.Fori(0, NI) as i:
                dve.wait_ge(turned, i + 1)
                dve.wait_ge(made, 2 * i + 1)
                nc.vector.tensor_copy(hT[:].rearrange("p r d -> p (r d)"), p_t[:, 0:R * D]).then_inc(copied, 1)
                for c, (r, n) in enumerate(parts):
                    dve.wait_ge(made, 2 * i + c + 2)
                    dve.sem_inc(tick, 1)
                    nc.vector.tensor_copy(K.kv[:, bass.ds(i * R + r, n), :], p_kv[:, 0:n, :]).then_inc(kv_kept, 1)


def key_value_edges(nc, K, Dr, A, s):
    aT, dst_b = s.sb("attrT", [D, 2, GE]), s.sb("dst_b", [P, 2, GE], I32)
    dhot = s.sb("dst_hotT", [P, 2, G, 2, P])
    rows = s.sb("rows", [P, 2, G, 2 * D])
    pos = s.sb("pos", [P, 2, G], I32)
    p_kv = s.ps("p_kv", [P, 2, 4, 512])
    landed = [s.sem("landed0"), s.sem("landed1")]
    scattered = [s.sem("scattered0"), s.sem("scattered1")]
    dhot_ready, kv_ready, copied, pos_ready, tick = (s.sem(n) for n in ("dhot", "kv", "copied", "pos", "tick"))
    with nc.Block() as block:
        @block.sync
        def _(sp):
            with nc.sync.Fori(0, NG // 2) as i:
                for h in range(2):
                    g = i * 2 + h
                    sp.wait_ge(kv_ready, 4 * g + 4)
                    sp.sem_inc(tick, 1)
                    nc.sync.dma_start(aT[:, h, :], A["attr128T"][:, bass.ds(g * GE, GE)]).then_inc(landed[h], 16)
                    nc.sync.dma_start(dst_b[:, h, :], A["dst_row"][:, bass.ds(g * GE, GE)].broadcast_to([P, GE])).then_inc(landed[h], 16)

        @block.vector
        def _(dve):
            def pair(i, first):
                for h in range(2):
                    g = i * 2 + h
                    blk = load_values(nc, DVE, K.dst_blk[0:1, bass.ds(g * G, G)], NB - 1)
                    dve.wait_ge(landed[h], i * 32 + 32)
                    dve.wait_ge(kv_ready, 4 * g + 4)
                    dve.sem_inc(tick, 1)
                    for j in range(G):
                        for k in range(2):
                            ins = nc.vector.tensor_scalar(dhot[:, h, j, k, :], dst_b[:, h, j * P:(j + 1) * P],
                                                          K.node_col[:, bass.ds(blk[j] + k, 1)], None, ALU.is_equal)
                        if j % 2:
                            ins.then_inc(dhot_ready, 1)
                    if not first:
                        dve.wait_ge(scattered[h], i * 16 * G)
                        dve.sem_inc(tick, 1)
                    nc.vector.tensor_copy(pos[:, h, :], K.pos[:, bass.ds(g * G, G)]).then_inc(pos_ready, 1)

            pair(0, True)
            with nc.vector.Fori(1, NG // 2) as i:
                pair(i, False)

        @block.tensor
        def _(pe):
            pe.sem_inc(kv_ready, 8)
            with nc.tensor.Fori(0, NG // 2) as i:
                for h in range(2):
                    g = i * 2 + h
                    blk = load_values(nc, PE, K.dst_blk[0:1, bass.ds(g * G, G)], NB - 1)
                    pe.wait_ge(landed[h], i * 32 + 32)
                    for c in range(4):
                        pe.wait_ge(copied, 4 * g + c + 1)
                        pe.wait_ge(dhot_ready, 4 * g + c + 1)
                        pe.sem_inc(tick, 1)
                        for m in range(2):
                            j = 2 * c + m
                            to = p_kv[:, h, c, m * 2 * D:(m + 1) * 2 * D]
                            nc.tensor.matmul(to, aT[:, h, j * P:(j + 1) * P], K.wekv[:], start=True, stop=False)
                            nc.tensor.matmul(to, dhot[:, h, j, 0, :], K.kv[:, bass.ds(blk[j], 1), :].rearrange("p a f -> p (a f)"), start=False, stop=False)
                            mm = nc.tensor.matmul(to, dhot[:, h, j, 1, :], K.kv[:, bass.ds(blk[j] + 1, 1), :].rearrange("p a f -> p (a f)"), start=False, stop=True)
                        mm.then_inc(kv_ready, 1)

        @block.scalar
        def _(act):
            act.sem_inc(copied, 8)

            def pair(i, first):
                for h in range(2):
                    g = i * 2 + h
                    if not first:
                        act.wait_ge(scattered[h], i * 16 * G)
                    for c in range(4):
                        act.wait_ge(kv_ready, 4 * g + c + 9)
                        nc.scalar.copy(rows[:, h, 2 * c:2 * c + 2, :].rearrange("p m f -> p (m f)"), p_kv[:, h, c, :]).then_inc(copied, 1)

            pair(0, True)
            with nc.scalar.Fori(1, NG // 2) as i:
                pair(i, False)

        @block.gpsimd
        def _(pool):
            with nc.gpsimd.Fori(0, NG // 2) as i:
                for h in range(2):
                    g = i * 2 + h
                    pool.wait_ge(pos_ready, g + 1)
                    for c in range(4):
                        pool.wait_ge(copied, 4 * g + c + 9)
                        pool.sem_inc(tick, 1)
                        for j in range(2 * c, 2 * c + 2):
                            nc.gpsimd.indirect_dma_start(Dr.by_src2, bass.IndirectOffsetOnAxis(pos[:, h, j:j + 1], 0), rows[:, h, j, :], None).then_inc(scattered[h], 16)
            for h in range(2):
                pool.wait_ge(scattered[h], NG // 2 * G * 16)


def attention_logits(nc, K, Dr, s):
    kk, src_b = s.sb("kk", [P, 2, G, D]), s.sb("src_b", [P, 2, GE])
    shot = s.sb("src_hotT", [P, 2, G, 2, P])
    prod, prodT = s.sb("prod", [P, 2, G, D]), s.sb("prodT", [D, 2, GE])
    logit = s.sb("logit", [H, 2, GE])
    p_q, p_t, p_a = s.ps("p_q", [P, 2, 4, D]), s.ps("p_t", [D, 2, 512]), s.ps("p_a", [H, 2, 512])
    landed = [s.sem("landed0"), s.sem("landed1")]
    stored = [s.sem("stored0"), s.sem("stored1")]
    shot_ready, q_ready, prod_ready, t_ready, prodT_ready, a_ready, logit_ready, tick = (s.sem(n) for n in ("shot", "q", "prod", "t", "prodT", "a", "logit", "tick"))
    with nc.Block() as block:
        @block.sync
        def _(sp):
            sp.sem_inc(stored[0], 16)
            sp.sem_inc(stored[1], 16)
            with nc.sync.Fori(0, NG // 2) as i:
                for h in range(2):
                    g = i * 2 + h
                    sp.wait_ge(prod_ready, 2 * g + 2)
                    sp.sem_inc(tick, 1)
                    nc.sync.dma_start(kk[:, h], Dr.by_src2[bass.ds(g * GE, GE), 0:D].rearrange("(j p) f -> p j f", p=P)).then_inc(landed[h], 16)
                    nc.sync.dma_start(src_b[:, h, :], Dr.srt[:, bass.ds(g * GE, GE)].broadcast_to([P, GE])).then_inc(landed[h], 16)

        @block.vector
        def _(dve):
            dve.sem_inc(prod_ready, 4)
            with nc.vector.Fori(0, NG // 2) as i:
                for h in range(2):
                    g = i * 2 + h
                    blk = load_values(nc, DVE, K.srt_blk[0:1, bass.ds(g * G, G)], NB - 1)
                    dve.wait_ge(landed[h], i * 32 + 32)
                    dve.wait_ge(q_ready, 2 * g + 2)
                    dve.sem_inc(tick, 1)
                    for c in range(2):
                        for j in range(4 * c, 4 * c + 4):
                            for k in range(2):
                                ins = nc.vector.tensor_scalar(shot[:, h, j, k, :], src_b[:, h, j * P:(j + 1) * P],
                                                              K.node_col[:, bass.ds(blk[j] + k, 1)], None, ALU.is_equal)
                        ins.then_inc(shot_ready, 1)
                    dve.wait_ge(t_ready, 2 * g + 2)
                    for c in range(2):
                        dve.wait_ge(q_ready, 2 * g + c + 5)
                        nc.vector.tensor_tensor(out=prod[:, h, 4 * c:4 * c + 4, :], in0=p_q[:, c], in1=kk[:, h, 4 * c:4 * c + 4, :], op=ALU.mult).then_inc(prod_ready, 1)

        @block.tensor
        def _(pe):
            pe.sem_inc(q_ready, 4)
            pe.sem_inc(t_ready, 4)
            pe.sem_inc(a_ready, 4)
            with nc.tensor.Fori(0, NG // 2) as i:
                for h in range(2):
                    g = i * 2 + h
                    blk = load_values(nc, PE, K.srt_blk[0:1, bass.ds(g * G, G)], NB - 1)
                    for c in range(2):
                        pe.wait_ge(shot_ready, 2 * g + c + 1)
                        pe.wait_ge(prod_ready, 2 * g + c + 3)
                        pe.sem_inc(tick, 1)
                        for j in range(4 * c, 4 * c + 4):
                            nc.tensor.matmul(p_q[:, c, j % 4, :], shot[:, h, j, 0, :], K.q[:, bass.ds(blk[j], 1), :].rearrange("p a f -> p (a f)"), start=True, stop=False)
                            mm = nc.tensor.matmul(p_q[:, c, j % 4, :], shot[:, h, j, 1, :], K.q[:, bass.ds(blk[j] + 1, 1), :].rearrange("p a f -> p (a f)"), start=False, stop=True)
                        mm.then_inc(q_ready, 1)
                    for c in range(2):
                        pe.wait_ge(prod_ready, 2 * g + c + 5)
                        pe.wait_ge(prodT_ready, 2 * g + c + 1)
                        for j in range(4 * c, 4 * c + 4):
                            tr = nc.tensor.transpose(p_t[:, c, (j % 4) * P:(j % 4 + 1) * P], prod[:, h, j, :], K.ident[:])
                        tr.then_inc(t_ready, 1)
                    for c in range(2):
                        pe.wait_ge(prodT_ready, 2 * g + c + 3)
                        pe.wait_ge(logit_ready, 2 * g + c + 1)
                        nc.tensor.matmul(p_a[:, c, :], K.mix[:], prodT[:, h, c * 512:(c + 1) * 512], start=True, stop=True).then_inc(a_ready, 1)

        @block.scalar
        def _(act):
            act.sem_inc(prodT_ready, 2)
            act.sem_inc(logit_ready, 2)
            with nc.scalar.Fori(0, NG // 2) as i:
                for h in range(2):
                    g = i * 2 + h
                    act.wait_ge(a_ready, 2 * g + 2)
                    for c in range(2):
                        act.wait_ge(t_ready, 2 * g + c + 5)
                        nc.scalar.copy(prodT[:, h, c * 512:(c + 1) * 512], p_t[:, c, :]).then_inc(prodT_ready, 1)
                    act.wait_ge(stored[h], i * 16 + 16)
                    for c in range(2):
                        act.wait_ge(a_ready, 2 * g + c + 5)
                        nc.scalar.copy(logit[:, h, c * 512:(c + 1) * 512], p_a[:, c, :]).then_inc(logit_ready, 1)
                    act.wait_ge(logit_ready, 2 * g + 4)
                    act.sem_inc(tick, 1)
                    nc.scalar.dma_start(Dr.logitT[:, bass.ds(g * GE, GE)], logit[:, h, :]).then_inc(stored[h], 16)
            for h in range(2):
                act.wait_ge(stored[h], NG // 2 * 16 + 16)


def softmax_weights(nc, K, Dr, s):
    CH = P // H
    M = EP // CH
    a, src = s.sb("a", [P, M]), s.sb("src", [P, M])
    gap = s.sb("gap", [P, M + 1])
    best = s.sb("best", [P, M])
    edge = s.sb("edge", [P, 4])
    row = s.sb("row", [1, 8, P])
    carry = s.sb("carry", [P, 2])
    p_row, p_col = s.ps("p_row", [1, 4, P]), s.ps("p_col", [P, 512])
    landed, chain, rows_ready, cols_ready, e_ready, stored = (s.sem(n) for n in ("landed", "chain", "rows", "cols", "e", "stored"))
    count = [0]
    FIRST, LAST, TOP, SAME, WHOLE, OPEN, SHUT, STATE = range(8)

    with nc.Block() as block:
        @block.sync
        def _(sp):
            nc.sync.dma_start(a[:], Dr.logitT.rearrange("h (c m) -> (h c) m", c=CH)).then_inc(landed, 16)
            for h in range(H):
                nc.sync.dma_start(src[h * CH:(h + 1) * CH, :], Dr.srt.rearrange("a (c m) -> (a c) m", c=CH)).then_inc(landed, 16)
            sp.wait_ge(e_ready, 1)
            nc.sync.dma_start(Dr.expT.rearrange("h (c m) -> (h c) m", c=CH), a[:]).then_inc(stored, 16)
            sp.wait_ge(stored, 16)

        @block.vector
        def _(dve):
            def step(ins):
                ins.then_inc(chain, 1)
                count[0] += 1
                dve.wait_ge(chain, count[0])

            step(nc.vector.memset(gap[:], 0.0))
            dve.wait_ge(landed, 16 * (H + 1))
            step(nc.vector.tensor_tensor(out=gap[:, 1:M], in0=src[:, 1:M], in1=src[:, 0:M - 1], op=ALU.not_equal))
            step(nc.vector.tensor_scalar(gap[:], gap[:], -FAR, None, ALU.mult))
            for back in range(2):
                flip = slice(None, None, -1) if back else slice(None)
                gaps = gap[:, 1:M + 1] if back else gap[:, 0:M]
                data = best if back else a
                trial = src if back else best
                if not back:
                    step(nc.vector.tensor_copy(edge[:, FIRST:FIRST + 1], src[:, 0:1]))
                    step(nc.vector.tensor_copy(edge[:, LAST:LAST + 1], src[:, M - 1:M]))
                step(nc.vector.tensor_tensor_scan(out=trial[:, flip], data0=gaps[:, flip], data1=data[:, flip], initial=-FAR, op0=ALU.add, op1=ALU.max))
                step(nc.vector.tensor_copy(edge[:, TOP:TOP + 1], trial[:, 0:1] if back else trial[:, M - 1:M]))
                dve.wait_ge(rows_ready, 3 * back + 3)
                step(nc.vector.tensor_copy(row[:, 0:3, :], p_row[:, 0:3, :]))
                step(nc.vector.memset(row[:, SAME, :], 0.0))
                heads = row[:].rearrange("a k (h c) -> a k h c", c=CH)
                here, there = (slice(0, CH - 1), slice(1, CH)) if back else (slice(1, CH), slice(0, CH - 1))
                step(nc.vector.tensor_tensor(out=heads[:, SAME, :, here], in0=heads[:, LAST if back else FIRST, :, here],
                                             in1=heads[:, FIRST if back else LAST, :, there], op=ALU.is_equal))
                step(nc.vector.tensor_tensor(out=row[:, WHOLE, :], in0=row[:, FIRST, :], in1=row[:, LAST, :], op=ALU.is_equal))
                step(nc.vector.tensor_tensor(out=row[:, OPEN, :], in0=row[:, SAME, :], in1=row[:, WHOLE, :], op=ALU.mult))
                step(nc.vector.tensor_scalar(row[:, OPEN, :], row[:, OPEN, :], FAR, -FAR, ALU.mult, ALU.add))
                step(nc.vector.tensor_scalar(row[:, SHUT, :], row[:, SAME, :], FAR, -FAR, ALU.mult, ALU.add))
                step(nc.vector.tensor_tensor_scan(out=row[:, STATE, flip], data0=row[:, OPEN, flip], data1=row[:, TOP, flip], initial=-FAR, op0=ALU.add, op1=ALU.max))
                step(nc.vector.tensor_tensor(out=heads[:, SHUT, :, here], in0=heads[:, SHUT, :, here], in1=heads[:, STATE, :, there], op=ALU.add))
                dve.wait_ge(cols_ready, back + 1)
                step(nc.vector.tensor_copy(carry[:, back:back + 1], p_col[:, back:back + 1]))
                step(nc.vector.tensor_tensor_scan(out=trial[:, flip], data0=gaps[:, flip], data1=data[:, flip], initial=carry[:, back:back + 1], op0=ALU.add, op1=ALU.max))
            step(nc.vector.tensor_sub(a[:], a[:], src[:]))

        @block.tensor
        def _(pe):
            for back, (borders, carried) in enumerate(BORDERS):
                pe.wait_ge(chain, borders)
                for k in range(3):
                    nc.tensor.transpose(p_row[0:1, k, :], edge[:, k:k + 1], K.ident[:]).then_inc(rows_ready, 1)
                pe.wait_ge(chain, carried)
                nc.tensor.transpose(p_col[:, back:back + 1], row[0:1, SHUT, :], K.ident[0:1, 0:1]).then_inc(cols_ready, 1)

        @block.scalar
        def _(act):
            act.wait_ge(chain, LAST_STEP)
            nc.scalar.activation(a[:], a[:], ACT.Exp).then_inc(e_ready, 1)


BORDERS = [(7, 16), (20, 29)]
LAST_STEP = 32


def weighted_sums(nc, K, Dr, s):
    vv, expT = s.sb("vv", [P, 2, G, D]), s.sb("expT", [H, 2, GE])
    ex, wv = s.sb("ex", [P, 2, G, H]), s.sb("wv", [P, 2, G, D])
    hot = s.sb("hot", [P, 2, G, P])
    p_ex = s.ps("p_ex", [P, 2, 512])
    p_sum, p_den = s.ps("p_sum", [D, 2, 4, P]), s.ps("p_den", [H, 2, 4, P])
    landed = [s.sem("landed0"), s.sem("landed1")]
    t_ready, ex_ready, wv_ready, hot_ready, summed, added, tick, cleared = (
        s.sem(n) for n in ("t", "ex", "wv", "hot", "summed", "added", "tick", "cleared"))
    with nc.Block() as block:
        @block.sync
        def _(sp):
            with nc.sync.Fori(0, NG // 2) as i:
                for h in range(2):
                    g = i * 2 + h
                    sp.wait_ge(wv_ready, g + 1)
                    sp.sem_inc(tick, 1)
                    nc.sync.dma_start(vv[:, h], Dr.by_src2[bass.ds(g * GE, GE), D:2 * D].rearrange("(j p) f -> p j f", p=P)).then_inc(landed[h], 16)
                    nc.sync.dma_start(expT[:, h, :], Dr.expT[:, bass.ds(g * GE, GE)]).then_inc(landed[h], 16)

        @block.scalar
        def _(act):
            with nc.scalar.Fori(0, NG // 2) as i:
                for h in range(2):
                    g = i * 2 + h
                    act.wait_ge(t_ready, g + 1)
                    act.wait_ge(summed, 2 * g + 2)
                    nc.scalar.copy(ex[:, h].rearrange("p j h -> p (j h)"), p_ex[:, h, 0:G * H]).then_inc(ex_ready, 1)

        @block.vector
        def _(dve):
            dve.sem_inc(wv_ready, 2)
            dve.sem_inc(added, 2 * G)
            nc.vector.memset(K.acc[:], 0.0).then_inc(cleared, 1)
            nc.vector.memset(K.den[:], 0.0).then_inc(cleared, 1)
            dve.wait_ge(cleared, 2)

            def weigh(h):
                nc.vector.tensor_tensor(out=wv[:, h].rearrange("p j (h d) -> p (j h) d", d=HD), in0=vv[:, h].rearrange("p j (h d) -> p (j h) d", d=HD),
                                        in1=ex[:, h].rearrange("p j h -> p (j h)").unsqueeze(2).broadcast_to([P, G * H, HD]), op=ALU.mult).then_inc(wv_ready, 1)

            def one_hot(g, h, j):
                ins = nc.vector.tensor_scalar(hot[:, h, j, :], K.lane[:, 0:P], K.srt_in[:, bass.ds(g * G + j, 1)], None, ALU.is_equal)
                if j % 4 == 3:
                    ins.then_inc(hot_ready, 1)

            def group(g, h, last, loads):
                at = load_values(nc, DVE, K.srt_i[0:1, bass.ds(g * G, G)], N)
                if not last:
                    dve.wait_ge(summed, 2 * g + 4)
                    dve.wait_ge(landed[1 - h], loads * 32)
                    dve.wait_ge(ex_ready, g + 2)
                    dve.sem_inc(tick, 1)
                    weigh(1 - h)
                for j in range(G):
                    if not last:
                        one_hot(g + 1, 1 - h, j)
                    if j % 4 == 0:
                        dve.wait_ge(summed, 2 * g + j // 4 + 5)
                    dve.wait_ge(added, 2 * ((g + 1) * G + j))
                    window, under = K.acc[:, bass.ds(at[j], P)], K.den[:, bass.ds(at[j], P)]
                    nc.vector.tensor_tensor(out=window, in0=window, in1=p_sum[:, j // 4, j % 4, :], op=ALU.add).then_inc(added, 1)
                    nc.vector.tensor_tensor(out=under, in0=under, in1=p_den[:, j // 4, j % 4, :], op=ALU.add).then_inc(added, 1)

            dve.wait_ge(landed[0], 32)
            dve.wait_ge(ex_ready, 1)
            weigh(0)
            for j in range(G):
                one_hot(0, 0, j)
            with nc.vector.Fori(0, NG // 2 - 1) as i:
                for h in range(2):
                    group(i * 2 + h, h, False, i + 1 + h)
            group(NG - 2, 0, False, NG // 2)
            group(NG - 1, 1, True, 0)

        @block.tensor
        def _(pe):
            pe.sem_inc(summed, 4)

            def turn(h, loads):
                pe.wait_ge(landed[h], loads * 32)
                pe.sem_inc(tick, 1)
                for j in range(G):
                    tr = nc.tensor.transpose(p_ex[:, h, j * H:(j + 1) * H], expT[:, h, j * P:(j + 1) * P], K.ident[0:H, 0:H])
                tr.then_inc(t_ready, 1)

            def products(g, h):
                pe.wait_ge(wv_ready, g + 3)
                for c in range(2):
                    pe.wait_ge(hot_ready, 2 * g + c + 1)
                    pe.wait_ge(added, 2 * (g * G + 4 * c + 4))
                    for j in range(4 * c, 4 * c + 4):
                        nc.tensor.matmul(p_sum[:, c, j % 4, :], wv[:, h, j, :], hot[:, h, j, :], start=True, stop=True)
                        mm = nc.tensor.matmul(p_den[:, c, j % 4, :], ex[:, h, j, :], hot[:, h, j, :], start=True, stop=True)
                    mm.then_inc(summed, 1)

            turn(0, 1)
            with nc.tensor.Fori(0, NG // 2 - 1) as i:
                for h in range(2):
                    turn(1 - h, i + 1 + h)
                    products(i * 2 + h, h)
            turn(1, NG // 2)
            products(NG - 2, 0)
            products(NG - 1, 1)


def nodes_after_attention(nc, K, s):
    C = R * P
    hs, hT = s.sb("h", [P, R, D]), s.sb("hT", [P, C])
    rden, guard = s.sb("rden", [H, C]), s.sb("guard", [H, C])
    mean, diff = s.sb("mean", [D, C]), s.sb("diff", [D, C])
    p_t, p_v, p_d, p_o = s.ps("p_t", [P, 1024]), s.ps("p_v", [D, 2, 512]), s.ps("p_d", [D, 2, 512]), s.ps("p_o", [P, 1024])
    h_ready, turned, copied, v_ready, d_ready, diff_ready, o_ready, added, tick, g_ready, r_ready, m_ready = (
        s.sem(n) for n in ("h", "t", "copied", "v", "d", "diff", "o", "added", "tick", "g", "r", "m"))
    with nc.Block() as block:
        @block.scalar
        def _(act):
            with nc.scalar.Fori(0, NI) as i:
                act.wait_ge(copied, i + 1)
                act.wait_ge(added, i + 1)
                normed(nc, K, act, i, hs, tick).then_inc(h_ready, 1)

        @block.tensor
        def _(pe):
            pe.sem_inc(v_ready, 1)
            pe.sem_inc(d_ready, 1)
            pe.sem_inc(o_ready, 1)
            with nc.tensor.Fori(0, NI) as i:
                pe.wait_ge(h_ready, i + 1)
                for r in range(R):
                    tr = nc.tensor.transpose(p_t[:, r * P:(r + 1) * P], hs[:, r, :], K.ident[:])
                tr.then_inc(turned, 1)
                pe.wait_ge(copied, i + 2)
                pe.wait_ge(diff_ready, i + 1)
                for c in range(2):
                    mm = nc.tensor.matmul(p_v[:, c, 0:C // 2], K.wqkv[:, 2 * D:3 * D], hT[:, c * (C // 2):(c + 1) * (C // 2)], start=True, stop=True)
                mm.then_inc(v_ready, 1)
                pe.wait_ge(r_ready, i + 1)
                for c in range(2):
                    mm = nc.tensor.matmul(p_d[:, c, 0:C // 2], K.rep[:], rden[:, c * (C // 2):(c + 1) * (C // 2)], start=True, stop=True)
                mm.then_inc(d_ready, 1)
                pe.wait_ge(diff_ready, i + 2)
                pe.wait_ge(added, i + 1)
                for r in range(R):
                    mm = nc.tensor.matmul(p_o[:, r * D:(r + 1) * D], diff[:, r * P:(r + 1) * P], K.w_out[:], start=True, stop=True)
                mm.then_inc(o_ready, 1)

        @block.vector
        def _(dve):
            dve.sem_inc(copied, 1)
            dve.sem_inc(diff_ready, 1)
            dve.sem_inc(added, 1)
            halves = "p (c n) -> p c n"
            with nc.vector.Fori(0, NI) as i:
                nc.vector.tensor_scalar(guard[:], K.den[:, in_step(i)], 1e-30, None, ALU.max).then_inc(g_ready, 1)
                dve.wait_ge(g_ready, i + 1)
                dve.wait_ge(d_ready, i + 1)
                nc.vector.reciprocal(rden[:], guard[:]).then_inc(r_ready, 1)
                dve.wait_ge(turned, i + 1)
                dve.wait_ge(v_ready, i + 1)
                nc.vector.tensor_copy(hT[:], p_t[:, 0:C]).then_inc(copied, 1)
                dve.wait_ge(d_ready, i + 2)
                nc.vector.tensor_tensor(out=mean[:].rearrange(halves, c=2), in0=K.acc[:, in_step(i)].rearrange(halves, c=2), in1=p_d[:, :, 0:C // 2], op=ALU.mult).then_inc(m_ready, 1)
                dve.wait_ge(m_ready, i + 1)
                dve.wait_ge(v_ready, i + 2)
                dve.wait_ge(o_ready, i + 1)
                nc.vector.tensor_tensor(out=diff[:].rearrange(halves, c=2), in0=p_v[:, :, 0:C // 2], in1=mean[:].rearrange(halves, c=2), op=ALU.subtract).then_inc(diff_ready, 1)
                dve.wait_ge(o_ready, i + 2)
                x = K.x[:, bass.ds(i * R, R), :]
                nc.vector.tensor_tensor(out=x, in0=x, in1=p_o[:, 0:C].rearrange("p (r d) -> p r d", d=D), op=ALU.add).then_inc(added, 1)


def nodes_before_gine(nc, K, Dr, s):
    hs, tab = s.sb("h", [P, R, D]), s.sb("tab", [P, R, D])
    we1T, bc, bias, own = s.sb("we1T", [P, 2, 16]), s.sb("bc", [1, D]), s.sb("bias", [P, D]), s.sb("own", [P, 1])
    p_t, p_w, p_c = s.ps("p_t", [P, 1024]), s.ps("p_w", [P, 512]), s.ps("p_c", [P, 4, P])
    h_ready, tab_ready, turned, kept, stored, tick, w_ready, c_ready = (s.sem(n) for n in ("h", "tab", "t", "kept", "stored", "tick", "w", "c"))
    with nc.Block() as block:
        @block.scalar
        def _(act):
            with nc.scalar.Fori(0, NI) as i:
                act.wait_ge(tab_ready, i + 1)
                act.wait_ge(turned, i + 1)
                normed(nc, K, act, i, hs, tick).then_inc(h_ready, 1)

        @block.tensor
        def _(pe):
            pe.sem_inc(turned, 1)
            for m in range(2):
                tr = nc.tensor.transpose(p_w[:, m * 16:(m + 1) * 16], K.we1[:, m * P:(m + 1) * P], K.ident[0:16, 0:16])
            tr.then_inc(w_ready, 1)
            pe.wait_ge(c_ready, 1)
            for m in range(2):
                nc.tensor.matmul(p_c[0:16, 0, :], we1T[:, m, :], K.we2[:, m, :], start=(m == 0), stop=(m == 1))
            for m in range(2):
                mm = nc.tensor.matmul(p_c[0:1, 1, :], K.be1[:, m:m + 1], K.we2[:, m, :], start=(m == 0), stop=(m == 1))
            mm.then_inc(w_ready, 1)
            pe.wait_ge(c_ready, 3)
            nc.tensor.matmul(p_c[:, 2, :], K.ones[0:1, :], bc[:], start=True, stop=True).then_inc(w_ready, 1)
            with nc.tensor.Fori(0, NI) as i:
                pe.wait_ge(h_ready, i + 1)
                pe.wait_ge(kept, i + 1)
                for r in range(R):
                    tr = nc.tensor.transpose(p_t[:, r * P:(r + 1) * P], hs[:, r, :], K.ident[:])
                tr.then_inc(turned, 1)

        @block.vector
        def _(dve):
            dve.sem_inc(tab_ready, 1)
            dve.sem_inc(kept, 1)
            nc.vector.memset(K.acc[:, NR:NW], 0.0)
            dve.wait_ge(w_ready, 1)
            nc.vector.tensor_copy(we1T[:].rearrange("p m k -> p (m k)"), p_w[:, 0:32]).then_inc(c_ready, 1)
            dve.wait_ge(w_ready, 2)
            nc.vector.tensor_copy(K.wc[:], p_c[0:16, 0, :]).then_inc(c_ready, 1)
            nc.vector.tensor_add(bc[:], K.be2[:], p_c[0:1, 1, :]).then_inc(c_ready, 1)
            dve.wait_ge(w_ready, 3)
            nc.vector.tensor_copy(bias[:], p_c[:, 2, :]).then_inc(c_ready, 1)
            nc.vector.tensor_scalar(own[:], K.eps[:], 1.0, None, ALU.add).then_inc(c_ready, 1)
            dve.wait_ge(c_ready, 5)
            with nc.vector.Fori(0, NI) as i:
                dve.wait_ge(h_ready, i + 1)
                dve.wait_ge(stored, i * 16 + 16)
                nc.vector.tensor_tensor(out=tab[:], in0=hs[:], in1=bias[:].unsqueeze(1).broadcast_to([P, R, D]), op=ALU.add).then_inc(tab_ready, 1)
                dve.wait_ge(turned, i + 2)
                nc.vector.tensor_scalar(K.acc[:, in_step(i)], p_t[:, 0:R * P], own[:, 0:1], None, ALU.mult).then_inc(kept, 1)

        @block.sync
        def _(sp):
            sp.sem_inc(stored, 16)
            with nc.sync.Fori(0, NI) as i:
                sp.wait_ge(tab_ready, i + 2)
                sp.sem_inc(tick, 1)
                nc.sync.dma_start(Dr.table.rearrange("(b p) d -> p b d", p=P)[:, bass.ds(i * R, R), :], tab[:]).then_inc(stored, 16)
            sp.wait_ge(stored, 16 * NI + 16)


def nodes_after_gine(nc, K, out, s):
    C = R * P
    BM, GA, BE, ME, VA = range(5)
    sc1, sh1 = s.sb("sc1", [P, 2]), s.sb("sh1", [P, 2])
    sc2, sh2 = s.sb("sc2", [P, D]), s.sb("sh2", [P, D])
    act1 = s.sb("act1", [P, 2, C])
    t, y = s.sb("t", [P, R, D]), s.sb("y", [P, R, D])
    p_u, p_o = s.ps("p_u", [P, 2, 1024]), s.ps("p_o", [P, 1024])
    chain, root, folded, u_ready, r_ready, o_ready, t_ready, y_ready, stored, tick, s_ready = (
        s.sem(n) for n in ("chain", "root", "folded", "u", "r", "o", "t", "y", "stored", "tick", "s"))
    z = s.sb("z", [P, R, D])
    with nc.Block() as block:
        @block.vector
        def _(dve):
            n = [0]

            def step(ins):
                ins.then_inc(chain, 1)
                n[0] += 1
                dve.wait_ge(chain, n[0])

            step(nc.vector.tensor_scalar(sc1[:], K.bn1[:, :, VA], BN_EPS, None, ALU.add))
            step(nc.vector.tensor_scalar(sc2[:], K.bn2[:, VA, :], BN_EPS, None, ALU.add))
            dve.wait_ge(root, 2)
            step(nc.vector.reciprocal(sc1[:], sc1[:]))
            step(nc.vector.reciprocal(sc2[:], sc2[:]))
            step(nc.vector.tensor_mul(sc1[:], sc1[:], K.bn1[:, :, GA]))
            step(nc.vector.tensor_mul(sc2[:], sc2[:], K.bn2[:, GA, :]))
            step(nc.vector.tensor_sub(sh1[:], K.bn1[:, :, BM], K.bn1[:, :, ME]))
            step(nc.vector.tensor_sub(sh2[:], K.bn2[:, BM, :], K.bn2[:, ME, :]))
            step(nc.vector.tensor_mul(sh1[:], sh1[:], sc1[:]))
            step(nc.vector.tensor_mul(sh2[:], sh2[:], sc2[:]))
            step(nc.vector.tensor_add(sh1[:], sh1[:], K.bn1[:, :, BE]))
            step(nc.vector.tensor_add(sh2[:], sh2[:], K.bn2[:, BE, :]))
            dve.sem_inc(folded, 1)
            dve.sem_inc(t_ready, 1)
            with nc.vector.Fori(0, NI) as i:
                dve.wait_ge(o_ready, i + 2)
                nc.vector.tensor_tensor(out=t[:], in0=p_o[:, 0:C].rearrange("p (r d) -> p r d", d=D), in1=sc2[:].unsqueeze(1).broadcast_to([P, R, D]), op=ALU.mult).then_inc(t_ready, 1)
                dve.wait_ge(t_ready, i + 2)
                nc.vector.tensor_tensor(out=z[:], in0=t[:], in1=sh2[:].unsqueeze(1).broadcast_to([P, R, D]), op=ALU.add).then_inc(s_ready, 1)
                dve.wait_ge(s_ready, i + 1)
                dve.wait_ge(stored, i * 16 + 16)
                nc.vector.tensor_tensor(out=y[:], in0=z[:], in1=K.x[:, bass.ds(i * R, R), :], op=ALU.add).then_inc(y_ready, 1)
                dve.wait_ge(y_ready, i + 1)

        @block.scalar
        def _(act):
            act.wait_ge(chain, 2)
            nc.scalar.activation(sc1[:], sc1[:], ACT.Sqrt).then_inc(root, 1)
            nc.scalar.activation(sc2[:], sc2[:], ACT.Sqrt).then_inc(root, 1)
            act.wait_ge(folded, 1)
            act.sem_inc(r_ready, 1)
            with nc.scalar.Fori(0, NI) as i:
                act.wait_ge(u_ready, i + 1)
                act.wait_ge(o_ready, i + 1)
                for m in range(2):
                    ins = nc.scalar.activation(act1[:, m, :], p_u[:, m, 0:C], ACT.Relu, bias=sh1[:, m:m + 1], scale=sc1[:, m:m + 1])
                ins.then_inc(r_ready, 1)

        @block.tensor
        def _(pe):
            pe.sem_inc(o_ready, 1)
            with nc.tensor.Fori(0, NI) as i:
                pe.wait_ge(r_ready, i + 1)
                pe.sem_inc(tick, 1)
                for m in range(2):
                    for r in range(R):
                        mm = nc.tensor.matmul(p_u[:, m, r * P:(r + 1) * P], K.wm1[:, m * P:(m + 1) * P], K.acc[:, bass.ds((i * R + r) * P, P)], start=True, stop=True)
                mm.then_inc(u_ready, 1)
                pe.wait_ge(r_ready, i + 2)
                pe.wait_ge(t_ready, i + 1)
                for r in range(R):
                    for m in range(2):
                        mm = nc.tensor.matmul(p_o[:, r * D:(r + 1) * D], act1[:, m, r * P:(r + 1) * P], K.wm2[:, m, :], start=(m == 0), stop=(m == 1))
                mm.then_inc(o_ready, 1)

        @block.sync
        def _(sp):
            sp.sem_inc(stored, 16)
            with nc.sync.Fori(0, NI) as i:
                sp.wait_ge(y_ready, i + 1)
                sp.sem_inc(tick, 1)
                nc.sync.dma_start(out.rearrange("(b p) d -> p b d", p=P)[:, bass.ds(i * R, R), :], y[:]).then_inc(stored, 16)
            sp.wait_ge(stored, 16 * NI + 16)


class Names:
    pass


def build(nc, A, out):
    K, Dr = Names(), Names()
    Dr.by_src0 = nc.dram_tensor("by_src0", (EP, XC), F32, kind=SCRATCH).ap()
    Dr.by_src2 = nc.dram_tensor("by_src2", (EP, 2 * D), F32, kind=SCRATCH).ap()
    Dr.srt = nc.dram_tensor("srt", (1, EP), F32, kind=SCRATCH).ap()
    Dr.logitT = nc.dram_tensor("logitT", (H, EP), F32, kind=SCRATCH).ap()
    Dr.expT = nc.dram_tensor("expT", (H, EP), F32, kind=SCRATCH).ap()
    Dr.table = nc.dram_tensor("table", (NR, D), F32, kind=SCRATCH).ap()
    with Space(nc, "k") as k:
        K.x = k.sb("x", [P, NB, D])
        K.src_f, K.ew = k.sb("src_f", [P, T]), k.sb("ew", [P, T])
        K.dst_f, K.dst_i = k.sb("dst_f", [P, T]), k.sb("dst_i", [P, T], I32)
        K.srt_f, K.srt_i, K.dst_blk = k.sb("srt_f", [P, T]), k.sb("srt_i", [1, T], I32), k.sb("dst_blk", [1, T], I32)
        K.srt_blk, K.pos, K.mix = k.sb("srt_blk", [1, T], I32), k.sb("pos", [P, T], I32), k.sb("mix", [D, H])
        K.lane, K.node_col = k.sb("lane", [P, P]), k.sb("node_col", [P, NB + 1])
        K.ident, K.ones, K.rep = k.sb("ident", [P, P]), k.sb("ones", [P, P]), k.sb("rep", [H, D])
        K.dinv, K.root = k.sb("dinv", [P, NB]), k.sb("root", [P, NB])
        K.rstd, K.sd, K.shift = k.sb("rstd", [P, NB]), k.sb("sd", [P, NB]), k.sb("shift", [P, NB])
        K.w_in, K.b_in = k.sb("w_in", [D, F0]), k.sb("b_in", [1, F0])
        K.w_f1, K.b_f1 = k.sb("w_f1", [32, 2 * F0]), k.sb("b_f1", [2 * F0, 1])
        K.w_f2, K.b_f2, K.b_f2g = k.sb("w_f2", [2 * F0, F0]), k.sb("b_f2", [1, F0]), k.sb("b_f2g", [1, G * F0])
        K.w_o1, K.b_o1, K.w_o2, K.b_o2 = k.sb("w_o1", [F0, D]), k.sb("b_o1", [D, 1]), k.sb("w_o2", [D, D]), k.sb("b_o2", [1, D])
        K.w1, K.b1 = k.sb("w1", [D, D]), k.sb("b1", [P, D])
        K.wqkv, K.wekv = k.sb("wqkv", [D, 3 * D]), k.sb("wekv", [D, 2 * D])
        K.w_exp, K.w_out = k.sb("w_exp", [H, H]), k.sb("w_out", [D, D])
        K.we1, K.be1, K.we2, K.be2 = k.sb("we1", [16, 2 * D]), k.sb("be1", [P, 2]), k.sb("we2", [P, 2, D]), k.sb("be2", [1, D])
        K.eps, K.wm1, K.wm2 = k.sb("eps", [P, 1]), k.sb("wm1", [D, 2 * D]), k.sb("wm2", [P, 2, D])
        K.bn1, K.bn2 = k.sb("bn1", [P, 2, 5]), k.sb("bn2", [P, 5, D])
        with Space(nc, "e") as e:
            K.src_i, K.key_i, K.low_i = e.sb("src_i", [P, T], I32), e.sb("key_i", [P, T], I32), e.sb("low_i", [P, T], I32)
            K.src_hi, K.src_lo, K.dst_hi, K.dst_lo = e.sb("src_hi", [P, T]), e.sb("src_lo", [P, T]), e.sb("dst_hi", [P, T]), e.sb("dst_lo", [P, T])
            K.below, K.above, K.place0 = e.sb("below", [P, P]), e.sb("above", [P, P]), e.sb("place0", [NB, P])
            with Space(nc, "setup") as s:
                setup(nc, A, K, s)
            with Space(nc, "hist") as s:
                histograms(nc, K, s)
            with Space(nc, "norm0") as s:
                layer_norm_stats(nc, K, s)
            K.h_in = e.sb("h_in", [P, NB + 1, F0])
            with Space(nc, "nodes0") as s:
                nodes_before_filter(nc, K, s)
            with Space(nc, "edges0") as s:
                filter_edges(nc, K, Dr, A, s)
        with Space(nc, "w") as w:
            K.srt_in, K.dst_in = w.sb("srt_in", [P, T]), w.sb("dst_in", [P, T])
            with Space(nc, "a1") as a:
                K.acc = a.sb("acc", [P, NW])
                with Space(nc, "sum0") as s:
                    K.node_row = s.sb("node_row", [P, NW])
                    sum_by_source(nc, K, Dr, s)
                with Space(nc, "row") as s:
                    sorted_row(nc, K, Dr, s)
                with Space(nc, "out0") as s:
                    nodes_after_filter(nc, K, s)
                with Space(nc, "norm1") as s:
                    layer_norm_stats(nc, K, s)
                with Space(nc, "nodes1") as s:
                    nodes_before_gcn(nc, K, Dr, s)
                with Space(nc, "sum1") as s:
                    sum_by_target(nc, K, Dr, A, s, gine=False)
                with Space(nc, "out1") as s:
                    nodes_after_gcn(nc, K, s)
            with Space(nc, "norm2") as s:
                layer_norm_stats(nc, K, s)
            with Space(nc, "q") as q:
                K.q = q.sb("q", [P, NB + 1, D])
                with Space(nc, "kv") as kv:
                    K.kv = kv.sb("kv", [P, NB + 1, 2 * D])
                    with Space(nc, "nodes2") as s:
                        nodes_before_attention(nc, K, s)
                    with Space(nc, "edges2") as s:
                        key_value_edges(nc, K, Dr, A, s)
                with Space(nc, "logits") as s:
                    attention_logits(nc, K, Dr, s)
            with Space(nc, "softmax") as s:
                softmax_weights(nc, K, Dr, s)
            with Space(nc, "a2") as a:
                K.acc = a.sb("acc", [P, NW])
                K.wc = a.sb("wc", [16, D])
                with Space(nc, "den") as d:
                    K.den = d.sb("den", [H, NW])
                    with Space(nc, "sum2") as s:
                        weighted_sums(nc, K, Dr, s)
                    with Space(nc, "out2") as s:
                        nodes_after_attention(nc, K, s)
                with Space(nc, "norm3") as s:
                    layer_norm_stats(nc, K, s)
                with Space(nc, "nodes3") as s:
                    nodes_before_gine(nc, K, Dr, s)
                with Space(nc, "sum3") as s:
                    sum_by_target(nc, K, Dr, A, s, gine=True)
                with Space(nc, "out3") as s:
                    nodes_after_gine(nc, K, out, s)



SCRATCH = "Internal"


def kernel(**inputs):
    import numpy as np
    import concourse.bacc as bacc
    from concourse.bass_utils import run_bass_kernel_spmd as run

    nc = bacc.Bacc("TRN2", target_bir_lowering=False, num_devices=1)
    a = {n: np.ascontiguousarray(v) for n, v in inputs.items()}

    def edges(v, fill):
        return np.concatenate([v, np.full((EP - E,) + v.shape[1:], fill, v.dtype)])

    def in_tiles(v):
        return np.ascontiguousarray(v.reshape(T, P).T)

    src, dst, ew = edges(a.pop("src"), N), edges(a.pop("dst"), N), edges(a.pop("edge_weight"), 0)
    a["x"] = np.concatenate([a["x"], np.zeros((NR - N, D), a["x"].dtype)])
    a["src"], a["dst"], a["ew"] = in_tiles(src), in_tiles(dst), in_tiles(ew)
    a["src_row"], a["dst_row"] = src[None, :], dst[None, :]
    for n in (16, 32, 128):
        a[f"attr{n}T"] = np.ascontiguousarray(edges(a.pop(f"edge_attr_{n}"), 0).T)
    aps = {n: nc.dram_tensor(f"in_{n}", v.shape, mybir.dt.from_np(v.dtype), kind="ExternalInput").ap() for n, v in a.items()}
    out = nc.dram_tensor("out", (NR, D), F32, kind="ExternalOutput").ap()
    build(nc, aps, out)
    r = run(nc, [{f"in_{n}": v for n, v in a.items()}], core_ids=[0])
    return r.results[0]["out"][:N]
```

```python
from contextlib import ExitStack

import concourse.bass as bass
from concourse import mybir

F32 = mybir.dt.float32
I32 = mybir.dt.int32
BF16 = mybir.dt.bfloat16
ALU = mybir.AluOpType
ACT = mybir.ActivationFunctionType
AX_X = mybir.AxisListType.X
DVE = mybir.EngineType.DVE
PE = mybir.EngineType.PE

P = 128
N = 6250
E = 106250
D = 128
NB = -(-N // P)
NR = NB * P
NW = NR + P
G = 8
GE = G * P
T = -(-E // (2 * GE)) * 2 * G
NG = T // G
EP = T * P
R = 7
NI = NB // R
assert NI * R == NB and N < NR
F0 = 64
XC = F0 + 1
H = 8
HD = D // H
LOG2 = 0.6931471805599453
LN_EPS = 1e-5
BN_EPS = 1e-3
FAR = 1.0e37
IN_RANGE = "node numbers are 0..N by the kind of the inputs, and tables are padded past N"


def load_values(nc, engine, ap, top):
    return nc.values_load_multi_w_load_instructions(
        ap, engines=(engine,), min_val=0, max_val=top, skip_runtime_bounds_check_because=IN_RANGE)[1]


class Space:

    def __init__(self, nc, tag):
        self.nc, self.tag, self.ctx, self.sems = nc, tag, ExitStack(), []

    def __enter__(self):
        return self

    def __exit__(self, *a):
        for sem in self.sems:
            self.nc.sync.sem_clear(sem)
        return self.ctx.__exit__(*a)

    def sb(self, name, shape, dt=F32):
        return self.ctx.enter_context(self.nc.sbuf_tensor(f"{self.tag}_{name}", shape, dt))

    def ps(self, name, shape, dt=F32):
        return self.ctx.enter_context(self.nc.psum_tensor(f"{self.tag}_{name}", shape, dt))

    def sem(self, name):
        self.sems.append(self.ctx.enter_context(self.nc.semaphore(f"{self.tag}_{name}")))
        return self.sems[-1]


def setup(nc, A, K, s):
    loaded, made, tidy, blank, lanes = s.sem("loaded"), s.sem("made"), s.sem("tidy"), s.sem("blank"), s.sem("lanes")
    pairs = [
        (K.x[:], A["x"].rearrange("(b p) d -> p b d", p=P)),
        (K.src_i[:], A["src"]), (K.dst_i[:], A["dst"]), (K.ew[:], A["ew"]),
        (K.w_in[:], A["L0_gnn_w_in"]), (K.b_in[:], A["L0_gnn_b_in"].unsqueeze(0)),
        (K.w_f1[0:32, 0:F0], A["L0_gnn_w_f1"]), (K.w_f1[32:64, F0:2 * F0], A["L0_gnn_w_f1"]),
        (K.b_f1[0:F0, :], A["L0_gnn_b_f1"].unsqueeze(1)), (K.b_f1[F0:2 * F0, :], A["L0_gnn_b_f1"].unsqueeze(1)),
        (K.w_f2[0:F0, :], A["L0_gnn_w_f2"]), (K.w_f2[F0:2 * F0, :], A["L0_gnn_w_f2"]),
        (K.b_f2[:], A["L0_gnn_b_f2"].unsqueeze(0)),
        (K.w_o1[:], A["L0_gnn_w_o1"]), (K.b_o1[:], A["L0_gnn_b_o1"].unsqueeze(1)),
        (K.w_o2[:], A["L0_gnn_w_o2"]), (K.b_o2[:], A["L0_gnn_b_o2"].unsqueeze(0)),
        (K.w1[:], A["L1_gnn_W"]), (K.b1[:], A["L1_gnn_b"].unsqueeze(0).broadcast_to([P, D])),
        (K.wqkv[:, 0:D], A["L2_gnn_Wq"]), (K.wqkv[:, D:2 * D], A["L2_gnn_Wk"]), (K.wqkv[:, 2 * D:], A["L2_gnn_Wv"]),
        (K.wekv[:, 0:D], A["L2_gnn_Wek"]), (K.wekv[:, D:], A["L2_gnn_Wev"]),
        (K.w_exp[:], A["L2_gnn_W_exp"]), (K.w_out[:], A["L2_gnn_W_out"]),
        (K.we1[:], A["L3_gnn_We1"]), (K.be1[:], A["L3_gnn_be1"].rearrange("(m p) -> p m", p=P)),
        (K.we2[:], A["L3_gnn_We2"].rearrange("(m p) d -> p m d", p=P)),
        (K.be2[:], A["L3_gnn_be2"].unsqueeze(0)),
        (K.eps[:], A["L3_gnn_eps"].unsqueeze(0).broadcast_to([P, 1])),
        (K.wm1[:], A["L3_gnn_Wm1"]), (K.wm2[:], A["L3_gnn_Wm2"].rearrange("(m p) d -> p m d", p=P)),
    ]
    pairs += [(K.bn1[:, :, k], A[f"L3_gnn_{n}"].rearrange("(m p) -> p m", p=P)) for k, n in enumerate(("bm1", "g1", "b1", "m1", "v1"))]
    pairs += [(K.bn2[:, k, :], A[f"L3_gnn_{n}"].unsqueeze(0).broadcast_to([P, D])) for k, n in enumerate(("bm2", "g2", "b2", "m2", "v2"))]
    with nc.Block() as block:
        @block.sync
        def _(sp):
            sp.wait_ge(blank, 1)
            for to, of in pairs:
                with nc.allow_non_contiguous_dma("vectors of weights, once"):
                    sp.dma_start(to, of).then_inc(loaded, 16)

        @block.gpsimd
        def _(pool):
            nc.gpsimd.iota(K.lane[:], [[1, P]], base=0, channel_multiplier=0, allow_small_or_imprecise_dtypes=True).then_inc(lanes, 1)
            nc.gpsimd.iota(K.node_col[:], [[P, NB + 1]], base=0, channel_multiplier=1, allow_small_or_imprecise_dtypes=True)
            nc.gpsimd.memset(K.ident[:], 0.0).then_inc(made, 1)
            nc.gpsimd.memset(K.below[:], 1.0).then_inc(made, 1)
            nc.gpsimd.memset(K.above[:], 1.0).then_inc(made, 1)
            nc.gpsimd.memset(K.rep[:], 0.0).then_inc(made, 1)
            nc.gpsimd.memset(K.ones[:], 1.0)
            pool.wait_ge(made, 4)
            nc.gpsimd.affine_select(out=K.ident[:], in_=K.ident[:], compare_op=ALU.not_equal, fill=1.0, base=0,
                                    pattern=[[-1, P]], channel_multiplier=1).then_inc(made, 1)
            nc.gpsimd.affine_select(out=K.below[:], in_=K.below[:], compare_op=ALU.is_gt, fill=0.0, base=0,
                                    pattern=[[-1, P]], channel_multiplier=1).then_inc(made, 1)
            nc.gpsimd.affine_select(out=K.above[:], in_=K.above[:], compare_op=ALU.is_gt, fill=0.0, base=0,
                                    pattern=[[1, P]], channel_multiplier=-1).then_inc(made, 1)
            nc.gpsimd.affine_select(out=K.rep[:].rearrange("h (g d) -> h g d", g=H), in_=K.rep[:].rearrange("h (g d) -> h g d", g=H),
                                    compare_op=ALU.not_equal, fill=1.0, base=0,
                                    pattern=[[-1, H], [0, HD]], channel_multiplier=1).then_inc(made, 1)
            pool.wait_ge(made, 8)

        @block.vector
        def _(dve):
            nc.vector.memset(K.w_f1[:], 0.0).then_inc(blank, 1)
            dve.wait_ge(loaded, 16 * len(pairs))
            nc.vector.tensor_copy(K.src_f[:], K.src_i[:])
            nc.vector.tensor_copy(K.dst_f[:], K.dst_i[:])
            nc.vector.tensor_single_scalar(K.key_i[:], K.src_i[:], 7, ALU.logical_shift_right).then_inc(tidy, 1)
            nc.vector.tensor_single_scalar(K.low_i[:], K.src_i[:], P - 1, ALU.bitwise_and).then_inc(tidy, 1)
            dve.wait_ge(tidy, 2)
            nc.vector.tensor_copy(K.src_hi16[:], K.key_i[:])
            nc.vector.tensor_copy(K.src_lo16[:], K.low_i[:])
            nc.vector.tensor_copy(K.src_lo[:], K.low_i[:]).then_inc(tidy, 2)
            dve.wait_ge(lanes, 1)
            nc.vector.tensor_copy(K.lane16[:], K.lane[:])
            dve.wait_ge(tidy, 4)
            nc.vector.tensor_single_scalar(K.key_i[:], K.dst_i[:], 7, ALU.logical_shift_right).then_inc(tidy, 1)
            nc.vector.tensor_single_scalar(K.low_i[:], K.dst_i[:], P - 1, ALU.bitwise_and).then_inc(tidy, 1)
            dve.wait_ge(tidy, 6)
            nc.vector.tensor_copy(K.dst_hi[:], K.key_i[:])
            nc.vector.tensor_copy(K.dst_lo[:], K.low_i[:])
            nc.vector.tensor_copy(K.dst_blk[0:1, :], K.key_i[0:1, :])


def histograms(nc, K, s):
    oh_hi = s.sb("oh_hi", [P, 2, G, NB], BF16)
    oh_lo = s.sb("oh_lo", [P, 2, G, P], BF16)
    d_hi = s.sb("d_hi", [P, 2, G, NB])
    d_hiw = s.sb("d_hiw", [P, 2, G, NB])
    d_lo = s.sb("d_lo", [P, 2, G, P])
    zero = s.sb("zero", [P, P])
    count = s.sb("count", [NB, P])
    upto = s.sb("upto", [NB, P])
    deg_row = s.sb("deg", [NB, P])
    pos = s.sb("positive", [P, NB])
    p_dt = s.ps("p_dt", [P, 512])
    p_count, p_deg, p_off = s.ps("p_count", [P, 512]), s.ps("p_deg", [P, 512]), s.ps("p_off", [P, 512])
    src_hot, dst_hot, part, weighted, free = s.sem("src_hot"), s.sem("dst_hot"), s.sem("part"), s.sem("weighted"), s.sem("free")
    summed, chain, off_done, root, zeroed = (s.sem(n) for n in ("summed", "chain", "off", "root", "zeroed"))

    def step(dve, ins, n):
        ins.then_inc(chain, 1)
        dve.wait_ge(chain, n)

    with nc.Block() as block:
        @block.vector
        def _(dve):
            nc.vector.memset(zero[:], 0.0).then_inc(zeroed, 1)
            with nc.vector.Fori(0, NG // 2) as i:
                for h in range(2):
                    cols = bass.ds(i * 2 * G + h * G, G)
                    dve.wait_ge(free, i * 2 + h + 1)
                    nc.vector.tensor_tensor(out=oh_hi[:, h], in0=K.lane16[:, 0:NB].unsqueeze(1).broadcast_to([P, G, NB]),
                                            in1=K.src_hi16[:, cols].unsqueeze(2).broadcast_to([P, G, NB]), op=ALU.is_equal)
                    nc.vector.tensor_tensor(out=oh_lo[:, h], in0=K.lane16[:].unsqueeze(1).broadcast_to([P, G, P]),
                                            in1=K.src_lo16[:, cols].unsqueeze(2).broadcast_to([P, G, P]), op=ALU.is_equal).then_inc(src_hot, 1)
                    nc.vector.tensor_tensor(out=d_hi[:, h], in0=K.lane[:, 0:NB].unsqueeze(1).broadcast_to([P, G, NB]),
                                            in1=K.dst_hi[:, cols].unsqueeze(2).broadcast_to([P, G, NB]), op=ALU.is_equal).then_inc(part, 1)
                    nc.vector.tensor_tensor(out=d_lo[:, h], in0=K.lane[:, 0:P].unsqueeze(1).broadcast_to([P, G, P]),
                                            in1=K.dst_lo[:, cols].unsqueeze(2).broadcast_to([P, G, P]), op=ALU.is_equal).then_inc(dst_hot, 1)
            dve.wait_ge(summed, 1)
            step(dve, nc.vector.tensor_copy(count[:], p_count[0:NB, 0:P]), 1)
            step(dve, nc.vector.tensor_scalar(deg_row[:], p_deg[0:NB, 0:P], 1.0, None, ALU.add), 2)
            step(dve, nc.vector.tensor_tensor_scan(out=upto[:], data0=count[:], data1=zero[0:NB, :], initial=0.0, op0=ALU.add, op1=ALU.add), 3)
            dve.wait_ge(off_done, 1)
            step(dve, nc.vector.tensor_scalar(pos[:], p_dt[:, 0:NB], 0.0, None, ALU.is_gt), 4)
            step(dve, nc.vector.tensor_scalar(K.root[:], p_dt[:, 0:NB], 1e-30, None, ALU.max), 5)
            dve.wait_ge(off_done, 2)
            step(dve, nc.vector.tensor_sub(upto[:], upto[:], count[:]), 6)
            nc.vector.tensor_scalar(K.place0[:], upto[:], p_off[0:NB, 0:1], None, ALU.add)
            dve.wait_ge(root, 1)
            step(dve, nc.vector.reciprocal(K.dinv[:], K.root[:]), 7)
            nc.vector.tensor_mul(K.dinv[:], K.dinv[:], pos[:])

        @block.gpsimd
        def _(pool):
            with nc.gpsimd.Fori(0, NG // 2) as i:
                for h in range(2):
                    pool.wait_ge(part, i * 2 + h + 1)
                    nc.gpsimd.tensor_tensor(out=d_hiw[:, h], in0=d_hi[:, h],
                                            in1=K.ew[:, bass.ds(i * 2 * G + h * G, G)].unsqueeze(2).broadcast_to([P, G, NB]), op=ALU.mult).then_inc(weighted, 1)

        @block.tensor
        def _(pe):
            pe.sem_inc(free, 2)
            pe.wait_ge(zeroed, 1)
            nc.tensor.matmul(p_count[0:NB, 0:P], zero[:, 0:NB], zero[:], start=True, stop=False, skip_group_check=True)
            nc.tensor.matmul(p_deg[0:NB, 0:P], zero[:, 0:NB], zero[:], start=True, stop=False, skip_group_check=True)
            with nc.tensor.Fori(0, NG // 2) as i:
                for h in range(2):
                    pe.wait_ge(src_hot, i * 2 + h + 1)
                    for j in range(G):
                        nc.tensor.matmul(p_count[0:NB, 0:P], oh_hi[:, h, j, :], oh_lo[:, h, j, :], start=False, stop=False, skip_group_check=True)
                    pe.wait_ge(dst_hot, i * 2 + h + 1)
                    pe.wait_ge(weighted, i * 2 + h + 1)
                    for j in range(G):
                        mm = nc.tensor.matmul(p_deg[0:NB, 0:P], d_hiw[:, h, j, :], d_lo[:, h, j, :], start=False, stop=False, skip_group_check=True)
                    mm.then_inc(free, 1)
            pe.wait_ge(free, NG + 2)
            pe.sem_inc(summed, 1)
            pe.wait_ge(chain, 3)
            nc.tensor.transpose(p_dt[:, 0:NB], deg_row[:], K.ident[0:NB, 0:NB]).then_inc(off_done, 1)
            nc.tensor.matmul(p_off[0:NB, 0:1], K.above[0:NB, 0:NB], upto[:, P - 1:P], start=True, stop=True).then_inc(off_done, 1)

        @block.scalar
        def _(act):
            act.wait_ge(chain, 5)
            nc.scalar.activation(K.root[:], K.root[:], ACT.Sqrt).then_inc(root, 1)


def split3(nc, dve, of, parts, rest, done, n, tick):
    nc.vector.tensor_copy(parts[0], of).then_inc(done, 1)
    for k in (1, 2):
        dve.wait_ge(done, n + 2 * k - 1)
        dve.sem_inc(tick, 1)
        nc.vector.tensor_tensor(out=rest, in0=of if k == 1 else rest, in1=parts[k - 1], op=ALU.subtract).then_inc(done, 1)
        dve.wait_ge(done, n + 2 * k)
        dve.sem_inc(tick, 1)
        ins = nc.vector.tensor_copy(parts[k], rest).then_inc(done, 1)
    return ins


def rows_in_blocks(nc, K, s, numbers, blocks, row16):
    chunks = [(c, min(P, T - c * P)) for c in range(-(-T // P))]
    blk_f, low = s.sb("blocks", [1, T]), s.sb("in_block", [P, T])
    turned = s.sb("turned", [P, len(chunks), P], BF16)
    p_blk, p_t = s.ps("p_blk", [P, 1024]), s.ps("p_t", [P, -(-T // 512), 512])
    f_ready, blk_ready, in_ready, t_ready, c_ready, stored = (s.sem(n) for n in ("f", "blk", "in", "t", "c", "stored"))
    with nc.Block() as block:
        @block.vector
        def _(dve):
            nc.vector.tensor_copy(blk_f[:], blocks[:]).then_inc(f_ready, 1)
            dve.wait_ge(blk_ready, 1)
            nc.vector.scalar_tensor_tensor(out=low[:], in0=p_blk[:, 0:T], scalar=-float(P), in1=numbers[:], op0=ALU.mult, op1=ALU.add).then_inc(in_ready, 1)
            dve.wait_ge(t_ready, 1)
            for c, n in chunks:
                nc.vector.tensor_copy(turned[0:n, c, :], p_t[0:n, c // 4, c % 4 * P:(c % 4 + 1) * P]).then_inc(c_ready, 1)

        @block.tensor
        def _(pe):
            pe.wait_ge(f_ready, 1)
            for c in range(0, T, 512):
                n = min(512, T - c)
                mm = nc.tensor.matmul(p_blk[:, c:c + n], K.ones[0:1, :], blk_f[:, c:c + n], start=True, stop=True)
            mm.then_inc(blk_ready, 1)
            pe.wait_ge(in_ready, 1)
            for c, n in chunks:
                tr = nc.tensor.transpose(p_t[0:n, c // 4, c % 4 * P:(c % 4 + 1) * P], low[:, c * P:c * P + n], K.ident[:])
            tr.then_inc(t_ready, 1)

        @block.sync
        def _(sp):
            for c, n in chunks:
                sp.wait_ge(c_ready, c + 1)
                nc.sync.dma_start(row16.rearrange("a (t p) -> (a t) p", p=P)[c * P:c * P + n, :], turned[0:n, c, :]).then_inc(stored, 16)
            sp.wait_ge(stored, 16 * len(chunks))


def layer_norm_stats(nc, K, s):
    st = s.sb("stats", [P, R, 6])
    mv = s.sb("mean_var", [P, NB, 2])
    mv_r = s.sb("mean_var_r", [P, R, 2])
    tick, have, aggregated, copied, chain, root = (s.sem(n) for n in ("tick", "have", "aggregated", "copied", "chain", "root"))
    with nc.Block() as block:
        @block.vector
        def _(dve):
            dve.sem_inc(copied, 1)
            with nc.vector.Fori(0, NI) as i:
                for r in range(R):
                    nc.vector.bn_stats(st[:, r, :], K.x[:, bass.ds(i * R + r, 1), :].rearrange("p a d -> p (a d)")).then_inc(have, 1)
                dve.wait_ge(copied, i + 1)
                dve.wait_ge(have, i * R + R)
                dve.sem_inc(tick, 1)
                for r in range(R):
                    nc.vector.bn_aggr(mv_r[:, r, :], st[:, r, :]).then_inc(aggregated, 1)
                dve.wait_ge(aggregated, i * R + R)
                nc.vector.tensor_copy(mv[:, bass.ds(i * R, R), :], mv_r[:]).then_inc(copied, 1)
            dve.wait_ge(copied, NI + 1)
            nc.vector.tensor_scalar(K.rstd[:], mv[:, :, 1], LN_EPS, None, ALU.add).then_inc(chain, 1)
            dve.wait_ge(root, 1)
            nc.vector.reciprocal(K.rstd[:], K.sd[:]).then_inc(chain, 1)
            dve.wait_ge(chain, 2)
            nc.vector.scalar_tensor_tensor(out=K.shift[:], in0=mv[:, :, 0], scalar=-1.0, in1=K.rstd[:], op0=ALU.mult, op1=ALU.mult)

        @block.scalar
        def _(act):
            act.wait_ge(chain, 1)
            nc.scalar.activation(K.sd[:], K.rstd[:], ACT.Sqrt).then_inc(root, 1)


def normed(nc, K, act, i, to, tick):
    act.sem_inc(tick, 1)
    for r in range(R):
        ins = nc.scalar.activation(to[:, r, :], K.x[:, bass.ds(i * R + r, 1), :].rearrange("p a d -> p (a d)"), ACT.Relu,
                                   bias=K.shift[:, bass.ds(i * R + r, 1)], scale=K.rstd[:, bass.ds(i * R + r, 1)])
    return ins


def in_step(i):
    return bass.ds(i * R * P, R * P)


def nodes_before_filter(nc, K, s):
    hs, hT = s.sb("h", [P, R, D]), s.sb("hT", [P, R, D])
    minus = s.sb("minus", [P, 1])
    p_t = s.ps("p_t", [P, 1024])
    p_y = s.ps("p_y", [P, 512])
    p_b = s.ps("p_b", [1, 512])
    rest = s.sb("rest", [P, R, F0])
    bias, bias_rest = s.sb("bias", [1, 4, F0]), s.sb("bias_rest", [1, 4, F0])
    bias3 = s.sb("bias3", [1, 3, 4 * F0], BF16)
    h_ready, turned, copied, projected, kept, tick, biases, filled, b_ready, b_split, moved = (
        s.sem(n) for n in ("h_ready", "turned", "copied", "projected", "kept", "tick", "biases", "filled", "b", "b_split", "moved"))

    with nc.Block() as block:
        @block.scalar
        def _(act):
            with nc.scalar.Fori(0, NI) as i:
                act.wait_ge(copied, i + 1)
                normed(nc, K, act, i, hs, tick).then_inc(h_ready, 1)

        @block.tensor
        def _(pe):
            pe.sem_inc(projected, 1)
            pe.wait_ge(filled, 1)
            nc.tensor.matmul(p_b[0:1, 0:F0], minus[0:F0, 0:1], K.w_f2[0:F0, :], start=True, stop=True)
            nc.tensor.matmul(p_b[0:1, D:2 * D], minus[:, 0:1], K.w_o2[:], start=True, stop=True).then_inc(biases, 1)
            with nc.tensor.Fori(0, NI) as i:
                pe.wait_ge(h_ready, i + 1)
                for r in range(R):
                    tr = nc.tensor.transpose(p_t[:, r * D:(r + 1) * D], hs[:, r, :], K.ident[:])
                tr.then_inc(turned, 1)
                pe.wait_ge(copied, i + 2)
                pe.wait_ge(kept, i * 5 + 5)
                for r in range(R):
                    y = p_y[:, r * F0:(r + 1) * F0]
                    nc.tensor.matmul(y, hT[:, r, :], K.w_in[:], start=True, stop=False)
                    mm = nc.tensor.matmul(y, K.ones[0:1, :], K.b_in[:], start=False, stop=True)
                mm.then_inc(projected, 1)

        @block.vector
        def _(dve):
            dve.sem_inc(copied, 1)
            dve.sem_inc(kept, 5)
            nc.vector.memset(minus[:], -LOG2).then_inc(filled, 1)
            nc.vector.memset(K.b_f2g[:], 0.0)
            nc.vector.memset(K.h_in[:, NB:NB + 1, :, :], 0.0)
            with nc.vector.Fori(0, NI) as i:
                dve.wait_ge(turned, i + 1)
                dve.wait_ge(projected, i + 1)
                nc.vector.tensor_copy(hT[:].rearrange("p r d -> p (r d)"), p_t[:, 0:R * D]).then_inc(copied, 1)
                dve.wait_ge(projected, i + 2)
                dve.sem_inc(tick, 1)
                split3(nc, dve, p_y[:, 0:R * F0].rearrange("p (r f) -> p r f", f=F0), [K.h_in[:, bass.ds(i * R, R), m, :] for m in range(3)],
                       rest[:], kept, i * 5 + 5, tick)
            dve.wait_ge(biases, 1)
            nc.vector.tensor_add(K.b_o2[:], K.b_o2[:], p_b[0:1, D:2 * D])
            nc.vector.tensor_tensor(out=bias[:], in0=K.b_f2[:].unsqueeze(1).broadcast_to([1, 4, F0]),
                                    in1=p_b[0:1, 0:F0].unsqueeze(1).broadcast_to([1, 4, F0]), op=ALU.add).then_inc(b_ready, 1)
            dve.wait_ge(b_ready, 1)
            split3(nc, dve, bias[:], [bias3[:, m, :].rearrange("a (j f) -> a j f", f=F0) for m in range(3)], bias_rest[:], b_split, 0, tick)

        @block.sync
        def _(sp):
            sp.wait_ge(b_split, 5)
            for m in range(3):
                for at in (m, F0 + m):
                    sp.dma_start(K.b_f2g[at:at + 1, :], bias3[:, m, :]).then_inc(moved, 16)
            sp.wait_ge(moved, 96)


def filter_edges(nc, K, Dr, A, s):
    aT = s.sb("attrT", [64, 2, GE // 2])
    dst_b = s.sb("dst_b", [P, 2, GE], BF16)
    src_b = s.sb("src_b", [P, 2, GE], I32)
    mag, low, re, ln = (s.sb(n, [P, GE // 2]) for n in ("mag", "low", "relu", "ln"))
    sp = s.sb("softplus", [P, 2, GE // 2])
    ws = s.sb("w_cut", [P, 2, G, F0])
    dhot = s.sb("dst_hotT", [P, 2, 2, GE], BF16)
    oh_hi = s.sb("src_hi_hot", [P, 2, G, NB], BF16)
    oh_lo = s.sb("src_lo_hot", [P, 2, G, P], BF16)
    hiT = s.sb("src_hi_hotT", [NB, 2, GE])
    place = s.sb("place", [NB, 2 * G, P])
    scrap = s.sb("scrap", [P, 2, 2, G, P], BF16)
    before, among = s.sb("before", [P, 2, G]), s.sb("among", [P, 2, G])
    ident16 = s.sb("ident16", [P, P], BF16)
    ones16 = s.sb("ones16", [P, P], BF16)
    pos = s.sb("pos", [P, 2, G], I32)
    rows = s.sb("rows", [P, 2, G, XC])
    p_z = s.ps("p_z", [P, 512])
    p_w = s.ps("p_w", [P, 2, 4, F0])
    p_hd = s.ps("p_hd", [P, G, 2 * F0])
    p_first = s.ps("p_first", [P, 2, 4, P])
    p_new = s.ps("p_new", [NB, 4, P])
    p_hiT = s.ps("p_hiT", [NB, GE], BF16)
    landed = [s.sem("landed0"), s.sem("landed1")]
    scattered = [s.sem("scattered0"), s.sem("scattered1")]
    (z_ready, sp_ready, w_ready, ws_ready, dhot_ready, hd_ready, hot_ready, hiT_ps, hiT_ready, new_ready, place_ready, first_ready,
     pos_ready, rows_ready, summed, tick, chain, a_mag, a_exp, among_ready, before_ready, start16) = (
        s.sem(n) for n in ("z", "sp", "w", "ws", "dhot", "hd", "hot", "hiT_ps", "hiT", "new", "place", "first", "pos", "rows",
                           "summed", "tick", "chain", "mag", "exp", "among", "before", "start"))
    ln_ready, hd_kept, hd_sum = s.sem("ln"), s.sem("hd_kept"), s.sem("hd_sum")
    hd = s.sb("hd", [P, 2, G, 2 * F0])

    with nc.Block() as block:
        @block.sync
        def _(sp_):
            with nc.sync.Fori(0, NG // 2) as i:
                for h in range(2):
                    edges = bass.ds((i * 2 + h) * GE, GE)
                    sp_.wait_ge(z_ready, i * 2 + h + 1)
                    nc.sync.sem_inc(tick, 1)
                    sp_.wait_ge(among_ready, i * 2 + h + 1)
                    nc.sync.sem_inc(tick, 1)
                    for c in range(2):
                        nc.sync.dma_start(aT[32 * c:32 * c + 32, h, :], A["attr32T"][:, bass.ds((i * 2 + h) * GE + c * (GE // 2), GE // 2)]).then_inc(landed[h], 16)
                    nc.sync.dma_start(dst_b[:, h, :], Dr.dst16[:, edges].broadcast_to([P, GE])).then_inc(landed[h], 16)
                    nc.sync.dma_start(src_b[:, h, :], A["src_row"][:, edges].broadcast_to([P, GE])).then_inc(landed[h], 16)

        @block.tensor
        def _(pe):
            pe.sem_inc(z_ready, 2)
            pe.sem_inc(hd_ready, 2)
            pe.sem_inc(w_ready, 4)
            pe.sem_inc(first_ready, 4)
            pe.sem_inc(new_ready, 4)
            pe.wait_ge(start16, 3)

            def filter_first(g, h, loads):
                pe.wait_ge(landed[h], loads * 64)
                pe.wait_ge(a_mag, g + 1)
                nc.tensor.matmul(p_z[:], K.w_f1[:], aT[:, h, :], start=True, stop=True).then_inc(z_ready, 1)

            def sources(g, h, c):
                pe.wait_ge(place_ready, 2 * g + c + 1)
                for j in range(4 * c, 4 * c + 4):
                    mm = nc.tensor.matmul(p_new[:, j % 4, :], oh_hi[:, h, j, :], oh_lo[:, h, j, :], start=True, stop=True)
                mm.then_inc(new_ready, 1)

            def turn(g, h):
                pe.wait_ge(hot_ready, g + 1)
                pe.wait_ge(hiT_ready, g + 2)
                pe.sem_inc(tick, 1)
                for j in range(G):
                    tr = nc.tensor.transpose(p_hiT[:, j * P:(j + 1) * P], oh_hi[:, h, j, :], ident16[:])
                tr.then_inc(hiT_ps, 1)

            def group(g, h, loads, last):
                sources(g, h, 1)
                blk = load_values(nc, PE, K.dst_blk[0:1, bass.ds(g * G, G)], NB - 1)
                pe.wait_ge(dhot_ready, g + 1)
                pe.wait_ge(hd_kept, g + 1)
                pe.sem_inc(tick, 1)
                for j in range(G):
                    for k in range(2):
                        hot, of = dhot[:, h, k, j * P:(j + 1) * P], bass.ds(blk[j] + k, 1)
                        nc.tensor.matmul(p_hd[:, j, :], hot, K.h_in[:, of, 0:2, :].rearrange("p a m f -> p (a m f)"), start=(k == 0), stop=False, skip_group_check=True)
                        mm = nc.tensor.matmul(p_hd[:, j, 0:F0], hot, K.h_in[:, of, 2, :].rearrange("p a f -> p (a f)"), start=False, stop=(k == 1), skip_group_check=True)
                mm.then_inc(hd_ready, 1)
                pe.wait_ge(hiT_ready, g + 3)
                for c in range(2):
                    pe.wait_ge(place_ready, 2 * g + c + 2)
                    pe.wait_ge(before_ready, 2 * g + c + 1)
                    for j in range(4 * c, 4 * c + 4):
                        mm = nc.tensor.matmul(p_first[:, c, j % 4, :], hiT[:, h, j * P:(j + 1) * P], place[:, h * G + j, :], start=True, stop=True)
                    mm.then_inc(first_ready, 1)
                if not last:
                    turn(g + 1, 1 - h)
                    sources(g + 1, 1 - h, 0)
                pe.wait_ge(sp_ready, g + 2)
                pe.wait_ge(ws_ready, g + 2)
                pe.sem_inc(tick, 1)
                for c in range(2):
                    half = slice(c * F0, (c + 1) * F0)
                    if c:
                        pe.wait_ge(w_ready, 2 * g + 5)
                    nc.tensor.matmul(p_w[:, c].rearrange("p j f -> p (j f)"), ones16[half, :], K.b_f2g[half, :], start=True, stop=False, skip_group_check=True)
                    for j in range(4):
                        mm = nc.tensor.matmul(p_w[:, c, j, :], sp[half, h, j * P:(j + 1) * P], K.w_f2[half, :], start=False, stop=(j == 3), skip_group_check=True)
                    mm.then_inc(w_ready, 1)
                if not last:
                    filter_first(g + 1, 1 - h, loads)

            filter_first(0, 0, 1)
            turn(0, 0)
            sources(0, 0, 0)
            with nc.tensor.Fori(0, NG // 2 - 1) as i:
                for h in range(2):
                    group(i * 2 + h, h, i + 1 + h, False)
            group(NG - 2, 0, NG // 2, False)
            group(NG - 1, 1, 0, True)

        @block.scalar
        def _(act):
            act.sem_inc(a_mag, 1)
            act.sem_inc(hd_kept, 1)
            act.sem_inc(hiT_ready, 2)
            act.sem_inc(ws_ready, 2)

            def softplus(g, h):
                act.wait_ge(z_ready, g + 3)
                nc.scalar.activation(mag[:], p_z[:], ACT.Abs, bias=K.b_f1[:]).then_inc(chain, 1)
                act.wait_ge(sp_ready, g + 1)
                nc.scalar.activation(re[:], p_z[:], ACT.Relu, bias=K.b_f1[:]).then_inc(a_mag, 1)
                act.wait_ge(chain, g + 1)
                nc.scalar.activation(low[:], mag[:], ACT.Exp, scale=-1.0).then_inc(a_exp, 1)
                act.wait_ge(a_exp, g + 1)
                nc.scalar.activation(ln[:], low[:], ACT.Ln, bias=K.ones[:, 0:1]).then_inc(ln_ready, 1)

            def keep_turned(g, h):
                act.wait_ge(hiT_ps, g + 1)
                act.wait_ge(first_ready, 2 * g + 2)
                nc.scalar.copy(hiT[:, h, :], p_hiT[:]).then_inc(hiT_ready, 1)

            def group(g, h, last):
                act.wait_ge(hd_ready, g + 3)
                nc.scalar.copy(hd[:, h], p_hd[:]).then_inc(hd_kept, 1)
                if not last:
                    keep_turned(g + 1, 1 - h)
                act.wait_ge(w_ready, 2 * g + 6)
                act.wait_ge(rows_ready, g + 1)
                act.sem_inc(tick, 1)
                for j in range(G):
                    ins = nc.scalar.activation(ws[:, h, j, :], p_w[:, j // 4, j % 4, :], ACT.Copy, scale=K.ew[:, bass.ds(g * G + j, 1)])
                ins.then_inc(ws_ready, 1)
                if not last:
                    softplus(g + 1, 1 - h)

            softplus(0, 0)
            keep_turned(0, 0)
            with nc.scalar.Fori(0, NG // 2 - 1) as i:
                for h in range(2):
                    group(i * 2 + h, h, False)
            group(NG - 2, 0, False)
            group(NG - 1, 1, True)

        @block.vector
        def _(dve):
            dve.sem_inc(place_ready, 1)
            dve.sem_inc(rows_ready, 1)
            dve.sem_inc(before_ready, 2)
            dve.sem_inc(pos_ready, 2)
            dve.sem_inc(sp_ready, 1)
            dve.sem_inc(among_ready, 2)
            nc.vector.tensor_copy(ident16[:], K.ident[:]).then_inc(start16, 1)
            nc.vector.tensor_copy(place[:, 0, :], K.place0[:]).then_inc(start16, 1)
            nc.vector.tensor_copy(ones16[:], K.ones[:]).then_inc(start16, 1)
            dve.wait_ge(start16, 3)

            def source_hots(g, h):
                cols = bass.ds(g * G, G)
                nc.vector.tensor_tensor(out=oh_hi[:, h], in0=K.lane16[:, 0:NB].unsqueeze(1).broadcast_to([P, G, NB]),
                                        in1=K.src_hi16[:, cols].unsqueeze(2).broadcast_to([P, G, NB]), op=ALU.is_equal)
                nc.vector.tensor_tensor(out=oh_lo[:, h], in0=K.lane16[:].unsqueeze(1).broadcast_to([P, G, P]),
                                        in1=K.src_lo16[:, cols].unsqueeze(2).broadcast_to([P, G, P]), op=ALU.is_equal).then_inc(hot_ready, 1)

            def destination_hots(g, h, loads):
                dve.wait_ge(landed[h], loads * 64)
                dve.wait_ge(hd_ready, g + 1)
                for k in range(2):
                    ins = nc.vector.tensor_scalar(dhot[:, h, k, :], dst_b[:, h, :], K.node_col[:, k:k + 1], None, ALU.is_equal)
                ins.then_inc(dhot_ready, 1)

            def softplus(g, h):
                dve.wait_ge(ln_ready, g + 1)
                dve.wait_ge(w_ready, 2 * g + 2)
                nc.vector.tensor_add(sp[:, h, :], re[:], ln[:]).then_inc(sp_ready, 1)

            def places(g, h, c):
                dve.wait_ge(new_ready, 2 * g + c + 5)
                for j in range(4 * c, 4 * c + 4):
                    k = h * G + j
                    if j:
                        dve.wait_ge(summed, g * G + j)
                    nc.vector.tensor_add(place[:, (k + 1) % (2 * G), :], place[:, k, :], p_new[:, j % 4, :]).then_inc(summed, 1)
                    if j % 4 == 3:
                        dve.wait_ge(summed, g * G + j + 1)
                        dve.sem_inc(place_ready, 1)
                    ins = nc.vector.scalar_tensor_tensor(out=scrap[:, 0, h, j, :], in0=src_b[:, h, j * P:(j + 1) * P], scalar=K.src_f[:, bass.ds(g * G + j, 1)],
                                                         in1=K.below[:], op0=ALU.is_equal, op1=ALU.mult, accum_out=among[:, h, j:j + 1])
                if c == 1:
                    ins.then_inc(among_ready, 1)

            def positions(g, h, i, first):
                for c in range(2):
                    dve.wait_ge(first_ready, 2 * g + c + 5)
                    dve.sem_inc(tick, 1)
                    for j in range(4 * c, 4 * c + 4):
                        ins = nc.vector.scalar_tensor_tensor(out=scrap[:, 1, h, j, :], in0=K.lane[:, 0:P], scalar=K.src_lo[:, bass.ds(g * G + j, 1)],
                                                             in1=p_first[:, c, j % 4, :], op0=ALU.is_equal, op1=ALU.mult, accum_out=before[:, h, j:j + 1])
                    ins.then_inc(before_ready, 1)
                if not first:
                    dve.wait_ge(scattered[h], i * 16 * G)
                    dve.sem_inc(tick, 1)
                dve.wait_ge(among_ready, g + 3)
                dve.wait_ge(before_ready, 2 * g + 4)
                nc.vector.tensor_add(pos[:, h, :], before[:, h, :], among[:, h, :]).then_inc(pos_ready, 1)
                dve.wait_ge(pos_ready, g + 3)
                dve.sem_inc(tick, 1)
                nc.vector.tensor_copy(K.pos[:, bass.ds(g * G, G)], pos[:, h, :])

            def products(g, h):
                dve.wait_ge(hd_kept, g + 2)
                nc.vector.tensor_tensor(out=hd[:, h, :, 0:F0], in0=hd[:, h, :, 0:F0], in1=hd[:, h, :, F0:2 * F0], op=ALU.add).then_inc(hd_sum, 1)
                nc.vector.tensor_copy(rows[:, h, :, F0], K.src_f[:, bass.ds(g * G, G)])
                dve.wait_ge(hd_sum, g + 1)
                dve.wait_ge(ws_ready, g + 3)
                nc.vector.tensor_mul(rows[:, h, :, 0:F0], hd[:, h, :, 0:F0], ws[:, h]).then_inc(rows_ready, 1)

            def group(i, h, first, last):
                g = i * 2 + h
                places(g, h, 0)
                if not last:
                    source_hots(g + 1, 1 - h)
                    destination_hots(g + 1, 1 - h, i + 1 + h)
                if not (first and h == 0):
                    products(g - 1, 1 - h)
                places(g, h, 1)
                softplus(g, h)
                positions(g, h, i, first)

            source_hots(0, 0)
            destination_hots(0, 0, 1)
            for h in range(2):
                group(0, h, True, False)
            with nc.vector.Fori(1, NG // 2 - 1) as i:
                for h in range(2):
                    group(i, h, False, False)
            group(NG // 2 - 1, 0, False, False)
            group(NG // 2 - 1, 1, False, True)
            products(NG - 1, 1)

        @block.gpsimd
        def _(pool):
            with nc.gpsimd.Fori(0, NG // 2) as i:
                for h in range(2):
                    g = i * 2 + h
                    pool.wait_ge(pos_ready, g + 3)
                    pool.wait_ge(rows_ready, g + 2)
                    pool.sem_inc(tick, 1)
                    for j in range(G):
                        nc.gpsimd.indirect_dma_start(Dr.by_src0, bass.IndirectOffsetOnAxis(pos[:, h, j:j + 1], 0), rows[:, h, j, :], None).then_inc(scattered[h], 16)
            for h in range(2):
                pool.wait_ge(scattered[h], NG // 2 * G * 16)


def sum_by_source(nc, K, Dr, s):
    L = 4
    assert NG % L == 0
    rows = s.sb("rows", [P, L, G, XC])
    hot = s.sb("hot", [P, 2, G, P])
    p_sum = s.ps("p_sum", [F0, 2, 4, P])
    landed = [s.sem(f"landed{q}") for q in range(L)]
    numbered, hot_ready, summed, added, tick, noted, cleared = (s.sem(n) for n in ("numbered", "hot", "summed", "added", "tick", "noted", "cleared"))
    with nc.Block() as block:
        @block.sync
        def _(sp):
            def load(g, q):
                nc.sync.dma_start(rows[:, q], Dr.by_src0[bass.ds(g * GE, GE), :].rearrange("(j p) f -> p j f", p=P)).then_inc(landed[q], 16)

            for q in range(L):
                load(q, q)
            with nc.sync.Fori(1, NG // L) as i:
                for q in range(L):
                    sp.wait_ge(summed, 2 * L * i + 2 * q - 2 * L + 6)
                    nc.sync.sem_inc(tick, 1)
                    load(i * L + q, q)

        @block.gpsimd
        def _(pool):
            nc.gpsimd.iota(K.node_row[:], [[1, NW]], base=0, channel_multiplier=0, allow_small_or_imprecise_dtypes=True).then_inc(numbered, 1)
            with nc.gpsimd.Fori(0, NG // L) as i:
                for q in range(L):
                    g = i * L + q
                    pool.wait_ge(landed[q], i * 16 + 16)
                    pool.sem_inc(tick, 1)
                    nc.gpsimd.tensor_copy(K.srt_f[:, bass.ds(g * G, G)], rows[:, q, :, F0])
                    nc.gpsimd.tensor_copy(K.srt_i[0:1, bass.ds(g * G, G)], rows[0:1, q, :, F0]).then_inc(noted, 1)

        @block.vector
        def _(dve):
            dve.sem_inc(added, G)
            nc.vector.memset(K.acc[:], 0.0).then_inc(cleared, 1)
            dve.wait_ge(cleared, 1)
            dve.wait_ge(numbered, 1)

            def first_nodes(g, groups=1):
                return load_values(nc, DVE, K.srt_i[0:1, bass.ds(g * G, groups * G)], N)

            def one_hot(q, j, at):
                ins = nc.vector.tensor_scalar(hot[:, q % 2, j, :], K.node_row[:, bass.ds(at[j], P)], rows[:, q, j, F0:XC], None, ALU.is_equal)
                if j % 4 == 3:
                    ins.then_inc(hot_ready, 1)

            def group(g, q, at, end):
                last = end and q == L - 1
                more = 0 if q % 2 else 1 if end and q == L - 2 else 2
                if not last:
                    dve.wait_ge(noted, g + 1 + max(more, 1))
                    dve.wait_ge(summed, 2 * g + 4)
                    dve.sem_inc(tick, 1)
                if more:
                    at = list(at) + list(first_nodes(g + 1, more))
                ahead = at[G:]
                for j in range(G):
                    if not last:
                        one_hot((q + 1) % L, j, ahead)
                    if j % 4 == 0:
                        dve.wait_ge(summed, 2 * g + j // 4 + 5)
                    dve.wait_ge(added, (g + 1) * G + j)
                    window = K.acc[0:F0, bass.ds(at[j], P)]
                    nc.vector.tensor_tensor(out=window, in0=window, in1=p_sum[:, j // 4, j % 4, :], op=ALU.add).then_inc(added, 1)
                return ahead

            dve.wait_ge(noted, 1)
            dve.wait_ge(summed, 4)
            dve.sem_inc(tick, 1)
            at = first_nodes(0)
            for j in range(G):
                one_hot(0, j, at)
            with nc.vector.Fori(0, NG // L - 1) as i:
                at = first_nodes(i * L)
                for q in range(L):
                    at = group(i * L + q, q, at, False)
            at = first_nodes(NG - L)
            for q in range(L):
                at = group(NG - L + q, q, at, True)

        @block.tensor
        def _(pe):
            pe.sem_inc(summed, 4)
            with nc.tensor.Fori(0, NG // L) as i:
                for q in range(L):
                    g = i * L + q
                    pe.wait_ge(landed[q], i * 16 + 16)
                    pe.wait_ge(noted, g + 1)
                    for c in range(2):
                        pe.wait_ge(hot_ready, 2 * g + c + 1)
                        pe.wait_ge(added, g * G + 4 * c + 4)
                        for j in range(4 * c, 4 * c + 4):
                            mm = nc.tensor.matmul(p_sum[:, c, j % 4, :], rows[:, q, j, 0:F0], hot[:, q % 2, j, :], start=True, stop=True)
                        mm.then_inc(summed, 1)


def sorted_row(nc, K, Dr, s):
    turned = s.sb("turned", [P, -(-T // P), P])
    p_t = s.ps("p_t", [P, -(-T // 512), 512])
    p_first = s.ps("p_first", [P, 2, 1024])
    t_ready, c_ready, f_ready, stored = s.sem("t"), s.sem("c"), s.sem("f"), s.sem("stored")
    chunks = [(c, min(P, T - c * P)) for c in range(-(-T // P))]
    with nc.Block() as block:
        @block.tensor
        def _(pe):
            for k, numbers in enumerate((K.srt_f, K.dst_f)):
                for c in range(0, T, 512):
                    n = min(512, T - c)
                    mm = nc.tensor.matmul(p_first[:, k, c:c + n], K.ones[0:1, :], numbers[0:1, c:c + n], start=True, stop=True)
                mm.then_inc(f_ready, 1)
            for c, n in chunks:
                nc.tensor.transpose(p_t[0:n, c // 4, c % 4 * P:(c % 4 + 1) * P], K.srt_f[:, c * P:c * P + n], K.ident[:]).then_inc(t_ready, 1)

        @block.vector
        def _(dve):
            nc.vector.tensor_single_scalar(K.srt_blk[:], K.srt_i[:], 7, ALU.logical_shift_right)
            dve.wait_ge(t_ready, len(chunks))
            for k, numbers in enumerate((K.srt_f, K.dst_f)):
                dve.wait_ge(f_ready, k + 1)
                nc.vector.tensor_sub(numbers[:], numbers[:], p_first[:, k, 0:T])
            for c, n in chunks:
                nc.vector.tensor_copy(turned[0:n, c, :], p_t[0:n, c // 4, c % 4 * P:(c % 4 + 1) * P]).then_inc(c_ready, 1)

        @block.sync
        def _(sp):
            for c, n in chunks:
                sp.wait_ge(c_ready, c + 1)
                nc.sync.dma_start(Dr.srt.rearrange("a (t p) -> (a t) p", p=P)[c * P:c * P + n, :], turned[0:n, c, :]).then_inc(stored, 16)
            sp.wait_ge(stored, 16 * len(chunks))


def nodes_after_filter(nc, K, s):
    C = R * P
    mag, low, re, ln = s.sb("mag", [D, C]), s.sb("low", [D, C]), s.sb("relu", [D, C]), s.sb("ln", [D, C])
    p_u, p_o = s.ps("p_u", [D, 2, 512]), s.ps("p_o", [P, 1024])
    u_ready, m_ready, e_ready, sp_ready, o_ready, added, tick = (s.sem(n) for n in ("u", "m", "e", "sp", "o", "added", "tick"))
    with nc.Block() as block:
        @block.tensor
        def _(pe):
            pe.sem_inc(o_ready, 1)
            with nc.tensor.Fori(0, NI) as i:
                pe.wait_ge(sp_ready, i + 1)
                pe.sem_inc(tick, 1)
                for c in range(2):
                    mm = nc.tensor.matmul(p_u[:, c, 0:C // 2], K.w_o1[:], K.acc[0:F0, bass.ds(i * C + c * (C // 2), C // 2)], start=True, stop=True)
                mm.then_inc(u_ready, 1)
                pe.wait_ge(sp_ready, i + 2)
                pe.wait_ge(added, i + 1)
                for r in range(R):
                    o, cols = p_o[:, r * D:(r + 1) * D], slice(r * P, (r + 1) * P)
                    nc.tensor.matmul(o, re[:, cols], K.w_o2[:], start=True, stop=False)
                    nc.tensor.matmul(o, ln[:, cols], K.w_o2[:], start=False, stop=False)
                    mm = nc.tensor.matmul(o, K.ones[0:1, :], K.b_o2[:], start=False, stop=True)
                mm.then_inc(o_ready, 1)

        @block.scalar
        def _(act):
            act.sem_inc(sp_ready, 1)
            with nc.scalar.Fori(0, NI) as i:
                act.wait_ge(u_ready, i + 1)
                act.wait_ge(o_ready, i + 1)
                nc.scalar.activation(mag[:].rearrange("p (c n) -> p c n", c=2), p_u[:, :, 0:C // 2], ACT.Abs, bias=K.b_o1[:]).then_inc(m_ready, 1)
                nc.scalar.activation(re[:].rearrange("p (c n) -> p c n", c=2), p_u[:, :, 0:C // 2], ACT.Relu, bias=K.b_o1[:])
                act.wait_ge(m_ready, i + 1)
                nc.scalar.activation(low[:], mag[:], ACT.Exp, scale=-1.0).then_inc(e_ready, 1)
                act.wait_ge(e_ready, i + 1)
                nc.scalar.activation(ln[:], low[:], ACT.Ln, bias=K.ones[:, 0:1]).then_inc(sp_ready, 1)

        @block.vector
        def _(dve):
            dve.sem_inc(added, 1)
            with nc.vector.Fori(0, NI) as i:
                x = K.x[:, bass.ds(i * R, R), :]
                dve.wait_ge(o_ready, i + 2)
                nc.vector.tensor_tensor(out=x, in0=x, in1=p_o[:, 0:R * D].rearrange("p (r d) -> p r d", d=D), op=ALU.add).then_inc(added, 1)


def nodes_before_gcn(nc, K, Dr, s):
    hs, dh = s.sb("h", [P, R, D]), s.sb("dh", [P, R, D])
    p_t = s.ps("p_t", [P, 1024])
    h_ready, x_ready, dh_ready, turned, kept, stored, tick = (s.sem(n) for n in ("h", "x", "dh", "t", "kept", "stored", "tick"))
    with nc.Block() as block:
        @block.scalar
        def _(act):
            with nc.scalar.Fori(0, NI) as i:
                act.wait_ge(dh_ready, i + 1)
                normed(nc, K, act, i, hs, tick).then_inc(h_ready, 1)

        @block.vector
        def _(dve):
            dve.sem_inc(dh_ready, 1)
            dve.sem_inc(kept, 1)
            nc.vector.memset(K.acc[:, NR:NW], 0.0)
            with nc.vector.Fori(0, NI) as i:
                x = K.x[:, bass.ds(i * R, R), :]
                dve.wait_ge(h_ready, i + 1)
                nc.vector.tensor_tensor(out=x, in0=x, in1=hs[:], op=ALU.add)
                dve.wait_ge(stored, i * 16 + 16)
                dve.wait_ge(kept, i + 1)
                nc.vector.tensor_tensor(out=dh[:], in0=hs[:], in1=K.dinv[:, bass.ds(i * R, R)].unsqueeze(2).broadcast_to([P, R, D]), op=ALU.mult).then_inc(dh_ready, 1)
                dve.wait_ge(turned, i + 1)
                dve.sem_inc(tick, 1)
                nc.vector.tensor_copy(K.acc[:, in_step(i)], p_t[:, 0:R * P]).then_inc(kept, 1)

        @block.tensor
        def _(pe):
            with nc.tensor.Fori(0, NI) as i:
                pe.wait_ge(dh_ready, i + 2)
                pe.wait_ge(kept, i + 1)
                for r in range(R):
                    tr = nc.tensor.transpose(p_t[:, r * P:(r + 1) * P], dh[:, r, :], K.ident[:])
                tr.then_inc(turned, 1)

        @block.sync
        def _(sp):
            sp.sem_inc(stored, 16)
            with nc.sync.Fori(0, NI) as i:
                sp.wait_ge(dh_ready, i + 2)
                sp.sem_inc(tick, 1)
                nc.sync.dma_start(Dr.table.rearrange("(b p) d -> p b d", p=P)[:, bass.ds(i * R, R), :], dh[:]).then_inc(stored, 16)
            sp.wait_ge(stored, 16 * NI + 16)


def sum_by_target(nc, K, Dr, A, s, gine):
    idx = s.sb("idx", [P, 2, G], I32)
    rows = s.sb("rows", [P, 2, G, D])
    hot = s.sb("hot", [P, 2, G, P])
    p_sum = s.ps("p_sum", [D, 2, 4, P])
    if gine:
        aT = s.sb("attrT", [16, 2, GE])
        msg = s.sb("msg", [P, 2, G, D])
        p_msg = s.ps("p_msg", [P, 2, 4, D])
    loads = 2 if gine else 1
    landed = [s.sem("landed0"), s.sem("landed1")]
    fetched = [s.sem("fetched0"), s.sem("fetched1")]
    hot_ready, summed, added, tick, m_ready, pre_ready, msg_ready = (s.sem(n) for n in ("hot", "summed", "added", "tick", "m", "pre", "msg"))
    used = pre_ready if gine else summed
    with nc.Block() as block:
        @block.sync
        def _(sp):
            with nc.sync.Fori(0, NG // 2) as i:
                for h in range(2):
                    g = i * 2 + h
                    sp.wait_ge(used, 2 * g + 2)
                    sp.sem_inc(tick, 1)
                    nc.sync.dma_start(idx[:, h, :], A["src"][:, bass.ds(g * G, G)]).then_inc(landed[h], 16)
                    if gine:
                        nc.sync.dma_start(aT[:, h, :], A["attr16T"][:, bass.ds(g * GE, GE)]).then_inc(landed[h], 16)

        @block.gpsimd
        def _(pool):
            with nc.gpsimd.Fori(0, NG // 2) as i:
                for h in range(2):
                    pool.wait_ge(landed[h], (i + 1) * 16 * loads)
                    pool.sem_inc(tick, 1)
                    for j in range(G):
                        nc.gpsimd.indirect_dma_start(rows[:, h, j, :], None, Dr.table, bass.IndirectOffsetOnAxis(idx[:, h, j:j + 1], 0)).then_inc(fetched[h], 16)

        @block.vector
        def _(dve):
            dve.sem_inc(added, G)

            def one_hot(g, h, j):
                to, weight = K.dst_f[:, bass.ds(g * G + j, 1)], K.ew[:, bass.ds(g * G + j, 1)]
                if gine:
                    ins = nc.vector.tensor_scalar(hot[:, h, j, :], K.lane[:, 0:P], to, None, ALU.is_equal)
                else:
                    ins = nc.vector.tensor_scalar(hot[:, h, j, :], K.lane[:, 0:P], to, weight, ALU.is_equal, ALU.mult)
                if j % 4 == 3:
                    ins.then_inc(hot_ready, 1)

            def messages(g, h, fetches):
                dve.wait_ge(fetched[h], fetches * 16 * G)
                dve.sem_inc(tick, 1)
                for c in range(2):
                    dve.wait_ge(m_ready, 2 * g + c + 1)
                    nc.vector.tensor_tensor(out=msg[:, h, 4 * c:4 * c + 4, :], in0=p_msg[:, c], in1=rows[:, h, 4 * c:4 * c + 4, :], op=ALU.add).then_inc(pre_ready, 1)

            def group(g, h, last, fetches):
                at = load_values(nc, DVE, K.dst_i[0:1, bass.ds(g * G, G)], N)
                if not last:
                    dve.wait_ge(summed, 2 * g + 4)
                    dve.sem_inc(tick, 1)
                for j in range(G):
                    if not last:
                        one_hot(g + 1, 1 - h, j)
                    if j % 4 == 0:
                        dve.wait_ge(summed, 2 * g + j // 4 + 5)
                    dve.wait_ge(added, (g + 1) * G + j)
                    window = K.acc[:, bass.ds(at[j], P)]
                    nc.vector.tensor_tensor(out=window, in0=window, in1=p_sum[:, j // 4, j % 4, :], op=ALU.add).then_inc(added, 1)
                if gine and not last:
                    messages(g + 1, 1 - h, fetches)

            for j in range(G):
                one_hot(0, 0, j)
            if gine:
                dve.sem_inc(pre_ready, 4)
                messages(0, 0, 1)
            with nc.vector.Fori(0, NG // 2 - 1) as i:
                for h in range(2):
                    group(i * 2 + h, h, False, i + 1 + h)
            group(NG - 2, 0, False, NG // 2)
            group(NG - 1, 1, True, 0)

        @block.tensor
        def _(pe):
            pe.sem_inc(summed, 4)
            with nc.tensor.Fori(0, NG // 2) as i:
                for h in range(2):
                    g = i * 2 + h
                    if gine:
                        pe.wait_ge(landed[h], (i + 1) * 32)
                        for c in range(2):
                            pe.wait_ge(pre_ready, 2 * g + c + 3)
                            for j in range(4 * c, 4 * c + 4):
                                mm = nc.tensor.matmul(p_msg[:, c, j % 4, :], aT[:, h, j * P:(j + 1) * P], K.wc[:], start=True, stop=True)
                            mm.then_inc(m_ready, 1)
                    else:
                        pe.wait_ge(fetched[h], (i + 1) * 16 * G)
                    for c in range(2):
                        pe.wait_ge(hot_ready, 2 * g + c + 1)
                        pe.wait_ge(added, g * G + 4 * c + 4)
                        if gine:
                            pe.wait_ge(msg_ready, 2 * g + c + 1)
                        for j in range(4 * c, 4 * c + 4):
                            mm = nc.tensor.matmul(p_sum[:, c, j % 4, :], (msg if gine else rows)[:, h, j, :], hot[:, h, j, :], start=True, stop=True)
                        mm.then_inc(summed, 1)

        if gine:
            @block.scalar
            def _(act):
                with nc.scalar.Fori(0, NG // 2) as i:
                    for h in range(2):
                        g = i * 2 + h
                        for c in range(2):
                            act.wait_ge(pre_ready, 2 * g + c + 5)
                            part = msg[:, h, 4 * c:4 * c + 4, :]
                            nc.scalar.activation(part, part, ACT.Relu).then_inc(msg_ready, 1)


def nodes_after_gcn(nc, K, s):
    sums, t, z = s.sb("sums", [D, R * P]), s.sb("t", [P, R, D]), s.sb("z", [P, R, D])
    p_o = s.ps("p_o", [P, 1024])
    s_ready, o_ready, t_ready, z_ready, added, tick = (s.sem(n) for n in ("s", "o", "t", "z", "added", "tick"))
    with nc.Block() as block:
        @block.scalar
        def _(act):
            with nc.scalar.Fori(0, NI) as i:
                act.wait_ge(o_ready, i + 1)
                act.sem_inc(tick, 1)
                nc.scalar.copy(sums[:], K.acc[:, in_step(i)]).then_inc(s_ready, 1)

        @block.tensor
        def _(pe):
            pe.sem_inc(o_ready, 1)
            with nc.tensor.Fori(0, NI) as i:
                pe.wait_ge(s_ready, i + 1)
                pe.wait_ge(t_ready, i + 1)
                for r in range(R):
                    mm = nc.tensor.matmul(p_o[:, r * D:(r + 1) * D], sums[:, r * P:(r + 1) * P], K.w1[:], start=True, stop=True)
                mm.then_inc(o_ready, 1)

        @block.vector
        def _(dve):
            dve.sem_inc(t_ready, 1)
            dve.sem_inc(added, 1)
            with nc.vector.Fori(0, NI) as i:
                x = K.x[:, bass.ds(i * R, R), :]
                dve.wait_ge(o_ready, i + 2)
                nc.vector.tensor_tensor(out=t[:], in0=p_o[:, 0:R * D].rearrange("p (r d) -> p r d", d=D),
                                        in1=K.dinv[:, bass.ds(i * R, R)].unsqueeze(2).broadcast_to([P, R, D]), op=ALU.mult).then_inc(t_ready, 1)
                dve.wait_ge(t_ready, i + 2)
                dve.wait_ge(added, i + 1)
                nc.vector.tensor_tensor(out=z[:], in0=t[:], in1=K.b1[:].unsqueeze(1).broadcast_to([P, R, D]), op=ALU.add).then_inc(z_ready, 1)
                dve.wait_ge(z_ready, i + 1)
                nc.vector.scalar_tensor_tensor(out=x, in0=z[:], scalar=0.0, in1=x, op0=ALU.max, op1=ALU.add).then_inc(added, 1)


def nodes_before_attention(nc, K, s):
    hs, hT, rest = s.sb("h", [P, R, D]), s.sb("hT", [P, R, D]), s.sb("rest", [P, 4, 2 * D])
    p_t, p_q, p_kv = s.ps("p_t", [P, 1024]), s.ps("p_q", [P, 4, D]), s.ps("p_kv", [P, 4, 2 * D])
    p_x = s.ps("p_x", [P, 512])
    h_ready, turned, copied, made, q_kept, kv_kept, tick, mixed = (s.sem(n) for n in ("h", "t", "copied", "made", "q", "kv", "tick", "mixed"))
    parts = [(0, 4), (4, 3)]
    with nc.Block() as block:
        @block.scalar
        def _(act):
            act.sem_inc(q_kept, 1)
            with nc.scalar.Fori(0, NI) as i:
                act.wait_ge(copied, i + 1)
                normed(nc, K, act, i, hs, tick).then_inc(h_ready, 1)
                for c, (r, n) in enumerate(parts):
                    act.wait_ge(made, 2 * i + c + 2)
                    act.sem_inc(tick, 1)
                    nc.scalar.copy(K.q[:, bass.ds(i * R + r, n), :], p_q[:, 0:n, :]).then_inc(q_kept, 1)

        @block.tensor
        def _(pe):
            pe.sem_inc(made, 1)
            nc.tensor.matmul(p_x[:, 0:H], K.rep[:], K.w_exp[:], start=True, stop=True).then_inc(mixed, 1)
            with nc.tensor.Fori(0, NI) as i:
                pe.wait_ge(h_ready, i + 1)
                for r in range(R):
                    tr = nc.tensor.transpose(p_t[:, r * P:(r + 1) * P], hs[:, r, :], K.ident[:])
                tr.then_inc(turned, 1)
                pe.wait_ge(copied, i + 2)
                for c, (r, n) in enumerate(parts):
                    pe.wait_ge(q_kept, 2 * i + c + 1)
                    pe.wait_ge(kv_kept, (2 * i + c) * 5 + 5)
                    for m in range(n):
                        nc.tensor.matmul(p_q[:, m, :], hT[:, r + m, :], K.wqkv[:, 0:D], start=True, stop=True)
                        mm = nc.tensor.matmul(p_kv[:, m, :], hT[:, r + m, :], K.wqkv[:, D:], start=True, stop=True)
                    mm.then_inc(made, 1)

        @block.vector
        def _(dve):
            dve.sem_inc(copied, 1)
            dve.sem_inc(kv_kept, 5)
            nc.vector.memset(K.q[:, NB:NB + 1, :], 0.0)
            nc.vector.memset(K.kv[:, NB:NB + 1, :, :], 0.0)
            dve.wait_ge(mixed, 1)
            nc.vector.tensor_scalar(K.mix[:], p_x[:, 0:H], float(HD) ** -0.5, None, ALU.mult)
            with nc.vector.Fori(0, NI) as i:
                dve.wait_ge(turned, i + 1)
                dve.wait_ge(made, 2 * i + 1)
                nc.vector.tensor_copy(hT[:].rearrange("p r d -> p (r d)"), p_t[:, 0:R * D]).then_inc(copied, 1)
                for c, (r, n) in enumerate(parts):
                    dve.wait_ge(made, 2 * i + c + 2)
                    dve.sem_inc(tick, 1)
                    split3(nc, dve, p_kv[:, 0:n, :], [K.kv[:, bass.ds(i * R + r, n), k, :] for k in range(3)], rest[:, 0:n, :], kv_kept, (2 * i + c) * 5 + 5, tick)


def key_value_edges(nc, K, Dr, A, s):
    aT, dst_b = s.sb("attrT", [D, 2, GE]), s.sb("dst_b", [P, 2, GE], BF16)
    dhot = s.sb("dst_hotT", [P, 2, 2, GE], BF16)
    rows = s.sb("rows", [P, 2, G, 2 * D])
    pos = s.sb("pos", [P, 2, G], I32)
    p_kv = s.ps("p_kv", [P, 2, 4, 512])
    landed = [s.sem("landed0"), s.sem("landed1")]
    scattered = [s.sem("scattered0"), s.sem("scattered1")]
    dhot_ready, kv_ready, copied, pos_ready, tick = (s.sem(n) for n in ("dhot", "kv", "copied", "pos", "tick"))
    with nc.Block() as block:
        @block.sync
        def _(sp):
            with nc.sync.Fori(0, NG // 2) as i:
                for h in range(2):
                    g = i * 2 + h
                    sp.wait_ge(kv_ready, 4 * g + 4)
                    sp.sem_inc(tick, 1)
                    nc.sync.dma_start(aT[:, h, :], A["attr128T"][:, bass.ds(g * GE, GE)]).then_inc(landed[h], 16)
                    nc.sync.dma_start(dst_b[:, h, :], Dr.dst16[:, bass.ds(g * GE, GE)].broadcast_to([P, GE])).then_inc(landed[h], 16)

        @block.vector
        def _(dve):
            def pair(i, first):
                for h in range(2):
                    g = i * 2 + h
                    dve.wait_ge(landed[h], i * 32 + 32)
                    dve.wait_ge(kv_ready, 4 * g + 4)
                    dve.sem_inc(tick, 1)
                    for k in range(2):
                        nc.vector.tensor_scalar(dhot[:, h, k, :], dst_b[:, h, :], K.node_col[:, k:k + 1], None, ALU.is_equal).then_inc(dhot_ready, 1)
                    if not first:
                        dve.wait_ge(scattered[h], i * 16 * G)
                        dve.sem_inc(tick, 1)
                    nc.vector.tensor_copy(pos[:, h, :], K.pos[:, bass.ds(g * G, G)]).then_inc(pos_ready, 1)

            pair(0, True)
            with nc.vector.Fori(1, NG // 2) as i:
                pair(i, False)

        @block.tensor
        def _(pe):
            pe.sem_inc(kv_ready, 8)
            with nc.tensor.Fori(0, NG // 2) as i:
                for h in range(2):
                    g = i * 2 + h
                    blk = load_values(nc, PE, K.dst_blk[0:1, bass.ds(g * G, G)], NB - 1)
                    pe.wait_ge(landed[h], i * 32 + 32)
                    pe.wait_ge(dhot_ready, 2 * g + 2)
                    pe.sem_inc(tick, 1)
                    for c in range(4):
                        pe.wait_ge(copied, 4 * g + c + 1)
                        pe.sem_inc(tick, 1)
                        for m in range(2):
                            j = 2 * c + m
                            to = p_kv[:, h, c, m * 2 * D:(m + 1) * 2 * D]
                            nc.tensor.matmul(to, aT[:, h, j * P:(j + 1) * P], K.wekv[:], start=True, stop=False)
                            for k in range(2):
                                for part in range(3):
                                    mm = nc.tensor.matmul(to, dhot[:, h, k, j * P:(j + 1) * P], K.kv[:, bass.ds(blk[j] + k, 1), part, :].rearrange("p a f -> p (a f)"),
                                                          start=False, stop=(k + part == 3))
                        mm.then_inc(kv_ready, 1)

        @block.scalar
        def _(act):
            act.sem_inc(copied, 8)

            def pair(i, first):
                for h in range(2):
                    g = i * 2 + h
                    if not first:
                        act.wait_ge(scattered[h], i * 16 * G)
                    for c in range(4):
                        act.wait_ge(kv_ready, 4 * g + c + 9)
                        nc.scalar.copy(rows[:, h, 2 * c:2 * c + 2, :].rearrange("p m f -> p (m f)"), p_kv[:, h, c, :]).then_inc(copied, 1)

            pair(0, True)
            with nc.scalar.Fori(1, NG // 2) as i:
                pair(i, False)

        @block.gpsimd
        def _(pool):
            with nc.gpsimd.Fori(0, NG // 2) as i:
                for h in range(2):
                    g = i * 2 + h
                    pool.wait_ge(pos_ready, g + 1)
                    for c in range(4):
                        pool.wait_ge(copied, 4 * g + c + 9)
                        pool.sem_inc(tick, 1)
                        for j in range(2 * c, 2 * c + 2):
                            nc.gpsimd.indirect_dma_start(Dr.by_src2, bass.IndirectOffsetOnAxis(pos[:, h, j:j + 1], 0), rows[:, h, j, :], None).then_inc(scattered[h], 16)
            for h in range(2):
                pool.wait_ge(scattered[h], NG // 2 * G * 16)


def attention_logits(nc, K, Dr, s):
    L = 4
    assert NG % L == 0
    kk, src_b = s.sb("kk", [P, L, G, D]), s.sb("src_b", [P, L, GE])
    shot = s.sb("src_hotT", [P, 2, G, 2, P])
    prod, prodT = s.sb("prod", [P, 2, G, D]), s.sb("prodT", [D, 2, GE])
    logit = s.sb("logit", [H, 2, GE])
    p_q, p_t, p_a = s.ps("p_q", [P, 2, 4, D]), s.ps("p_t", [D, 2, 512]), s.ps("p_a", [H, 2, 512])
    landed = [s.sem(f"landed{q}") for q in range(L)]
    stored = [s.sem("stored0"), s.sem("stored1")]
    shot_ready, q_ready, prod_ready, t_ready, prodT_ready, a_ready, logit_ready, tick = (s.sem(n) for n in ("shot", "q", "prod", "t", "prodT", "a", "logit", "tick"))
    with nc.Block() as block:
        @block.sync
        def _(sp):
            def load(g, q):
                nc.sync.dma_start(kk[:, q], Dr.by_src2[bass.ds(g * GE, GE), 0:D].rearrange("(j p) f -> p j f", p=P)).then_inc(landed[q], 16)
                nc.sync.dma_start(src_b[:, q, :], Dr.srt[:, bass.ds(g * GE, GE)].broadcast_to([P, GE])).then_inc(landed[q], 16)

            for q in range(L):
                load(q, q)
            with nc.sync.Fori(1, NG // L) as i:
                for q in range(L):
                    sp.wait_ge(prod_ready, 2 * L * i + 2 * q - 2 * L + 4)
                    sp.sem_inc(tick, 1)
                    load(i * L + q, q)

        @block.vector
        def _(dve):
            dve.sem_inc(prod_ready, 2)

            def one_hots(g, q, loads):
                blk = load_values(nc, DVE, K.srt_blk[0:1, bass.ds(g * G, G)], NB - 1)
                dve.wait_ge(landed[q], loads * 32)
                dve.wait_ge(q_ready, 2 * g + 2)
                dve.sem_inc(tick, 1)
                for j in range(G):
                    for k in range(2):
                        ins = nc.vector.tensor_scalar(shot[:, q % 2, j, k, :], src_b[:, q, j * P:(j + 1) * P],
                                                      K.node_col[:, bass.ds(blk[j] + k, 1)], None, ALU.is_equal)
                    if j % 4 == 3:
                        ins.then_inc(shot_ready, 1)

            def group(g, q, loads, last):
                if not last:
                    one_hots(g + 1, (q + 1) % L, loads)
                dve.wait_ge(t_ready, 2 * g + 2)
                for c in range(2):
                    dve.wait_ge(q_ready, 2 * g + c + 5)
                    nc.vector.tensor_tensor(out=prod[:, q % 2, 4 * c:4 * c + 4, :], in0=p_q[:, c], in1=kk[:, q, 4 * c:4 * c + 4, :], op=ALU.mult).then_inc(prod_ready, 1)

            one_hots(0, 0, 1)
            with nc.vector.Fori(0, NG // L - 1) as i:
                for q in range(L):
                    group(i * L + q, q, i + 1 + (q + 1) // L, False)
            for q in range(L):
                group(NG - L + q, q, NG // L, q == L - 1)

        @block.tensor
        def _(pe):
            pe.sem_inc(q_ready, 4)
            pe.sem_inc(t_ready, 4)
            pe.sem_inc(a_ready, 4)

            def queries(g, h):
                blk = load_values(nc, PE, K.srt_blk[0:1, bass.ds(g * G, G)], NB - 1)
                for c in range(2):
                    pe.wait_ge(shot_ready, 2 * g + c + 1)
                    pe.wait_ge(prod_ready, 2 * g + c + 1)
                    pe.sem_inc(tick, 1)
                    for j in range(4 * c, 4 * c + 4):
                        nc.tensor.matmul(p_q[:, c, j % 4, :], shot[:, h, j, 0, :], K.q[:, bass.ds(blk[j], 1), :].rearrange("p a f -> p (a f)"), start=True, stop=False)
                        mm = nc.tensor.matmul(p_q[:, c, j % 4, :], shot[:, h, j, 1, :], K.q[:, bass.ds(blk[j] + 1, 1), :].rearrange("p a f -> p (a f)"), start=False, stop=True)
                    mm.then_inc(q_ready, 1)

            def mixed(g, h):
                for c in range(2):
                    pe.wait_ge(prodT_ready, 2 * g + c + 3)
                    pe.wait_ge(logit_ready, 2 * g + c + 1)
                    nc.tensor.matmul(p_a[:, c, :], K.mix[:], prodT[:, h, c * 512:(c + 1) * 512], start=True, stop=True).then_inc(a_ready, 1)

            def group(g, h, first, last):
                if not last:
                    queries(g + 1, 1 - h)
                if not first:
                    mixed(g - 1, 1 - h)
                for c in range(2):
                    pe.wait_ge(prod_ready, 2 * g + c + 3)
                    pe.wait_ge(prodT_ready, 2 * g + c + 1)
                    for j in range(4 * c, 4 * c + 4):
                        tr = nc.tensor.transpose(p_t[:, c, (j % 4) * P:(j % 4 + 1) * P], prod[:, h, j, :], K.ident[:])
                    tr.then_inc(t_ready, 1)

            queries(0, 0)
            group(0, 0, True, False)
            group(1, 1, False, False)
            with nc.tensor.Fori(1, NG // 2 - 1) as i:
                for h in range(2):
                    group(i * 2 + h, h, False, False)
            group(NG - 2, 0, False, False)
            group(NG - 1, 1, False, True)
            mixed(NG - 1, 1)

        @block.scalar
        def _(act):
            act.sem_inc(prodT_ready, 2)
            act.sem_inc(logit_ready, 2)
            act.sem_inc(stored[0], 16)
            act.sem_inc(stored[1], 16)

            def turned(g, h):
                act.wait_ge(a_ready, 2 * g + 2)
                for c in range(2):
                    act.wait_ge(t_ready, 2 * g + c + 5)
                    nc.scalar.copy(prodT[:, h, c * 512:(c + 1) * 512], p_t[:, c, :]).then_inc(prodT_ready, 1)

            def logits(g, h, stores):
                act.wait_ge(stored[h], stores * 16 + 16)
                for c in range(2):
                    act.wait_ge(a_ready, 2 * g + c + 5)
                    nc.scalar.copy(logit[:, h, c * 512:(c + 1) * 512], p_a[:, c, :]).then_inc(logit_ready, 1)
                act.wait_ge(logit_ready, 2 * g + 4)
                act.sem_inc(tick, 1)
                nc.scalar.dma_start(Dr.logitT[:, bass.ds(g * GE, GE)], logit[:, h, :]).then_inc(stored[h], 16)

            turned(0, 0)
            with nc.scalar.Fori(0, NG // 2 - 1) as i:
                logits(i * 2, 0, i)
                turned(i * 2 + 1, 1)
                logits(i * 2 + 1, 1, i)
                turned(i * 2 + 2, 0)
            logits(NG - 2, 0, NG // 2 - 1)
            turned(NG - 1, 1)
            logits(NG - 1, 1, NG // 2 - 1)
            for h in range(2):
                act.wait_ge(stored[h], NG // 2 * 16 + 16)


def softmax_weights(nc, K, Dr, s):
    CH = P // H
    M = EP // CH
    a, src = s.sb("a", [P, M]), s.sb("src", [P, M])
    gap = s.sb("gap", [P, M + 1])
    best = s.sb("best", [P, M])
    edge = s.sb("edge", [P, 4])
    row = s.sb("row", [1, 8, P])
    carry = s.sb("carry", [P, 2])
    p_row, p_col = s.ps("p_row", [1, 4, P]), s.ps("p_col", [P, 512])
    landed, chain, rows_ready, cols_ready, e_ready, stored = (s.sem(n) for n in ("landed", "chain", "rows", "cols", "e", "stored"))
    count = [0]
    FIRST, LAST, TOP, SAME, WHOLE, OPEN, SHUT, STATE = range(8)

    with nc.Block() as block:
        @block.sync
        def _(sp):
            nc.sync.dma_start(a[:], Dr.logitT.rearrange("h (c m) -> (h c) m", c=CH)).then_inc(landed, 16)
            for h in range(H):
                nc.sync.dma_start(src[h * CH:(h + 1) * CH, :], Dr.srt.rearrange("a (c m) -> (a c) m", c=CH)).then_inc(landed, 16)
            sp.wait_ge(e_ready, 1)
            nc.sync.dma_start(Dr.expT.rearrange("h (c m) -> (h c) m", c=CH), a[:]).then_inc(stored, 16)
            sp.wait_ge(stored, 16)

        @block.vector
        def _(dve):
            def step(ins):
                ins.then_inc(chain, 1)
                count[0] += 1
                dve.wait_ge(chain, count[0])

            step(nc.vector.memset(gap[:], 0.0))
            dve.wait_ge(landed, 16 * (H + 1))
            step(nc.vector.tensor_tensor(out=gap[:, 1:M], in0=src[:, 1:M], in1=src[:, 0:M - 1], op=ALU.not_equal))
            step(nc.vector.tensor_scalar(gap[:], gap[:], -FAR, None, ALU.mult))
            for back in range(2):
                flip = slice(None, None, -1) if back else slice(None)
                gaps = gap[:, 1:M + 1] if back else gap[:, 0:M]
                data = best if back else a
                trial = src if back else best
                if not back:
                    step(nc.vector.tensor_copy(edge[:, FIRST:FIRST + 1], src[:, 0:1]))
                    step(nc.vector.tensor_copy(edge[:, LAST:LAST + 1], src[:, M - 1:M]))
                step(nc.vector.tensor_tensor_scan(out=trial[:, flip], data0=gaps[:, flip], data1=data[:, flip], initial=-FAR, op0=ALU.add, op1=ALU.max))
                step(nc.vector.tensor_copy(edge[:, TOP:TOP + 1], trial[:, 0:1] if back else trial[:, M - 1:M]))
                dve.wait_ge(rows_ready, 3 * back + 3)
                step(nc.vector.tensor_copy(row[:, 0:3, :], p_row[:, 0:3, :]))
                step(nc.vector.memset(row[:, SAME, :], 0.0))
                heads = row[:].rearrange("a k (h c) -> a k h c", c=CH)
                here, there = (slice(0, CH - 1), slice(1, CH)) if back else (slice(1, CH), slice(0, CH - 1))
                step(nc.vector.tensor_tensor(out=heads[:, SAME, :, here], in0=heads[:, LAST if back else FIRST, :, here],
                                             in1=heads[:, FIRST if back else LAST, :, there], op=ALU.is_equal))
                step(nc.vector.tensor_tensor(out=row[:, WHOLE, :], in0=row[:, FIRST, :], in1=row[:, LAST, :], op=ALU.is_equal))
                step(nc.vector.tensor_tensor(out=row[:, OPEN, :], in0=row[:, SAME, :], in1=row[:, WHOLE, :], op=ALU.mult))
                step(nc.vector.tensor_scalar(row[:, OPEN, :], row[:, OPEN, :], FAR, -FAR, ALU.mult, ALU.add))
                step(nc.vector.tensor_scalar(row[:, SHUT, :], row[:, SAME, :], FAR, -FAR, ALU.mult, ALU.add))
                step(nc.vector.tensor_tensor_scan(out=row[:, STATE, flip], data0=row[:, OPEN, flip], data1=row[:, TOP, flip], initial=-FAR, op0=ALU.add, op1=ALU.max))
                step(nc.vector.tensor_tensor(out=heads[:, SHUT, :, here], in0=heads[:, SHUT, :, here], in1=heads[:, STATE, :, there], op=ALU.add))
                dve.wait_ge(cols_ready, back + 1)
                step(nc.vector.tensor_copy(carry[:, back:back + 1], p_col[:, back:back + 1]))
                step(nc.vector.tensor_tensor_scan(out=trial[:, flip], data0=gaps[:, flip], data1=data[:, flip], initial=carry[:, back:back + 1], op0=ALU.add, op1=ALU.max))
            step(nc.vector.tensor_sub(a[:], a[:], src[:]))
            assert count[0] == LAST_STEP

        @block.tensor
        def _(pe):
            for back, (borders, carried) in enumerate(BORDERS):
                pe.wait_ge(chain, borders)
                for k in range(3):
                    nc.tensor.transpose(p_row[0:1, k, :], edge[:, k:k + 1], K.ident[:]).then_inc(rows_ready, 1)
                pe.wait_ge(chain, carried)
                nc.tensor.transpose(p_col[:, back:back + 1], row[0:1, SHUT, :], K.ident[0:1, 0:1]).then_inc(cols_ready, 1)

        @block.scalar
        def _(act):
            act.wait_ge(chain, LAST_STEP)
            nc.scalar.activation(a[:], a[:], ACT.Exp).then_inc(e_ready, 1)


BORDERS = [(7, 16), (20, 29)]
LAST_STEP = 32


def weighted_sums(nc, K, Dr, s):
    vv, expT = s.sb("vv", [P, 2, G, D]), s.sb("expT", [H, 2, GE])
    ex, wv = s.sb("ex", [P, 2, G, H]), s.sb("wv", [P, 2, G, D])
    hot = s.sb("hot", [P, 2, G, P])
    L = 4
    assert NG % L == 0
    p_ex = s.ps("p_ex", [P, 2, 512])
    p_sum, p_den = s.ps("p_sum", [D, 2, 4, P]), s.ps("p_den", [H, 2, 4, P])
    landed = [s.sem("landed0"), s.sem("landed1")]
    t_ready, ex_ready, wv_ready, hot_ready, summed, added, tick, cleared = (
        s.sem(n) for n in ("t", "ex", "wv", "hot", "summed", "added", "tick", "cleared"))
    with nc.Block() as block:
        @block.sync
        def _(sp):
            with nc.sync.Fori(0, NG // 2) as i:
                for h in range(2):
                    g = i * 2 + h
                    sp.wait_ge(wv_ready, g + 1)
                    sp.sem_inc(tick, 1)
                    nc.sync.dma_start(vv[:, h], Dr.by_src2[bass.ds(g * GE, GE), D:2 * D].rearrange("(j p) f -> p j f", p=P)).then_inc(landed[h], 16)
                    nc.sync.dma_start(expT[:, h, :], Dr.expT[:, bass.ds(g * GE, GE)]).then_inc(landed[h], 16)

        @block.gpsimd
        def _(pool):
            pool.sem_inc(wv_ready, 2)
            with nc.gpsimd.Fori(0, NG // 2) as i:
                for h in range(2):
                    g = i * 2 + h
                    pool.wait_ge(landed[h], i * 32 + 32)
                    pool.wait_ge(ex_ready, g + 1)
                    pool.wait_ge(summed, 2 * g + 2)
                    pool.sem_inc(tick, 1)
                    nc.gpsimd.tensor_tensor(out=wv[:, h].rearrange("p j (h d) -> p (j h) d", d=HD), in0=vv[:, h].rearrange("p j (h d) -> p (j h) d", d=HD),
                                            in1=ex[:, h].rearrange("p j h -> p (j h)").unsqueeze(2).broadcast_to([P, G * H, HD]), op=ALU.mult).then_inc(wv_ready, 1)

        @block.scalar
        def _(act):
            with nc.scalar.Fori(0, NG // 2) as i:
                for h in range(2):
                    g = i * 2 + h
                    act.wait_ge(t_ready, g + 1)
                    act.wait_ge(summed, 2 * g + 2)
                    nc.scalar.copy(ex[:, h].rearrange("p j h -> p (j h)"), p_ex[:, h, 0:G * H]).then_inc(ex_ready, 1)

        @block.vector
        def _(dve):
            dve.sem_inc(added, 2 * G)
            nc.vector.memset(K.acc[:], 0.0).then_inc(cleared, 1)
            nc.vector.memset(K.den[:], 0.0).then_inc(cleared, 1)
            dve.wait_ge(cleared, 2)

            def one_hot(g, h, j):
                ins = nc.vector.tensor_scalar(hot[:, h, j, :], K.lane[:, 0:P], K.srt_f[:, bass.ds(g * G + j, 1)], None, ALU.is_equal)
                if j % 4 == 3:
                    ins.then_inc(hot_ready, 1)

            def group(g, h, at, last):
                if not last:
                    dve.wait_ge(summed, 2 * g + 4)
                    dve.sem_inc(tick, 1)
                for j in range(G):
                    if not last:
                        one_hot(g + 1, 1 - h, j)
                    if j % 4 == 0:
                        dve.wait_ge(summed, 2 * g + j // 4 + 5)
                    dve.wait_ge(added, 2 * ((g + 1) * G + j))
                    window, under = K.acc[:, bass.ds(at[j], P)], K.den[:, bass.ds(at[j], P)]
                    nc.vector.tensor_tensor(out=window, in0=window, in1=p_sum[:, j // 4, j % 4, :], op=ALU.add).then_inc(added, 1)
                    nc.vector.tensor_tensor(out=under, in0=under, in1=p_den[:, j // 4, j % 4, :], op=ALU.add).then_inc(added, 1)

            for j in range(G):
                one_hot(0, 0, j)
            with nc.vector.Fori(0, NG // L - 1) as i:
                at = load_values(nc, DVE, K.srt_i[0:1, bass.ds(i * L * G, L * G)], N)
                for q in range(L):
                    group(i * L + q, q % 2, at[q * G:(q + 1) * G], False)
            at = load_values(nc, DVE, K.srt_i[0:1, bass.ds((NG - L) * G, L * G)], N)
            for q in range(L):
                group(NG - L + q, q % 2, at[q * G:(q + 1) * G], q == L - 1)

        @block.tensor
        def _(pe):
            pe.sem_inc(summed, 4)

            def turn(h, loads):
                pe.wait_ge(landed[h], loads * 32)
                pe.sem_inc(tick, 1)
                for j in range(G):
                    tr = nc.tensor.transpose(p_ex[:, h, j * H:(j + 1) * H], expT[:, h, j * P:(j + 1) * P], K.ident[0:H, 0:H])
                tr.then_inc(t_ready, 1)

            def products(g, h):
                pe.wait_ge(wv_ready, g + 3)
                for c in range(2):
                    pe.wait_ge(hot_ready, 2 * g + c + 1)
                    pe.wait_ge(added, 2 * (g * G + 4 * c + 4))
                    for j in range(4 * c, 4 * c + 4):
                        nc.tensor.matmul(p_sum[:, c, j % 4, :], wv[:, h, j, :], hot[:, h, j, :], start=True, stop=True)
                        mm = nc.tensor.matmul(p_den[:, c, j % 4, :], ex[:, h, j, :], hot[:, h, j, :], start=True, stop=True)
                    mm.then_inc(summed, 1)

            turn(0, 1)
            with nc.tensor.Fori(0, NG // 2 - 1) as i:
                for h in range(2):
                    turn(1 - h, i + 1 + h)
                    products(i * 2 + h, h)
            turn(1, NG // 2)
            products(NG - 2, 0)
            products(NG - 1, 1)


def nodes_after_attention(nc, K, s):
    C = R * P
    hs, hT = s.sb("h", [P, R, D]), s.sb("hT", [P, C])
    rden, guard = s.sb("rden", [H, C]), s.sb("guard", [H, C])
    mean, diff = s.sb("mean", [D, C]), s.sb("diff", [D, C])
    p_t, p_v, p_d, p_o = s.ps("p_t", [P, 1024]), s.ps("p_v", [D, 2, 512]), s.ps("p_d", [D, 2, 512]), s.ps("p_o", [P, 1024])
    h_ready, turned, copied, v_ready, d_ready, diff_ready, o_ready, added, tick, g_ready, r_ready, m_ready = (
        s.sem(n) for n in ("h", "t", "copied", "v", "d", "diff", "o", "added", "tick", "g", "r", "m"))
    with nc.Block() as block:
        @block.scalar
        def _(act):
            with nc.scalar.Fori(0, NI) as i:
                act.wait_ge(copied, i + 1)
                act.wait_ge(added, i + 1)
                normed(nc, K, act, i, hs, tick).then_inc(h_ready, 1)

        @block.tensor
        def _(pe):
            pe.sem_inc(v_ready, 1)
            pe.sem_inc(d_ready, 1)
            pe.sem_inc(o_ready, 1)
            with nc.tensor.Fori(0, NI) as i:
                pe.wait_ge(h_ready, i + 1)
                for r in range(R):
                    tr = nc.tensor.transpose(p_t[:, r * P:(r + 1) * P], hs[:, r, :], K.ident[:])
                tr.then_inc(turned, 1)
                pe.wait_ge(copied, i + 2)
                pe.wait_ge(diff_ready, i + 1)
                for c in range(2):
                    mm = nc.tensor.matmul(p_v[:, c, 0:C // 2], K.wqkv[:, 2 * D:3 * D], hT[:, c * (C // 2):(c + 1) * (C // 2)], start=True, stop=True)
                mm.then_inc(v_ready, 1)
                pe.wait_ge(r_ready, i + 1)
                for c in range(2):
                    mm = nc.tensor.matmul(p_d[:, c, 0:C // 2], K.rep[:], rden[:, c * (C // 2):(c + 1) * (C // 2)], start=True, stop=True)
                mm.then_inc(d_ready, 1)
                pe.wait_ge(diff_ready, i + 2)
                pe.wait_ge(added, i + 1)
                for r in range(R):
                    mm = nc.tensor.matmul(p_o[:, r * D:(r + 1) * D], diff[:, r * P:(r + 1) * P], K.w_out[:], start=True, stop=True)
                mm.then_inc(o_ready, 1)

        @block.vector
        def _(dve):
            dve.sem_inc(copied, 1)
            dve.sem_inc(diff_ready, 1)
            dve.sem_inc(added, 1)
            halves = "p (c n) -> p c n"
            with nc.vector.Fori(0, NI) as i:
                nc.vector.tensor_scalar(guard[:], K.den[:, in_step(i)], 1e-30, None, ALU.max).then_inc(g_ready, 1)
                dve.wait_ge(g_ready, i + 1)
                dve.wait_ge(d_ready, i + 1)
                nc.vector.reciprocal(rden[:], guard[:]).then_inc(r_ready, 1)
                dve.wait_ge(turned, i + 1)
                dve.wait_ge(v_ready, i + 1)
                nc.vector.tensor_copy(hT[:], p_t[:, 0:C]).then_inc(copied, 1)
                dve.wait_ge(d_ready, i + 2)
                nc.vector.tensor_tensor(out=mean[:].rearrange(halves, c=2), in0=K.acc[:, in_step(i)].rearrange(halves, c=2), in1=p_d[:, :, 0:C // 2], op=ALU.mult).then_inc(m_ready, 1)
                dve.wait_ge(m_ready, i + 1)
                dve.wait_ge(v_ready, i + 2)
                dve.wait_ge(o_ready, i + 1)
                nc.vector.tensor_tensor(out=diff[:].rearrange(halves, c=2), in0=p_v[:, :, 0:C // 2], in1=mean[:].rearrange(halves, c=2), op=ALU.subtract).then_inc(diff_ready, 1)
                dve.wait_ge(o_ready, i + 2)
                x = K.x[:, bass.ds(i * R, R), :]
                nc.vector.tensor_tensor(out=x, in0=x, in1=p_o[:, 0:C].rearrange("p (r d) -> p r d", d=D), op=ALU.add).then_inc(added, 1)


def nodes_before_gine(nc, K, Dr, s):
    hs, tab = s.sb("h", [P, R, D]), s.sb("tab", [P, R, D])
    we1T, bc, bias, own = s.sb("we1T", [P, 2, 16]), s.sb("bc", [1, D]), s.sb("bias", [P, D]), s.sb("own", [P, 1])
    p_t, p_w, p_c = s.ps("p_t", [P, 1024]), s.ps("p_w", [P, 512]), s.ps("p_c", [P, 4, P])
    h_ready, tab_ready, turned, kept, stored, tick, w_ready, c_ready = (s.sem(n) for n in ("h", "tab", "t", "kept", "stored", "tick", "w", "c"))
    with nc.Block() as block:
        @block.scalar
        def _(act):
            with nc.scalar.Fori(0, NI) as i:
                act.wait_ge(tab_ready, i + 1)
                act.wait_ge(turned, i + 1)
                normed(nc, K, act, i, hs, tick).then_inc(h_ready, 1)

        @block.tensor
        def _(pe):
            pe.sem_inc(turned, 1)
            for m in range(2):
                tr = nc.tensor.transpose(p_w[:, m * 16:(m + 1) * 16], K.we1[:, m * P:(m + 1) * P], K.ident[0:16, 0:16])
            tr.then_inc(w_ready, 1)
            pe.wait_ge(c_ready, 1)
            for m in range(2):
                nc.tensor.matmul(p_c[0:16, 0, :], we1T[:, m, :], K.we2[:, m, :], start=(m == 0), stop=(m == 1))
            for m in range(2):
                mm = nc.tensor.matmul(p_c[0:1, 1, :], K.be1[:, m:m + 1], K.we2[:, m, :], start=(m == 0), stop=(m == 1))
            mm.then_inc(w_ready, 1)
            pe.wait_ge(c_ready, 3)
            nc.tensor.matmul(p_c[:, 2, :], K.ones[0:1, :], bc[:], start=True, stop=True).then_inc(w_ready, 1)
            with nc.tensor.Fori(0, NI) as i:
                pe.wait_ge(h_ready, i + 1)
                pe.wait_ge(kept, i + 1)
                for r in range(R):
                    tr = nc.tensor.transpose(p_t[:, r * P:(r + 1) * P], hs[:, r, :], K.ident[:])
                tr.then_inc(turned, 1)

        @block.vector
        def _(dve):
            dve.sem_inc(tab_ready, 1)
            dve.sem_inc(kept, 1)
            nc.vector.memset(K.acc[:, NR:NW], 0.0)
            dve.wait_ge(w_ready, 1)
            nc.vector.tensor_copy(we1T[:].rearrange("p m k -> p (m k)"), p_w[:, 0:32]).then_inc(c_ready, 1)
            dve.wait_ge(w_ready, 2)
            nc.vector.tensor_copy(K.wc[:], p_c[0:16, 0, :]).then_inc(c_ready, 1)
            nc.vector.tensor_add(bc[:], K.be2[:], p_c[0:1, 1, :]).then_inc(c_ready, 1)
            dve.wait_ge(w_ready, 3)
            nc.vector.tensor_copy(bias[:], p_c[:, 2, :]).then_inc(c_ready, 1)
            nc.vector.tensor_scalar(own[:], K.eps[:], 1.0, None, ALU.add).then_inc(c_ready, 1)
            dve.wait_ge(c_ready, 5)
            with nc.vector.Fori(0, NI) as i:
                dve.wait_ge(h_ready, i + 1)
                dve.wait_ge(stored, i * 16 + 16)
                nc.vector.tensor_tensor(out=tab[:], in0=hs[:], in1=bias[:].unsqueeze(1).broadcast_to([P, R, D]), op=ALU.add).then_inc(tab_ready, 1)
                dve.wait_ge(turned, i + 2)
                nc.vector.tensor_scalar(K.acc[:, in_step(i)], p_t[:, 0:R * P], own[:, 0:1], None, ALU.mult).then_inc(kept, 1)

        @block.sync
        def _(sp):
            sp.sem_inc(stored, 16)
            with nc.sync.Fori(0, NI) as i:
                sp.wait_ge(tab_ready, i + 2)
                sp.sem_inc(tick, 1)
                nc.sync.dma_start(Dr.table.rearrange("(b p) d -> p b d", p=P)[:, bass.ds(i * R, R), :], tab[:]).then_inc(stored, 16)
            sp.wait_ge(stored, 16 * NI + 16)


def nodes_after_gine(nc, K, out, s):
    C = R * P
    BM, GA, BE, ME, VA = range(5)
    sc1, sh1 = s.sb("sc1", [P, 2]), s.sb("sh1", [P, 2])
    sc2, sh2 = s.sb("sc2", [P, D]), s.sb("sh2", [P, D])
    act1 = s.sb("act1", [P, 2, C])
    t, y = s.sb("t", [P, R, D]), s.sb("y", [P, R, D])
    p_u, p_o = s.ps("p_u", [P, 2, 1024]), s.ps("p_o", [P, 1024])
    chain, root, folded, u_ready, r_ready, o_ready, t_ready, y_ready, stored, tick, s_ready = (
        s.sem(n) for n in ("chain", "root", "folded", "u", "r", "o", "t", "y", "stored", "tick", "s"))
    z = s.sb("z", [P, R, D])
    with nc.Block() as block:
        @block.vector
        def _(dve):
            n = [0]

            def step(ins):
                ins.then_inc(chain, 1)
                n[0] += 1
                dve.wait_ge(chain, n[0])

            step(nc.vector.tensor_scalar(sc1[:], K.bn1[:, :, VA], BN_EPS, None, ALU.add))
            step(nc.vector.tensor_scalar(sc2[:], K.bn2[:, VA, :], BN_EPS, None, ALU.add))
            dve.wait_ge(root, 2)
            step(nc.vector.reciprocal(sc1[:], sc1[:]))
            step(nc.vector.reciprocal(sc2[:], sc2[:]))
            step(nc.vector.tensor_mul(sc1[:], sc1[:], K.bn1[:, :, GA]))
            step(nc.vector.tensor_mul(sc2[:], sc2[:], K.bn2[:, GA, :]))
            step(nc.vector.tensor_sub(sh1[:], K.bn1[:, :, BM], K.bn1[:, :, ME]))
            step(nc.vector.tensor_sub(sh2[:], K.bn2[:, BM, :], K.bn2[:, ME, :]))
            step(nc.vector.tensor_mul(sh1[:], sh1[:], sc1[:]))
            step(nc.vector.tensor_mul(sh2[:], sh2[:], sc2[:]))
            step(nc.vector.tensor_add(sh1[:], sh1[:], K.bn1[:, :, BE]))
            step(nc.vector.tensor_add(sh2[:], sh2[:], K.bn2[:, BE, :]))
            dve.sem_inc(folded, 1)
            dve.sem_inc(t_ready, 1)
            with nc.vector.Fori(0, NI) as i:
                dve.wait_ge(o_ready, i + 2)
                nc.vector.tensor_tensor(out=t[:], in0=p_o[:, 0:C].rearrange("p (r d) -> p r d", d=D), in1=sc2[:].unsqueeze(1).broadcast_to([P, R, D]), op=ALU.mult).then_inc(t_ready, 1)
                dve.wait_ge(t_ready, i + 2)
                nc.vector.tensor_tensor(out=z[:], in0=t[:], in1=sh2[:].unsqueeze(1).broadcast_to([P, R, D]), op=ALU.add).then_inc(s_ready, 1)
                dve.wait_ge(s_ready, i + 1)
                dve.wait_ge(stored, i * 16 + 16)
                nc.vector.tensor_tensor(out=y[:], in0=z[:], in1=K.x[:, bass.ds(i * R, R), :], op=ALU.add).then_inc(y_ready, 1)
                dve.wait_ge(y_ready, i + 1)

        @block.scalar
        def _(act):
            act.wait_ge(chain, 2)
            nc.scalar.activation(sc1[:], sc1[:], ACT.Sqrt).then_inc(root, 1)
            nc.scalar.activation(sc2[:], sc2[:], ACT.Sqrt).then_inc(root, 1)
            act.wait_ge(folded, 1)
            act.sem_inc(r_ready, 1)
            with nc.scalar.Fori(0, NI) as i:
                act.wait_ge(u_ready, i + 1)
                act.wait_ge(o_ready, i + 1)
                for m in range(2):
                    ins = nc.scalar.activation(act1[:, m, :], p_u[:, m, 0:C], ACT.Relu, bias=sh1[:, m:m + 1], scale=sc1[:, m:m + 1])
                ins.then_inc(r_ready, 1)

        @block.tensor
        def _(pe):
            pe.sem_inc(o_ready, 1)
            with nc.tensor.Fori(0, NI) as i:
                pe.wait_ge(r_ready, i + 1)
                pe.sem_inc(tick, 1)
                for m in range(2):
                    for r in range(R):
                        mm = nc.tensor.matmul(p_u[:, m, r * P:(r + 1) * P], K.wm1[:, m * P:(m + 1) * P], K.acc[:, bass.ds((i * R + r) * P, P)], start=True, stop=True)
                mm.then_inc(u_ready, 1)
                pe.wait_ge(r_ready, i + 2)
                pe.wait_ge(t_ready, i + 1)
                for r in range(R):
                    for m in range(2):
                        mm = nc.tensor.matmul(p_o[:, r * D:(r + 1) * D], act1[:, m, r * P:(r + 1) * P], K.wm2[:, m, :], start=(m == 0), stop=(m == 1))
                mm.then_inc(o_ready, 1)

        @block.sync
        def _(sp):
            sp.sem_inc(stored, 16)
            with nc.sync.Fori(0, NI) as i:
                sp.wait_ge(y_ready, i + 1)
                sp.sem_inc(tick, 1)
                nc.sync.dma_start(out.rearrange("(b p) d -> p b d", p=P)[:, bass.ds(i * R, R), :], y[:]).then_inc(stored, 16)
            sp.wait_ge(stored, 16 * NI + 16)


class Names:
    pass


def build(nc, A, out):
    K, Dr = Names(), Names()
    Dr.by_src0 = nc.dram_tensor("by_src0", (EP, XC), F32, kind=SCRATCH).ap()
    Dr.by_src2 = nc.dram_tensor("by_src2", (EP, 2 * D), F32, kind=SCRATCH).ap()
    Dr.srt = nc.dram_tensor("srt", (1, EP), F32, kind=SCRATCH).ap()
    Dr.dst16 = nc.dram_tensor("dst16", (1, EP), BF16, kind=SCRATCH).ap()
    Dr.srt16 = nc.dram_tensor("srt16", (1, EP), BF16, kind=SCRATCH).ap()
    Dr.logitT = nc.dram_tensor("logitT", (H, EP), F32, kind=SCRATCH).ap()
    Dr.expT = nc.dram_tensor("expT", (H, EP), F32, kind=SCRATCH).ap()
    Dr.table = nc.dram_tensor("table", (NR, D), F32, kind=SCRATCH).ap()
    with Space(nc, "k") as k:
        K.x = k.sb("x", [P, NB, D])
        K.ew = k.sb("ew", [P, T])
        K.dst_f, K.dst_i = k.sb("dst_f", [P, T]), k.sb("dst_i", [P, T], I32)
        K.srt_f, K.srt_i, K.dst_blk = k.sb("srt_f", [P, T]), k.sb("srt_i", [1, T], I32), k.sb("dst_blk", [1, T], I32)
        K.srt_blk, K.pos, K.mix = k.sb("srt_blk", [1, T], I32), k.sb("pos", [P, T], I32), k.sb("mix", [D, H])
        K.lane, K.node_col = k.sb("lane", [P, P]), k.sb("node_col", [P, NB + 1])
        K.ident, K.ones, K.rep = k.sb("ident", [P, P]), k.sb("ones", [P, P]), k.sb("rep", [H, D])
        K.dinv, K.root = k.sb("dinv", [P, NB]), k.sb("root", [P, NB])
        K.rstd, K.sd, K.shift = k.sb("rstd", [P, NB]), k.sb("sd", [P, NB]), k.sb("shift", [P, NB])
        K.w_in, K.b_in = k.sb("w_in", [D, F0]), k.sb("b_in", [1, F0])
        K.w_f1, K.b_f1 = k.sb("w_f1", [64, 2 * F0]), k.sb("b_f1", [2 * F0, 1])
        K.w_f2, K.b_f2, K.b_f2g = k.sb("w_f2", [2 * F0, F0]), k.sb("b_f2", [1, F0]), k.sb("b_f2g", [P, 4 * F0], BF16)
        K.w_o1, K.b_o1, K.w_o2, K.b_o2 = k.sb("w_o1", [F0, D]), k.sb("b_o1", [D, 1]), k.sb("w_o2", [D, D]), k.sb("b_o2", [1, D])
        K.w1, K.b1 = k.sb("w1", [D, D]), k.sb("b1", [P, D])
        K.wqkv, K.wekv = k.sb("wqkv", [D, 3 * D]), k.sb("wekv", [D, 2 * D])
        K.w_exp, K.w_out = k.sb("w_exp", [H, H]), k.sb("w_out", [D, D])
        K.we1, K.be1, K.we2, K.be2 = k.sb("we1", [16, 2 * D]), k.sb("be1", [P, 2]), k.sb("we2", [P, 2, D]), k.sb("be2", [1, D])
        K.eps, K.wm1, K.wm2 = k.sb("eps", [P, 1]), k.sb("wm1", [D, 2 * D]), k.sb("wm2", [P, 2, D])
        K.bn1, K.bn2 = k.sb("bn1", [P, 2, 5]), k.sb("bn2", [P, 5, D])
        with Space(nc, "e") as e:
            K.src_f = e.sb("src_f", [P, T])
            K.src_i, K.key_i, K.low_i = e.sb("src_i", [P, T], I32), e.sb("key_i", [P, T], I32), e.sb("low_i", [P, T], I32)
            K.lane16, K.src_hi16, K.src_lo16 = e.sb("lane16", [P, P], BF16), e.sb("src_hi16", [P, T], BF16), e.sb("src_lo16", [P, T], BF16)
            K.src_lo, K.dst_hi, K.dst_lo = e.sb("src_lo", [P, T]), e.sb("dst_hi", [P, T]), e.sb("dst_lo", [P, T])
            K.below, K.above, K.place0 = e.sb("below", [P, P]), e.sb("above", [P, P]), e.sb("place0", [NB, P])
            with Space(nc, "setup") as s:
                setup(nc, A, K, s)
            with Space(nc, "hist") as s:
                histograms(nc, K, s)
            with Space(nc, "dstrow") as s:
                rows_in_blocks(nc, K, s, K.dst_f, K.dst_blk, Dr.dst16)
            with Space(nc, "norm0") as s:
                layer_norm_stats(nc, K, s)
            K.h_in = e.sb("h_in", [P, NB + 1, 3, F0], BF16)
            with Space(nc, "nodes0") as s:
                nodes_before_filter(nc, K, s)
            with Space(nc, "edges0") as s:
                filter_edges(nc, K, Dr, A, s)
        with Space(nc, "a1") as a:
            K.acc = a.sb("acc", [P, NW])
            with Space(nc, "sum0") as s:
                K.node_row = s.sb("node_row", [P, NW])
                sum_by_source(nc, K, Dr, s)
            with Space(nc, "row") as s:
                sorted_row(nc, K, Dr, s)
            with Space(nc, "out0") as s:
                nodes_after_filter(nc, K, s)
            with Space(nc, "norm1") as s:
                layer_norm_stats(nc, K, s)
            with Space(nc, "nodes1") as s:
                nodes_before_gcn(nc, K, Dr, s)
            with Space(nc, "sum1") as s:
                sum_by_target(nc, K, Dr, A, s, gine=False)
            with Space(nc, "out1") as s:
                nodes_after_gcn(nc, K, s)
        with Space(nc, "norm2") as s:
            layer_norm_stats(nc, K, s)
        with Space(nc, "q") as q:
            K.q = q.sb("q", [P, NB + 1, D])
            with Space(nc, "kv") as kv:
                K.kv = kv.sb("kv", [P, NB + 1, 3, 2 * D], BF16)
                with Space(nc, "nodes2") as s:
                    nodes_before_attention(nc, K, s)
                with Space(nc, "edges2") as s:
                    key_value_edges(nc, K, Dr, A, s)
            with Space(nc, "logits") as s:
                attention_logits(nc, K, Dr, s)
        with Space(nc, "softmax") as s:
            softmax_weights(nc, K, Dr, s)
        with Space(nc, "a2") as a:
            K.acc = a.sb("acc", [P, NW])
            K.wc = a.sb("wc", [16, D])
            with Space(nc, "den") as d:
                K.den = d.sb("den", [H, NW])
                with Space(nc, "sum2") as s:
                    weighted_sums(nc, K, Dr, s)
                with Space(nc, "out2") as s:
                    nodes_after_attention(nc, K, s)
            with Space(nc, "norm3") as s:
                layer_norm_stats(nc, K, s)
            with Space(nc, "nodes3") as s:
                nodes_before_gine(nc, K, Dr, s)
            with Space(nc, "sum3") as s:
                sum_by_target(nc, K, Dr, A, s, gine=True)
            with Space(nc, "out3") as s:
                nodes_after_gine(nc, K, out, s)



SCRATCH = "Internal"


def kernel(**inputs):
    import numpy as np
    import concourse.bacc as bacc
    from concourse.bass_utils import run_bass_kernel_spmd as run

    nc = bacc.Bacc("TRN2", target_bir_lowering=False, num_devices=1)
    a = {n: np.ascontiguousarray(v) for n, v in inputs.items()}

    def edges(v, fill):
        return np.concatenate([v, np.full((EP - E,) + v.shape[1:], fill, v.dtype)])

    def in_tiles(v):
        return np.ascontiguousarray(v.reshape(T, P).T)

    src, dst, ew = edges(a.pop("src"), N), edges(a.pop("dst"), N), edges(a.pop("edge_weight"), 0)
    a["x"] = np.concatenate([a["x"], np.zeros((NR - N, D), a["x"].dtype)])
    a["src"], a["dst"], a["ew"] = in_tiles(src), in_tiles(dst), in_tiles(ew)
    a["src_row"] = src[None, :]
    for n in (16, 32, 128):
        a[f"attr{n}T"] = np.ascontiguousarray(edges(a.pop(f"edge_attr_{n}"), 0).T)
    aps = {n: nc.dram_tensor(f"in_{n}", v.shape, mybir.dt.from_np(v.dtype), kind="ExternalInput").ap() for n, v in a.items()}
    out = nc.dram_tensor("out", (NR, D), F32, kind="ExternalOutput").ap()
    build(nc, aps, out)
    r = run(nc, [{f"in_{n}": v for n, v in a.items()}], core_ids=[0])
    return r.results[0]["out"][:N]
```
